# Optimizing a Trainium2 kernel written in Bass

```python
import numpy as np
import jax
import jax.numpy as jnp

def _softmax(x, axis=-1):
    return jax.nn.softmax(x, axis=axis)

def _gelu(x):
    return jax.nn.gelu(x, approximate=True)

def _silu(x):
    return jax.nn.silu(x)

def _sigmoid(x):
    return jax.nn.sigmoid(x)

def _layernorm(x, axis=-1, eps=1e-05):
    m = jnp.mean(x, axis=axis, keepdims=True)
    v = jnp.var(x, axis=axis, keepdims=True)
    return (x - m) / jnp.sqrt(v + eps)

def _scatter_add(tgt, idx, src, axis=0):
    return tgt.at[idx].add(src)

def _segment_sum(src, seg, n):
    return jax.ops.segment_sum(src, seg, n)
kernel_name = 'mk_gnn_preln_d2_gnn_r8_e646ae'

def setup_inputs(seed: int=0):
    np.random.seed(seed)
    _w = jnp.asarray

    def _rec_inputs():
        import jax
        import jax.numpy as jnp
        _gk = jax.random.key(seed)
        x = 0.0001712 + 1 * jax.random.normal(jax.random.fold_in(_gk, 1), (12500, 16), jnp.float32)
        _s = jax.random.randint(jax.random.fold_in(_gk, 2), (200000,), 0, 12500, jnp.int32)
        _d = jax.random.randint(jax.random.fold_in(_gk, 3), (200000,), 0, 12500, jnp.int32)
        _loop = jnp.arange(12500, dtype=jnp.int32)
        src = jnp.concatenate([_s, _d, _loop])
        dst = jnp.concatenate([_d, _s, _loop])
        _o = jnp.argsort(dst, stable=True)
        src = src[_o]
        dst = dst[_o]
        return (x, src, dst)
    x, src, dst = _rec_inputs()

    def _L0_gnn_setup():
        import jax, jax.numpy as jnp
        import numpy as np
        N_NODES = 6250
        N_EDGES = 100000
        F_IN = 16
        F_OUT = 16
        HID = 256

        def _glorot(key, shape):
            fan_in, fan_out = (shape[0], shape[1])
            lim = np.sqrt(6.0 / (fan_in + fan_out)).astype(np.float32)
            return jax.random.uniform(key, shape, jnp.float32, -lim, lim)
        key = jax.random.key(seed)
        ks = jax.random.split(key, 12)
        x = jax.random.normal(ks[0], (N_NODES, F_IN), jnp.float32)
        edge_index = jax.random.randint(ks[1], (2, N_EDGES), 0, N_NODES, jnp.int64 if jax.config.jax_enable_x64 else jnp.int32)
        return {'x': x, 'edge_index': edge_index, 'pre_w1': _glorot(ks[2], (F_IN, HID)), 'pre_b1': jnp.zeros((HID,), jnp.float32), 'pre_w2': _glorot(ks[3], (HID, HID)), 'pre_b2': jnp.zeros((HID,), jnp.float32), 'conv_w': _glorot(ks[4], (HID, HID)), 'conv_b': jnp.zeros((HID,), jnp.float32), 'post_w1': _glorot(ks[5], (2 * HID, HID)), 'post_b1': jnp.zeros((HID,), jnp.float32), 'post_w2': _glorot(ks[6], (HID, F_OUT)), 'post_b2': jnp.zeros((F_OUT,), jnp.float32)}
    _L0_gnn_all = _L0_gnn_setup()
    _L0_gnn_in = {k: v for k, v in _L0_gnn_all.items() if k in ('pre_w1', 'pre_b1', 'pre_w2', 'pre_b2', 'conv_w', 'conv_b', 'post_w1', 'post_b1', 'post_w2', 'post_b2')}
    del _L0_gnn_all

    def _L1_gnn_setup():
        import jax, jax.numpy as jnp
        import numpy as np
        N_NODES = 12500
        N_EDGES = 400000
        D_FEAT = 16
        key = jax.random.key(seed)
        kx, ke = jax.random.split(key)
        x = jax.random.normal(kx, (N_NODES, D_FEAT), dtype=jnp.float32)
        edge_index = jax.random.randint(ke, (2, N_EDGES), 0, N_NODES, dtype=jnp.int64)
        return {'x': x, 'edge_index': edge_index}
    _L1_gnn_all = _L1_gnn_setup()
    _L1_gnn_in = {k: v for k, v in _L1_gnn_all.items() if k in ()}
    del _L1_gnn_all
    return {'x': x, 'src': src, 'dst': dst, 'L0_gnn_pre_w1': _L0_gnn_in['pre_w1'], 'L0_gnn_pre_b1': _L0_gnn_in['pre_b1'], 'L0_gnn_pre_w2': _L0_gnn_in['pre_w2'], 'L0_gnn_pre_b2': _L0_gnn_in['pre_b2'], 'L0_gnn_conv_w': _L0_gnn_in['conv_w'], 'L0_gnn_conv_b': _L0_gnn_in['conv_b'], 'L0_gnn_post_w1': _L0_gnn_in['post_w1'], 'L0_gnn_post_b1': _L0_gnn_in['post_b1'], 'L0_gnn_post_w2': _L0_gnn_in['post_w2'], 'L0_gnn_post_b2': _L0_gnn_in['post_b2']}

def reference(x, src, dst, L0_gnn_pre_w1, L0_gnn_pre_b1, L0_gnn_pre_w2, L0_gnn_pre_b2, L0_gnn_conv_w, L0_gnn_conv_b, L0_gnn_post_w1, L0_gnn_post_b1, L0_gnn_post_w2, L0_gnn_post_b2):
    import jax
    import jax.numpy as jnp

    def _L0_gnn_ref(x, edge_index, pre_w1, pre_b1, pre_w2, pre_b2, conv_w, conv_b, post_w1, post_b1, post_w2, post_b2):
        import jax, jax.numpy as jnp
        import numpy as np
        N_NODES = 6250
        N_EDGES = 100000
        F_IN = 16
        F_OUT = 16
        HID = 256

        def _glorot(key, shape):
            fan_in, fan_out = (shape[0], shape[1])
            lim = np.sqrt(6.0 / (fan_in + fan_out)).astype(np.float32)
            return jax.random.uniform(key, shape, jnp.float32, -lim, lim)
        h = jax.nn.relu(x @ pre_w1 + pre_b1) @ pre_w2 + pre_b2
        src, dst = (edge_index[0], edge_index[1])
        msg = jax.nn.relu(h[src] @ conv_w + conv_b)
        agg = jax.ops.segment_sum(msg, dst, num_segments=h.shape[0])
        h = jnp.concatenate([h, agg], axis=-1)
        out = jax.nn.relu(h @ post_w1 + post_b1) @ post_w2 + post_b2
        return jnp.tanh(out)

    def _L1_gnn_ref(x, edge_index):
        import jax, jax.numpy as jnp
        import numpy as np
        N_NODES = 12500
        N_EDGES = 400000
        D_FEAT = 16
        row = edge_index[0]
        col = edge_index[1]
        msg = jnp.take(x, col, axis=0)
        tmp = jnp.take(msg, col, axis=0)
        out = jax.ops.segment_sum(tmp, row, num_segments=x.shape[0])
        return out
    edge_index = jnp.stack([src, dst])
    h = jnp.maximum(_layernorm(x, axis=-1), 0.0)
    x = x + _L0_gnn_ref(h, edge_index, L0_gnn_pre_w1, L0_gnn_pre_b1, L0_gnn_pre_w2, L0_gnn_pre_b2, L0_gnn_conv_w, L0_gnn_conv_b, L0_gnn_post_w1, L0_gnn_post_b1, L0_gnn_post_w2, L0_gnn_post_b2)
    h = jnp.maximum(_layernorm(x, axis=-1), 0.0)
    x = x + _L1_gnn_ref(h, edge_index)
    return x

_drawn_inputs = setup_inputs


def setup_inputs(seed=0):
    import zlib

    import numpy as np

    out = dict(_drawn_inputs(seed))
    spreads = {'L0_gnn_pre_b1': (0.0, 0.1),
     'L0_gnn_pre_b2': (0.0, 0.1),
     'L0_gnn_conv_b': (0.0, 0.1),
     'L0_gnn_post_b1': (0.0, 0.333),
     'L0_gnn_post_b2': (0.0, 0.275)}
    factors = {}
    for name, (base, spread) in spreads.items():
        noise = np.random.default_rng([zlib.crc32(name.encode()), seed]).standard_normal(out[name].shape)
        drawn = base * np.exp(spread * noise) if base else spread * noise
        out[name] = jnp.asarray(drawn.astype(out[name].dtype))
    for name, factor in factors.items():
        out[name] = (out[name] * factor).astype(out[name].dtype)
    return out
```

```python
import concourse.bass as bass
from concourse import mybir
from contextlib import ExitStack

P = 128
N_NODES = 12500
F = 16
HID = 256
N_EDGES = 412500
BLOCKS = -(-N_NODES // P)
GROUPS = -(-BLOCKS // 8)
UNITS = -(-BLOCKS // 4)
NODES_PAD = BLOCKS * P
TILES = 8
SUPER = TILES * P
SUPERS = -(-N_EDGES // SUPER)
EDGES_PAD = SUPERS * SUPER
WINDOW = 64
REPEATS = 3
NOWHERE = 16383
CNT = REPEATS * BLOCKS
QROWS = -(-SUPERS * REPEATS // P) * P
QTILES = QROWS // P
SORT_COLS = 100
CHUNK = 512
CHUNKS = -(-NODES_PAD // CHUNK)
COUNT_MAX = 256.0
EPS = 1e-5
WEIGHT_LOADS = 18


def gnn_kernel(nc, x, src, dst, dst_flat, pre_w1, pre_b1, pre_w2, pre_b2, conv_w, conv_b,
               post_w1, post_b1, post_w2, post_b2, out):
    f32, bf16, i32 = mybir.dt.float32, mybir.dt.bfloat16, mybir.dt.int32
    ALU = mybir.AluOpType
    ACT = mybir.ActivationFunctionType
    AX = mybir.AxisListType
    ds = bass.ds

    ctx = ExitStack()
    with ctx:
        ctx.enter_context(nc.allow_non_contiguous_dma(reason="a few hundred strided words"))

        def sb(name, shape, dt=f32):
            return ctx.enter_context(nc.sbuf_tensor(name, shape, dt))

        def sem(name):
            return ctx.enter_context(nc.semaphore(name))

        msg_table = nc.dram_tensor("msg_table", [NODES_PAD, HID], f32).ap()
        count_table = nc.dram_tensor("count_table", [QROWS, NODES_PAD], bf16).ap()
        row_list = nc.dram_tensor("row_list", [4 * P * REPEATS, 1], i32).ap()
        general_agg = nc.dram_tensor("general_agg", [NODES_PAD + P, HID], f32).ap()
        general_out = nc.dram_tensor("general_out", [NODES_PAD + P, F], f32).ap()
        h_table = nc.dram_tensor("h_table", [NODES_PAD, F], f32).ap()

        x_sb = sb("x_sb", [P, GROUPS * 8, F])
        hT = sb("hT", [P, GROUPS, P])
        w1_pad = sb("w1_pad", [P, 8, HID])
        post_agg = sb("post_agg", [P, 2, HID])
        post2 = sb("post2", [P, 2, F])
        w_msg = sb("w_msg", [P, 2, HID])
        w_up = sb("w_up", [P, 2, HID])
        b1 = sb("b1", [P, 2])
        b2 = sb("b2", [P, 2])
        msg_bias = sb("msg_bias", [P, HID])
        pb1 = sb("pb1", [P, 2])
        up_bias = sb("up_bias", [P, 2])
        pb2 = sb("pb2", [P, F])
        ident = sb("ident", [P, P])
        ones = sb("ones", [P, P])
        part_sel = sb("part_sel", [3 * F, F])
        eps_col = sb("eps_col", [P, 1])
        stat_a = sb("stat_a", [P, GROUPS * 8])
        stat_b = sb("stat_b", [P, GROUPS * 8])

        agg = sb("agg", [P, 2, NODES_PAD + WINDOW])
        gat = sb("gat", [P, 2 * TILES, HID])
        adj = sb("adj", [P, SUPERS * TILES], bf16)
        slo = sb("slo", [P, SUPERS * TILES], bf16)
        key = sb("key", [P, SUPERS * TILES])
        w2, conv, post_h, w2T = (key[:, 2 * HID * i:2 * HID * (i + 1)].rearrange("p (k n) -> p k n", k=2)
                                 for i in range(4))
        b2_wide = key[:, 8 * HID:9 * HID].rearrange("p (k n) -> p k n", k=2)
        conv_b_wide = key[:, 9 * HID:10 * HID]
        src_i = sb("src_i", [P, SUPERS * TILES], i32)
        onehots = sb("onehots", [P, 2 * TILES * WINDOW + TILES * P + TILES * CNT])
        cnt = sb("cnt", [P, 2, CNT], bf16)
        cnt_max = sb("cnt_max", [P, CNT], bf16)
        idx = sb("idx", [P, 2, TILES], i32)
        iota_i = sb("iota_i", [P, CNT], i32)
        iota1 = sb("iota1", [P, CNT])
        iota0 = sb("iota0", [P, P])
        base_row = sb("base_row", [1, SUPERS], i32)
        base_i = sb("base_i", [P, 4], i32)
        six_i = sb("six_i", [P, 2, 4], i32)
        rho_i = sb("rho_i", [P, 4], i32)
        rho = sb("rho", [P, 4])
        rows_f = sb("rows_f", [P, 4, REPEATS])
        rows_i = sb("rows_i", [P, 4, REPEATS], i32)
        six_f = sb("six_f", [P, 4])
        bounds = sb("bounds", [P, 4, 4])
        row_idx = sb("row_idx", [P, QTILES], i32)
        ord_i = sb("ord_i", [P, 2, SORT_COLS], i32)
        ord_f = sb("ord_f", [P, SORT_COLS])
        bad = sb("bad", [P, 4])
        flag = sb("flag", [1, 1], i32)

        W = SUPERS * TILES
        over = agg[:, :, :].rearrange("p a n -> p (a n)")
        dst_i = over[:, 0:W].bitcast(i32)
        t_i = over[:, W:2 * W].bitcast(i32)
        dstf = over[:, 2 * W:3 * W]
        ta = over[:, 3 * W:4 * W]
        tb = over[:, 4 * W:5 * W]
        tc = over[:, 5 * W:6 * W]
        h0 = over[:, 6 * W:6 * W + GROUPS * 8 * F].rearrange("p (b f) -> p b f", f=F)
        bounds_wide = tb[:, 0:16 * P].rearrange("p (g v n) -> p g v n", g=4, v=4)
        n0 = 6 * W + GROUPS * 8 * F
        bound_all = over[:, n0:n0 + 2048].rearrange("p (v n) -> p v n", v=4)
        n0 += 2048
        near_i = over[:, n0:n0 + 512].bitcast(i32).rearrange("p (g s n) -> p g s n", g=4, s=2)
        near_f = over[:, n0 + 512:n0 + 1024].rearrange("p (g n) -> p g n", g=4)
        near_c = over[:, n0 + 1024:n0 + 1536].rearrange("p (g n) -> p g n", g=4)
        zT = gat[:, 0:8, :].rearrange("p a b -> p (a b)").rearrange("p (u k n) -> p u k n", u=2, k=2)
        m_raw = gat[:, 8:16, :].rearrange("p a b -> p (a b)").rearrange("p (u n) -> p u n", u=2)
        qT = gat[:, 8:12, :].rearrange("p a b -> p (a b)").rearrange("p (k n) -> p k n", k=2)
        n0, n1 = 2 * TILES * WINDOW, 2 * TILES * WINDOW + TILES * P
        oh_dst = onehots[:, 0:n0].rearrange("p (s k n) -> p s k n", s=2, k=TILES)
        oh_lo = onehots[:, n0:n1].bitcast(bf16).rearrange("p (s k n) -> p s k n", s=2, k=TILES)
        oh_key = onehots[:, n1:n1 + TILES * CNT].bitcast(bf16).rearrange("p (s k n) -> p s k n", s=2, k=TILES)
        m_sum = onehots[:, 0:2048].rearrange("p (s n) -> p s n", s=2)
        m_out = onehots[:, 2048:4096].rearrange("p (s n) -> p s n", s=2)
        o_sb = m_sum[:, :, :].rearrange("p a b -> p (a b)")[:, 0:BLOCKS * F].rearrange("p (b f) -> p b f", f=F)
        hb = m_out[:, :, :].rearrange("p a b -> p (a b)")[:, 0:BLOCKS * F].rearrange("p (b f) -> p b f", f=F)
        NB4 = 4
        ctiles = over[:, 0:NB4 * QTILES * CHUNK // 2].bitcast(bf16).rearrange("p (u c n) -> p u c n", u=NB4, c=QTILES)
        o0 = NB4 * QTILES * CHUNK // 2
        partsT = over[0:3 * F, o0:o0 + NODES_PAD]

        g0, gw = o0 + NODES_PAD, QTILES * F
        g_rows = over[:, g0:g0 + gw].rearrange("p (q f) -> p q f", f=F)
        g_rest = over[:, g0 + gw:g0 + 3 * gw].rearrange("p (s q f) -> p s q f", s=2, f=F)
        g_parts = over[:, g0 + 3 * gw:g0 + 3 * gw + 3 * gw // 2].bitcast(bf16).rearrange("p (q f) -> p q f", f=3 * F)

        dst_again = dst_i
        zeros = over[:, W:W + (BLOCKS + 1) * HID // 4]
        e_rows, e_summed, e_back = gat[:, 0, :], gat[:, 1, :], gat[:, 4, :]
        e_wide, e_same = gat[:, 2, 0:P], gat[:, 2, P:2 * P]
        e_lower, e_tmp = gat[:, 3, 0:P], gat[:, 3, P:2 * P]
        e_key, e_pad, e_dup, e_spare, e_count, e_gap, e_to = (gat[:, 5, i:i + 1] for i in range(7))
        e_from_i, e_to_i, e_spare_i, e_look_i = (gat[:, 6, i:i + 1].bitcast(i32) for i in range(4))

        ps = ctx.enter_context(nc.psum_tensor("ps", [P, 8, 512], f32))

        x_loaded = sem("x_loaded")
        edges_loaded = sem("edges_loaded")
        base_loaded = sem("base_loaded")
        weights_loaded = sem("weights_loaded")
        consts = sem("consts")
        w1_zero = sem("w1_zero")
        dve_step = sem("dve_step")
        pool_step = sem("pool_step")
        act_step = sem("act_step")
        var_ready = sem("var_ready")
        std_ready = sem("std_ready")
        h_ready = sem("h_ready")
        hT_done = sem("hT_done")
        hT_ready = sem("hT_ready")
        w2T_done = sem("w2T_done")
        w2T_ready = sem("w2T_ready")
        fused_done = sem("fused_done")
        fused_ready = sem("fused_ready")
        b2_ready = sem("b2_ready")
        near_asked = sem("near_asked")
        near_loaded = sem("near_loaded")
        bounds_ready = sem("bounds_ready")
        bounds_spread = sem("bounds_spread")
        rows_ready = sem("rows_ready")
        rows_stored = sem("rows_stored")
        rows_loaded = sem("rows_loaded")
        z_done = sem("z_done")
        zT_ready = sem("zT_ready")
        m_done = sem("m_done")
        m_copied = sem("m_copied")
        m_ready = sem("m_ready")
        m_added = sem("m_added")
        m_stored = [sem(f"m_stored{i}") for i in range(2)]
        agg_clear = sem("agg_clear")
        pad_rows_stored = sem("pad_rows_stored")
        idx_staged = sem("idx_staged")
        gathered = [sem(f"gathered{i}") for i in range(2 * TILES)]
        onehots_built = sem("onehots_built")
        tiles_used = sem("tiles_used")
        agg_added = sem("agg_added")
        counts_copied = sem("counts_copied")
        counts_maxed = sem("counts_maxed")
        counts_stored = [sem(f"counts_stored{i}") for i in range(2)]
        bad_ready = sem("bad_ready")
        bad_summed = sem("bad_summed")
        flag_ready = sem("flag_ready")
        u_done = sem("u_done")
        uT_ready = sem("uT_ready")
        q_done = sem("q_done")
        qT_ready = sem("qT_ready")
        o_done = sem("o_done")
        o_added = sem("o_added")
        tanh_done = sem("tanh_done")
        var2_ready = sem("var2_ready")
        std2_ready = sem("std2_ready")
        h2_ready = sem("h2_ready")
        h2_stored = sem("h2_stored")
        g_gathered = sem("g_gathered")
        g_split = sem("g_split")
        c_loaded = [sem(f"c_loaded{i}") for i in range(4)]
        chunk_done = sem("chunk_done")
        chunk_copied = sem("chunk_copied")
        sum_done = sem("sum_done")
        out_ready = sem("out_ready")
        out_stored = sem("out_stored")
        base_clear = sem("base_clear")
        bounds_taken = sem("bounds_taken")

        e_ready = [sem(f"e_ready{i}") for i in range(2)]
        e_zeroed = [sem(f"e_zeroed{i}") for i in range(2)]
        e_dst_loaded = [sem(f"e_dst_loaded{i}") for i in range(2)]
        e_consts = [sem(f"e_consts{i}") for i in range(2)]
        e_step = [sem(f"e_step{i}") for i in range(2)]
        e_asked = [sem(f"e_asked{i}") for i in range(2)]
        e_looked = sem("e_looked")
        e_gathered = [sem(f"e_gathered{i}") for i in range(2)]
        e_widened = [sem(f"e_widened{i}") for i in range(2)]
        e_turned = [sem(f"e_turned{i}") for i in range(2)]
        e_compared = [sem(f"e_compared{i}") for i in range(2)]
        e_placed = [sem(f"e_placed{i}") for i in range(2)]
        e_multiplied = [sem(f"e_multiplied{i}") for i in range(2)]
        e_copied = [sem(f"e_copied{i}") for i in range(2)]
        e_scattered = [sem(f"e_scattered{i}") for i in range(2)]
        b_loaded = sem("b_loaded")
        b_turned = sem("b_turned")
        b_copied = sem("b_copied")
        out_summed = sem("out_summed")
        general_loaded = sem("general_loaded")

        block = ctx.enter_context(nc.Block())

        EDGE_TILES = SUPERS * TILES
        width = (HID, F)

        def general_flag(eng):
            eng.wait_ge(flag_ready, 1)
            return eng.value_load(flag[0:1, 0:1], min_val=0, max_val=1) > 0

        def general_sp(sp, part):
            sp.wait_ge(e_ready[part], 1)
            sp.dma_start(dst_again, dst).then_inc(e_dst_loaded[part], 16)
            target = (general_agg, general_out)[part].rearrange("(p b) n -> p (b n)", p=P)
            step = min(target.shape[1], zeros.shape[1])
            for c in range(0, target.shape[1], step):
                sp.dma_start(target[:, c:c + step], zeros[:, 0:step]).then_inc(e_zeroed[part], 16)

        def general_pool(pool, part):
            pool.wait_ge(e_ready[part], 1)
            pool.iota(e_spare_i, [[0, 1]], base=NODES_PAD, channel_multiplier=1).then_inc(e_consts[part], 1)
            pool.affine_select(out=e_lower, in_=ones[:, :], compare_op=ALU.is_gt, fill=0.0, base=0,
                               pattern=[[-1, P]], channel_multiplier=1).then_inc(e_consts[part], 1)
            pool.wait_ge(e_zeroed[part], 16 * (4, 1)[part])
            asked = pool.alloc_register(f"asked{part}")
            looked = pool.alloc_register(f"looked{part}")
            placed = pool.alloc_register(f"placed{part}")
            pool.reg_mov(asked, 1)
            pool.reg_mov(looked, 16)
            pool.reg_mov(placed, 1)
            with pool.Fori(0, EDGE_TILES):
                pool.wait_ge(e_asked[part], asked)
                pool.reg_add(asked, asked, 1)
                if part == 1:
                    pool.indirect_dma_start(e_look_i, None, dst_flat[:].rearrange("(r n) -> r n", n=1),
                                            bass.IndirectOffsetOnAxis(ap=e_from_i, axis=0)).then_inc(e_looked, 16)
                    pool.wait_ge(e_looked, looked)
                    pool.reg_add(looked, looked, 16)
                pool.indirect_dma_start(e_rows[:, 0:width[part]], None, (msg_table, h_table)[part],
                                        bass.IndirectOffsetOnAxis(ap=(e_from_i, e_look_i)[part], axis=0))\
                    .then_inc(e_gathered[part], 16)
                pool.wait_ge(e_copied[part], placed)
                pool.wait_ge(e_placed[part], placed)
                pool.reg_add(placed, placed, 1)
                pool.indirect_dma_start((general_agg, general_out)[part], bass.IndirectOffsetOnAxis(ap=e_to_i, axis=0),
                                        e_summed[:, 0:width[part]], None, compute_op=ALU.add)\
                    .then_inc(e_scattered[part], 16)

        def general_act(act, part):
            with act.Fori(0, EDGE_TILES) as t:
                act.wait_ge(e_multiplied[part], t + 1)
                act.activation(e_summed[:, 0:width[part]], ps[:, 6, 0:width[part]], ACT.Copy).then_inc(e_copied[part], 1)

        def general_pe(pe, part):
            with pe.Fori(0, EDGE_TILES) as t:
                pe.wait_ge(e_widened[part], t + 1)
                pe.matmul(ps[:, 5, 0:P], e_wide, ident[:, :], start=True, stop=True).then_inc(e_turned[part], 1)
                pe.wait_ge(e_compared[part], t + 1)
                pe.wait_ge(e_gathered[part], 16 * (t + 1))
                pe.matmul(ps[:, 6, 0:width[part]], e_same, e_rows[:, 0:width[part]], start=True, stop=True)\
                    .then_inc(e_multiplied[part], 1)

        def general_dve(dve, part):
            dve.memset(zeros, 0.0).then_inc(e_ready[part], 1)
            dve.wait_ge(e_consts[part], 2)
            dve.tensor_copy(e_spare, e_spare_i)
            dve.wait_ge(e_dst_loaded[part], 16)
            steps = 9 if part else 7

            def tile(t, first=False):
                done = [0]

                def link(ins):
                    done[0] += 1
                    ins.then_inc(e_step[part], 1)
                    dve.wait_ge(e_step[part], steps * t + done[0])

                if not first:
                    dve.wait_ge(e_scattered[part], 16 * t)
                dve.tensor_scalar(e_from_i, (src_i[:, :], dst_again)[part][:, ds(t, 1)], 0.0, None, ALU.add).then_inc(e_asked[part], 1)
                link(dve.tensor_scalar(e_pad, dst_again[:, ds(t, 1)], float(NOWHERE), None, ALU.is_ge))
                if part == 0:
                    link(dve.tensor_scalar(e_key, dst_again[:, ds(t, 1)], 0.0, None, ALU.add))
                else:
                    link(dve.tensor_scalar(e_gap, e_pad, float(NOWHERE), None, ALU.mult))
                    link(dve.tensor_scalar(e_key, src_i[:, ds(t, 1)], 0.0, None, ALU.add))
                    link(dve.tensor_tensor(e_key, e_key, e_gap, ALU.add))
                dve.tensor_copy(e_wide, e_key.to_broadcast([P, P])).then_inc(e_widened[part], 1)
                dve.wait_ge(e_turned[part], t + 1)
                dve.tensor_scalar(e_same, ps[:, 5, 0:P], e_key, None, ALU.is_equal).then_inc(e_compared[part], 1)
                dve.wait_ge(e_compared[part], t + 1)
                link(dve.tensor_tensor(e_tmp, e_same, e_lower, ALU.mult))
                link(dve.tensor_reduce(e_count, e_tmp, AX.X, ALU.add))
                link(dve.scalar_tensor_tensor(out=e_dup, in0=e_count, scalar=0.0, in1=e_pad, op0=ALU.is_gt, op1=ALU.max))
                link(dve.tensor_tensor(e_gap, e_spare, e_key, ALU.subtract))
                link(dve.scalar_tensor_tensor(out=e_to, in0=e_gap, scalar=e_dup, in1=e_key, op0=ALU.mult, op1=ALU.add))
                assert done[0] == steps
                dve.tensor_copy(e_to_i, e_to).then_inc(e_placed[part], 1)

            tile(0, True)
            with dve.Fori(1, EDGE_TILES) as t:
                tile(t)
            dve.wait_ge(e_scattered[part], 16 * EDGE_TILES)

        @block.sync
        def _(sp):
            sp.dma_start(x_sb[:, :, :].rearrange("p b f -> p (b f)"), x).then_inc(x_loaded, 16)
            sp.dma_start(dst_i, dst).then_inc(edges_loaded, 16)
            sp.dma_start(src_i[:, :], src).then_inc(edges_loaded, 16)
            for s in range(2):
                sp.dma_start(ord_i[:, s, :], dst_flat[s:s + P * SORT_COLS].rearrange("(p n) -> p n", n=SORT_COLS))\
                  .then_inc(edges_loaded, 16)
            sp.wait_ge(rows_ready, 1)
            sp.dma_start(row_list.rearrange("(g p r) one -> p g (r one)", p=P, r=REPEATS), rows_i[:, :, :])\
              .then_inc(rows_stored, 16)
            sp.wait_ge(rows_stored, 16)
            sp.dma_start(row_idx[:, :], row_list[0:QROWS, :].rearrange("(c p) one -> p (c one)", p=P))\
              .then_inc(rows_loaded, 16)

            def store_messages(g, s, blocks=4):
                sp.wait_ge(m_ready, 2 * g + s + 1)
                rows = msg_table[ds((8 * g + 4 * s) * P, blocks * P), :].rearrange("(b p) n -> p b n", p=P)
                sp.dma_start(rows, m_out[:, s, 0:blocks * HID].rearrange("p (b n) -> p b n", n=HID))\
                  .then_inc(m_stored[s], 16)

            with sp.Fori(0, GROUPS - 1) as g:
                store_messages(g, 0)
                store_messages(g, 1)
            store_messages(GROUPS - 1, 0, 2)

            def store_counts(i, s):
                t = 2 * i + s
                sp.wait_ge(counts_copied, t + 1)
                rows = count_table[ds(t * REPEATS, REPEATS), :].rearrange("r (l h) -> l r h", h=BLOCKS)
                sp.dma_start(rows, cnt[:, s, :].rearrange("p (r h) -> p r h", r=REPEATS)).then_inc(counts_stored[s], 16)

            with sp.Fori(0, SUPERS // 2) as i:
                store_counts(i, 0)
                store_counts(i, 1)
            store_counts(SUPERS // 2, 0)

            with sp.If(general_flag(sp)):
                general_sp(sp, 0)
                sp.wait_ge(e_scattered[0], 16 * EDGE_TILES)

                def load_block(b, first=False):
                    if not first:
                        sp.wait_ge(b_turned, b)
                    sp.dma_start(e_back, general_agg[ds(b * P, P), :]).then_inc(b_loaded, 16)

                load_block(0, True)
                with sp.Fori(1, BLOCKS) as b:
                    load_block(b)

            sp.wait_ge(counts_stored[0], 16 * (SUPERS // 2 + 1))
            sp.wait_ge(counts_stored[1], 16 * (SUPERS // 2))
            sp.wait_ge(pad_rows_stored, 16)
            sp.wait_ge(q_done, UNITS)
            for c in range(CHUNKS):
                n = min(CHUNK, NODES_PAD - c * CHUNK)
                if c >= NB4:
                    sp.wait_ge(chunk_done, c - NB4 + 1)
                cols = count_table[:, c * CHUNK:c * CHUNK + n].rearrange("(q p) n -> p q n", p=P)
                sp.dma_start(ctiles[:, c % NB4, :, 0:n], cols).then_inc(c_loaded[c % NB4], 16)
            with sp.If(general_flag(sp)):
                general_sp(sp, 1)
                sp.wait_ge(e_scattered[1], 16 * EDGE_TILES)
                sp.dma_start(o_sb, general_out[0:NODES_PAD, :].rearrange("(b p) f -> p b f", p=P))\
                  .then_inc(general_loaded, 16)
            sp.wait_ge(out_ready, 1)
            sp.dma_start(out, hb.rearrange("p b f -> p (b f)")).then_inc(out_stored, 16)
            sp.wait_ge(out_stored, 16)

        @block.gpsimd
        def _(pool):
            pool.memset(w1_pad[:, :, :], 0.0).then_inc(w1_zero, 1)
            pool.memset(ones[:, :], 1.0).then_inc(pool_step, 1)
            pool.wait_ge(pool_step, 1)
            pool.affine_select(out=ident[:, :], in_=ones[:, :], compare_op=ALU.is_equal, fill=0.0, base=0,
                               pattern=[[-1, P]], channel_multiplier=1).then_inc(consts, 1)
            for part in range(3):
                if part == 0:
                    pool.memset(part_sel[:, :], 0.0).then_inc(pool_step, 1)
                pool.wait_ge(pool_step, 2 + part)
                pool.affine_select(out=part_sel[:, :], in_=part_sel[:, :], compare_op=ALU.not_equal, fill=1.0,
                                   base=-F * part, pattern=[[-1, F]], channel_multiplier=1).then_inc(pool_step, 1)
            pool.wait_ge(pool_step, 5)
            pool.iota(iota_i[:, :], [[1, CNT]], base=1, channel_multiplier=0).then_inc(consts, 1)
            pool.wait_ge(near_asked, 1)
            for g in range(4):
                for s in range(2):
                    pool.indirect_dma_start(near_i[:, g, s, :], None, dst_flat[:].rearrange("(r n) -> r n", n=64),
                                            bass.IndirectOffsetOnAxis(ap=six_i[:, s, g:g + 1], axis=0))\
                        .then_inc(near_loaded, 16)
                pool.indirect_dma_start(rho_i[:, g:g + 1], None, dst_flat[:].rearrange("(r n) -> r n", n=1),
                                        bass.IndirectOffsetOnAxis(ap=base_i[:, g:g + 1], axis=0))\
                    .then_inc(near_loaded, 16)

            added_wanted = pool.alloc_register("added_wanted")
            used_wanted = pool.alloc_register("used_wanted")
            pool.reg_mov(added_wanted, 1)
            pool.reg_mov(used_wanted, 1)

            def message_bias(g, s, first=False, cols=1024):
                u = 2 * g + s
                pool.wait_ge(m_copied, u + 1)
                pool.tensor_tensor(m_sum[:, s, 0:cols].rearrange("p (b n) -> p b n", n=HID),
                                   m_raw[:, s, 0:cols].rearrange("p (b n) -> p b n", n=HID),
                                   msg_bias[:, :].unsqueeze(1).to_broadcast([P, cols // HID, HID]),
                                   ALU.add).then_inc(m_added, 1)
                if not first:
                    pool.wait_ge(m_stored[s], 16 * g)
                pool.wait_ge(m_added, added_wanted)
                pool.reg_add(added_wanted, added_wanted, 1)
                pool.tensor_scalar(m_out[:, s, 0:cols], m_sum[:, s, 0:cols], 0.0, None, ALU.max).then_inc(m_ready, 1)

            message_bias(0, 0, True)
            message_bias(0, 1, True)
            with pool.Fori(1, GROUPS - 1) as g:
                message_bias(g, 0)
                message_bias(g, 1)
            message_bias(GROUPS - 1, 0, cols=2 * HID)
            pool.wait_ge(m_stored[0], 16 * GROUPS)
            pool.wait_ge(m_stored[1], 16 * (GROUPS - 1))

            def gather(i, s, first=False):
                t = 2 * i + s
                pool.wait_ge(idx_staged, t + 1)
                for k in range(TILES):
                    if isinstance(t, int) and t >= 2:
                        pool.wait_ge(tiles_used, TILES * (t - 2) + k + 1)
                    elif not first:
                        pool.wait_ge(tiles_used, used_wanted)
                        pool.reg_add(used_wanted, used_wanted, 1)
                    pool.indirect_dma_start(gat[:, s * TILES + k, :], None, msg_table,
                                            bass.IndirectOffsetOnAxis(ap=idx[:, s, k:k + 1], axis=0))\
                        .then_inc(gathered[s * TILES + k], 16)

            gather(0, 0, True)
            gather(0, 1, True)
            with pool.Fori(1, SUPERS // 2) as i:
                gather(i, 0)
                gather(i, 1)
            gather(SUPERS // 2, 0)

            with pool.If(general_flag(pool)):
                general_pool(pool, 0)

            pool.wait_ge(rows_loaded, 16)
            pool.wait_ge(h2_stored, 16)
            for c in range(QTILES):
                pool.indirect_dma_start(g_rows[:, c, :], None, h_table,
                                        bass.IndirectOffsetOnAxis(ap=row_idx[:, c:c + 1], axis=0))\
                    .then_inc(g_gathered, 16)
            pool.wait_ge(g_gathered, 16 * QTILES)
            with pool.If(general_flag(pool)):
                general_pool(pool, 1)

        @block.scalar
        def _(act):
            act.dma_start(base_row[:, :], dst_flat[:].rearrange("(t e) -> e t", e=SUPER)[0:1, :]).then_inc(base_loaded, 16)
            act.wait_ge(base_clear, 1)
            for g in range(4):
                n = min(P, SUPERS - g * P)
                act.dma_start(base_i[0:n, g:g + 1], dst_flat[:].rearrange("(t e) -> t e", e=SUPER)[g * P:g * P + n, 0:1])\
                   .then_inc(base_loaded, 16)
            for tile, dram in ((w2, pre_w2), (conv, conv_w), (post_h, post_w1[0:HID, :]),
                               (post_agg, post_w1[HID:2 * HID, :]), (post2, post_w2)):
                act.dma_start(tile[:, :, :], dram.rearrange("(k p) n -> p k n", p=P)).then_inc(weights_loaded, 16)
            for tile, dram in ((b1, pre_b1), (b2, pre_b2), (pb1, post_b1)):
                act.dma_start(tile[:, :], dram.rearrange("(k p) -> p k", p=P)).then_inc(weights_loaded, 16)
            act.dma_start(conv_b_wide[:, :], conv_b.partition_broadcast(P)).then_inc(weights_loaded, 16)
            act.dma_start(pb2[:, :], post_b2.partition_broadcast(P)).then_inc(weights_loaded, 16)
            act.wait_ge(w1_zero, 1)
            for b in range(8):
                act.dma_start(w1_pad[F * b:F * b + F, b, :], pre_w1).then_inc(weights_loaded, 16)
            act.wait_ge(var_ready, 1)
            act.activation(stat_b[:, :], stat_a[:, :], ACT.Sqrt, bias=eps_col[:, 0:1], scale=1.0 / F).then_inc(std_ready, 1)
            act.wait_ge(w2T_done, 1)
            act.activation(w2T[:, :, :].rearrange("p k n -> p (k n)"), ps[:, 4, :], ACT.Copy).then_inc(w2T_ready, 1)
            act.wait_ge(hT_done, 1)
            act.activation(hT[:, :, :].rearrange("p g n -> p (g n)"),
                           ps[:, 0:4, :].rearrange("p a b -> p (a b)")[:, 0:GROUPS * P], ACT.Copy).then_inc(hT_ready, 1)
            act.wait_ge(fused_done, 1)
            act.activation(w_msg[:, :, :].rearrange("p k n -> p (k n)"), ps[:, 5, :], ACT.Copy).then_inc(fused_ready, 1)
            act.activation(w_up[:, :, :].rearrange("p k n -> p (k n)"), ps[:, 6, :], ACT.Copy).then_inc(fused_ready, 1)
            act.wait_ge(weights_loaded, 16 * WEIGHT_LOADS)

            def relu_z(g, s, first=False):
                u = 2 * g + s
                act.wait_ge(z_done, u + 1)
                if not first:
                    act.wait_ge(m_done, u - 1)
                for k in range(2):
                    last = act.activation(zT[:, s, k, :], ps[:, 2 * s + k, :], ACT.Relu, bias=b1[:, k:k + 1])
                last.then_inc(zT_ready, 1)

            def copy_m(g, s, first=False, cols=1024):
                u = 2 * g + s
                act.wait_ge(m_done, u + 1)
                if not first:
                    act.wait_ge(m_added, u - 1)
                act.activation(m_raw[:, s, 0:cols],
                               ps[:, 4 + 2 * s:6 + 2 * s, :].rearrange("p a b -> p (a b)")[:, 0:cols],
                               ACT.Copy).then_inc(m_copied, 1)

            relu_z(0, 0, True)
            relu_z(0, 1, True)
            copy_m(0, 0, True)
            relu_z(1, 0)
            copy_m(0, 1, True)
            with act.Fori(1, GROUPS - 1) as g:
                relu_z(g, 1)
                copy_m(g, 0)
                relu_z(g + 1, 0)
                copy_m(g, 1)
            copy_m(GROUPS - 1, 0, cols=2 * HID)

            act.wait_ge(agg_clear, 1)
            n = QROWS - SUPERS * REPEATS
            act.dma_start(count_table[SUPERS * REPEATS:QROWS, :], agg[0:n, 0, 0:NODES_PAD // 2].bitcast(bf16))\
               .then_inc(pad_rows_stored, 16)

            def copy_counts(i, s, first=False):
                t = 2 * i + s
                act.wait_ge(tiles_used, TILES * (t + 1))
                if not first:
                    act.wait_ge(counts_stored[s], 16 * i)
                    act.wait_ge(counts_maxed, t - 1)
                act.activation(cnt[:, s, :], ps[:, 4 + s, 0:CNT], ACT.Copy).then_inc(counts_copied, 1)

            copy_counts(0, 0, True)
            copy_counts(0, 1, True)
            with act.Fori(1, SUPERS // 2) as i:
                copy_counts(i, 0)
                copy_counts(i, 1)
            copy_counts(SUPERS // 2, 0)

            with act.If(general_flag(act)):
                general_act(act, 0)
                with act.Fori(0, BLOCKS) as b:
                    act.wait_ge(b_turned, b + 1)
                    act.activation(agg[:, :, ds(b * P, P)], ps[:, 5, 0:2 * P].rearrange("p (k n) -> p k n", k=2),
                                   ACT.Copy).then_inc(b_copied, 1)

            def relu_u(g, s, first=False):
                u = 2 * g + s
                act.wait_ge(u_done, u + 1)
                if not first:
                    act.wait_ge(q_done, u - 1)
                for k in range(2):
                    last = act.activation(zT[:, s, k, :], ps[:, 2 * s + k, :], ACT.Relu, bias=b1[:, k:k + 1])
                last.then_inc(uT_ready, 1)

            def relu_q(g, s, first=False, n=CHUNK):
                u = 2 * g + s
                act.wait_ge(q_done, u + 1)
                if not first:
                    act.wait_ge(o_done, u)
                for k in range(2):
                    last = act.activation(qT[:, k, 0:n], ps[:, 4 + k, 0:n], ACT.Relu, bias=up_bias[:, k:k + 1])
                last.then_inc(qT_ready, 1)

            relu_u(0, 0, True)
            relu_q(0, 0, True)
            relu_u(0, 1, True)
            relu_q(0, 1)
            relu_u(1, 0)
            with act.Fori(1, GROUPS - 1) as g:
                relu_q(g, 0)
                relu_u(g, 1)
                relu_q(g, 1)
                relu_u(g + 1, 0)
            relu_q(GROUPS - 1, 0, n=2 * P)
            act.wait_ge(o_added, UNITS)
            act.activation(hb, o_sb, ACT.Tanh).then_inc(tanh_done, 1)
            act.wait_ge(var2_ready, 1)
            act.activation(stat_b[:, 0:BLOCKS], stat_a[:, 0:BLOCKS], ACT.Sqrt, bias=eps_col[:, 0:1], scale=1.0 / F)\
               .then_inc(std2_ready, 1)
            act.wait_ge(h2_ready, 1)
            act.dma_start(h_table.rearrange("(b p) f -> p b f", p=P), hb).then_inc(h2_stored, 16)
            for c in range(CHUNKS):
                n = min(CHUNK, NODES_PAD - c * CHUNK)
                act.wait_ge(chunk_done, c + 1)
                act.activation(partsT[:, c * CHUNK:c * CHUNK + n], ps[0:3 * F, c % 4, 0:n], ACT.Copy)\
                   .then_inc(chunk_copied, 1)
            act.wait_ge(h2_stored, 16)
            with act.If(general_flag(act)):
                general_act(act, 1)

        @block.vector
        def _(dve):
            chain = [0]

            def link(ins):
                chain[0] += 1
                ins.then_inc(dve_step, 1)
                dve.wait_ge(dve_step, chain[0])

            dve.memset(base_i[:, :], 0).then_inc(base_clear, 1)
            link(dve.memset(eps_col[:, :], EPS))
            link(dve.memset(bad[:, :], 0.0))
            dve.memset(cnt_max[:, :], 0.0)
            dve.wait_ge(x_loaded, 16)
            NB_PAD = GROUPS * 8

            def layernorm(values, centred, squares, total, deviation, n, ready, answer):
                link(dve.tensor_reduce(total[:, 0:n], values, AX.X, ALU.add))
                link(dve.tensor_scalar(total[:, 0:n], total[:, 0:n], 1.0 / F, None, ALU.mult))
                link(dve.tensor_tensor(centred, values, total[:, 0:n].unsqueeze(2).to_broadcast([P, n, F]), ALU.subtract))
                link(dve.tensor_tensor(squares, centred, centred, ALU.mult))
                dve.tensor_reduce(total[:, 0:n], squares, AX.X, ALU.add).then_inc(ready, 1)
                dve.wait_ge(answer, 1)
                link(dve.reciprocal(deviation[:, 0:n], deviation[:, 0:n]))
                link(dve.tensor_tensor(centred, centred, deviation[:, 0:n].unsqueeze(2).to_broadcast([P, n, F]), ALU.mult))

            layernorm(x_sb[:, :, :], h0, ta[:, 0:NB_PAD * F].rearrange("p (b f) -> p b f", f=F), stat_a, stat_b,
                      NB_PAD, var_ready, std_ready)
            dve.tensor_scalar(h0, h0, 0.0, None, ALU.max).then_inc(h_ready, 1)
            dve.wait_ge(weights_loaded, 16 * WEIGHT_LOADS)
            dve.tensor_copy(b2_wide[:, :, :], b2[:, :].unsqueeze(2).to_broadcast([P, 2, P])).then_inc(b2_ready, 1)
            dve.wait_ge(base_loaded, 16 * 5)
            link(dve.tensor_scalar(six_i[:, 0, :], base_i[:, :], 6, None, ALU.logical_shift_right))
            link(dve.tensor_copy(six_f[:, :], six_i[:, 0, :]))
            dve.tensor_scalar(six_i[:, 1, :], six_f[:, :], 1.0, None, ALU.add).then_inc(near_asked, 1)
            dve.tensor_copy(bounds[:, :, 0], base_i[:, :])
            dve.wait_ge(consts, 2)
            link(dve.tensor_copy(iota1[:, :], iota_i[:, :]))
            link(dve.tensor_scalar(iota0[:, :], iota1[:, 0:P], -1.0, None, ALU.add))
            dve.wait_ge(fused_done, 1)
            dve.tensor_tensor(msg_bias[:, :], ps[:, 7, 0:HID], conv_b_wide[:, :], ALU.add).then_inc(fused_ready, 1)
            dve.tensor_tensor(up_bias[:, :], ps[:, 7, HID:HID + 2], pb1[:, :], ALU.add).then_inc(fused_ready, 1)
            dve.wait_ge(near_loaded, 16 * 12)
            link(dve.tensor_copy(rho[:, :], rho_i[:, :]))
            link(dve.tensor_copy(near_f, near_i[:, :, :, :].rearrange("p g s n -> p g (s n)")))
            link(dve.tensor_scalar(six_f[:, :], six_f[:, :], 64.0, None, ALU.mult))
            for k in range(REPEATS):
                link(dve.tensor_scalar(rows_f[:, :, k], rho[:, :], float(k), None, ALU.add))
                link(dve.tensor_tensor(near_c, near_f, rows_f[:, :, k:k + 1].to_broadcast([P, 4, P]), ALU.is_le))
                link(dve.tensor_reduce(bounds[:, :, k + 1], near_c, AX.X, ALU.add))
                link(dve.tensor_tensor(bounds[:, :, k + 1], bounds[:, :, k + 1], six_f[:, :], ALU.add))
            dve.tensor_copy(rows_i[:, :, :], rows_f[:, :, :]).then_inc(rows_ready, 1)
            dve.tensor_copy(bounds_wide[:, :, :, :], bounds[:, :, :].unsqueeze(3).to_broadcast([P, 4, 4, P]))\
               .then_inc(bounds_ready, 1)
            dve.wait_ge(bounds_spread, 1)
            link(dve.tensor_copy(bound_all[:, :, :], ps[:, 0:4, :]))
            dve.nop().then_inc(bounds_taken, 1)

            def of_super(v):
                return bound_all[:, v, 0:SUPERS].unsqueeze(2).to_broadcast([P, SUPERS, TILES])

            def edges(a):
                return a.rearrange("p (t k) -> p t k", k=TILES)

            dve.wait_ge(edges_loaded, 16 * 4)
            link(dve.tensor_copy(dstf, dst_i))
            link(dve.tensor_tensor(edges(ta), edges(dstf), of_super(0), ALU.subtract))
            link(dve.tensor_scalar(tb, ta, 0.0, None, ALU.is_ge))
            link(dve.scalar_tensor_tensor(out=tb, in0=ta, scalar=float(WINDOW), in1=tb, op0=ALU.is_lt, op1=ALU.mult))
            link(dve.scalar_tensor_tensor(out=adj[:, :], in0=ta, scalar=1.0, in1=tb, op0=ALU.add, op1=ALU.mult))
            link(dve.tensor_tensor(edges(ta), edges(dstf), of_super(1), ALU.is_ge))
            link(dve.tensor_tensor(edges(tc), edges(dstf), of_super(2), ALU.is_ge))
            link(dve.tensor_tensor(ta, ta, tc, ALU.add))
            link(dve.tensor_tensor(edges(tc), edges(dstf), of_super(3), ALU.is_lt))
            link(dve.tensor_tensor(tb, tb, tc, ALU.mult))
            link(dve.tensor_scalar(t_i, src_i[:, :], 7, None, ALU.logical_shift_right))
            link(dve.tensor_copy(tc, t_i))
            link(dve.scalar_tensor_tensor(out=tc, in0=ta, scalar=float(BLOCKS), in1=tc, op0=ALU.mult, op1=ALU.add))
            link(dve.scalar_tensor_tensor(out=key[:, :], in0=tc, scalar=1.0, in1=tb, op0=ALU.add, op1=ALU.mult))
            link(dve.tensor_scalar(t_i, src_i[:, :], 127, None, ALU.bitwise_and))
            link(dve.tensor_copy(slo[:, :], t_i))
            link(dve.scalar_tensor_tensor(out=tc, in0=dstf, scalar=float(NOWHERE), in1=tb, op0=ALU.is_lt, op1=ALU.is_gt))
            link(dve.tensor_reduce(bad[:, 0:1], tc, AX.X, ALU.add))
            link(dve.tensor_copy(ord_f[:, :], ord_i[:, 0, :]))
            link(dve.tensor_copy(ta[:, 0:SORT_COLS], ord_i[:, 1, :]))
            link(dve.tensor_tensor(tc[:, 0:SORT_COLS], ord_f[:, :], ta[:, 0:SORT_COLS], ALU.is_gt))
            link(dve.tensor_reduce(bad[:, 1:2], tc[:, 0:SORT_COLS], AX.X, ALU.add))
            dve.wait_ge(hT_done, 1)
            link(dve.memset(agg[:, 0, :], 0.0))
            link(dve.memset(agg[:, 1, :], 0.0))
            dve.nop().then_inc(agg_clear, 1)

            def stage(t, s):
                dve.tensor_copy(idx[:, s, :], src_i[:, ds(t * TILES, TILES)]).then_inc(idx_staged, 1)

            def build(t, s):
                at = ds(t * TILES, TILES)
                dve.tensor_tensor(oh_dst[:, s, :, :], iota1[:, 0:WINDOW].unsqueeze(1).to_broadcast([P, TILES, WINDOW]),
                                  adj[:, at].unsqueeze(2).to_broadcast([P, TILES, WINDOW]), ALU.is_equal)
                dve.tensor_tensor(oh_lo[:, s, :, :], iota0[:, :].unsqueeze(1).to_broadcast([P, TILES, P]),
                                  slo[:, at].unsqueeze(2).to_broadcast([P, TILES, P]), ALU.is_equal)
                dve.tensor_tensor(oh_key[:, s, :, :], iota1[:, :].unsqueeze(1).to_broadcast([P, TILES, CNT]),
                                  key[:, at].unsqueeze(2).to_broadcast([P, TILES, CNT]), ALU.is_equal)\
                   .then_inc(onehots_built, 1)

            def add(t, s):
                dve.wait_ge(tiles_used, TILES * (t + 1))
                if not isinstance(t, int) or t > 0:
                    dve.wait_ge(agg_added, t)
                base = dve.value_load(base_row[0:1, ds(t, 1)], min_val=0, max_val=NODES_PAD)
                dve.tensor_tensor(agg[:, :, ds(base, WINDOW)], ps[:, 2 * s:2 * s + 2, 0:WINDOW],
                                  agg[:, :, ds(base, WINDOW)], ALU.add).then_inc(agg_added, 1)

            def largest(t, s):
                dve.wait_ge(counts_copied, t + 1)
                if not isinstance(t, int) or t > 0:
                    dve.wait_ge(counts_maxed, t)
                dve.tensor_tensor(cnt_max[:, :], cnt_max[:, :], cnt[:, s, :], ALU.max).then_inc(counts_maxed, 1)

            stage(0, 0)
            stage(1, 1)
            dve.wait_ge(m_stored[0], 16 * GROUPS)
            dve.wait_ge(m_stored[1], 16 * (GROUPS - 1))
            build(0, 0)
            build(1, 1)
            dve.wait_ge(pad_rows_stored, 16)
            add(0, 0)
            stage(2, 0)
            build(2, 0)
            add(1, 1)
            stage(3, 1)
            largest(0, 0)

            def step(t, s, more=True):
                if more:
                    build(t + 1, 1 - s)
                add(t, s)
                if more:
                    stage(t + 2, s)
                largest(t - 1, 1 - s)

            with dve.Fori(1, SUPERS // 2 - 1) as i:
                step(2 * i, 0)
                step(2 * i + 1, 1)
            LAST = SUPERS - 1
            build(LAST - 1, 1)
            add(LAST - 2, 0)
            stage(LAST, 0)
            largest(LAST - 3, 1)
            build(LAST, 0)
            add(LAST - 1, 1)
            largest(LAST - 2, 0)
            add(LAST, 0)
            largest(LAST - 1, 1)
            largest(LAST, 0)

            dve.wait_ge(counts_maxed, SUPERS)
            link(dve.tensor_reduce(bad[:, 2:3], cnt_max[:, :], AX.X, ALU.max))
            link(dve.tensor_scalar(bad[:, 2:3], bad[:, 2:3], COUNT_MAX, None, ALU.is_ge))
            link(dve.tensor_reduce(bad[:, 3:4], bad[:, 0:3], AX.X, ALU.add))
            dve.nop().then_inc(bad_ready, 1)
            dve.wait_ge(bad_summed, 1)
            dve.tensor_scalar(flag[:, :], ps[0:1, 6, 0:1], 0.0, None, ALU.is_gt).then_inc(flag_ready, 1)
            with dve.If(general_flag(dve)):
                dve.wait_ge(agg_added, SUPERS)
                general_dve(dve, 0)

            def add_out(g, s, blocks=4):
                u = 2 * g + s
                dve.wait_ge(o_done, u + 1)
                dve.tensor_tensor(o_sb[:, ds(u * 4, blocks), :],
                                  ps[:, 6 + s, 0:blocks * F].rearrange("p (b f) -> p b f", f=F),
                                  pb2[:, :].unsqueeze(1).to_broadcast([P, blocks, F]), ALU.add).then_inc(o_added, 1)

            with dve.Fori(0, GROUPS - 1) as g:
                add_out(g, 0)
                add_out(g, 1)
            add_out(GROUPS - 1, 0, 2)

            x1 = x_sb[:, 0:BLOCKS, :]
            dve.wait_ge(tanh_done, 1)
            link(dve.tensor_tensor(x1, x1, hb, ALU.add))
            layernorm(x1, hb, o_sb, stat_a, stat_b, BLOCKS, var2_ready, std2_ready)
            dve.tensor_scalar(hb, hb, 0.0, None, ALU.max).then_inc(h2_ready, 1)
            dve.wait_ge(g_gathered, 16 * QTILES)
            link(dve.tensor_copy(g_parts[:, :, 0:F], g_rows[:, :, :]))
            link(dve.tensor_tensor(g_rest[:, 0], g_rows[:, :, :], g_parts[:, :, 0:F], ALU.subtract))
            link(dve.tensor_copy(g_parts[:, :, F:2 * F], g_rest[:, 0]))
            link(dve.tensor_tensor(g_rest[:, 1], g_rest[:, 0], g_parts[:, :, F:2 * F], ALU.subtract))
            dve.tensor_copy(g_parts[:, :, 2 * F:3 * F], g_rest[:, 1]).then_inc(g_split, 1)
            dve.wait_ge(h2_stored, 16)
            dve.wait_ge(sum_done, 1)
            dve.tensor_tensor(hb, x1,
                              ps[:, 4:8, :].rearrange("p a b -> p (a b)")[:, 0:BLOCKS * F].rearrange("p (b f) -> p b f", f=F),
                              ALU.add).then_inc(out_summed, 1)
            dve.wait_ge(out_summed, 1)
            with dve.If(general_flag(dve)):
                general_dve(dve, 1)
                dve.wait_ge(general_loaded, 16)
                dve.tensor_tensor(hb, x1, o_sb, ALU.add).then_inc(out_summed, 1)
                dve.wait_ge(out_summed, 2)
            dve.nop().then_inc(out_ready, 1)

        @block.tensor
        def _(pe):
            pe.wait_ge(consts, 1)
            pe.wait_ge(weights_loaded, 16 * WEIGHT_LOADS)
            for jt in range(2):
                for it in range(2):
                    last = pe.transpose(ps[:, 4, jt * HID + it * P:jt * HID + it * P + P],
                                        w2[:, it, jt * P:jt * P + P], ident[:, :])
            last.then_inc(w2T_done, 1)
            pe.wait_ge(h_ready, 1)
            for g in range(GROUPS):
                last = pe.transpose(ps[:, g // 4, (g % 4) * P:(g % 4 + 1) * P],
                                    h0[:, 8 * g:8 * g + 8, :].rearrange("p b f -> p (b f)"), ident[:, :])
            last.then_inc(hT_done, 1)
            pe.wait_ge(w2T_ready, 1)
            pe.wait_ge(b2_ready, 1)
            for bank, right in ((5, conv), (6, post_h)):
                for it in range(2):
                    for jt in range(2):
                        pe.matmul(ps[:, bank, it * HID:(it + 1) * HID], w2T[:, jt, it * P:(it + 1) * P],
                                  right[:, jt, :], start=(jt == 0), stop=(jt == 1))
            for jt in range(2):
                pe.matmul(ps[:, 7, 0:HID], b2_wide[:, jt, :], conv[:, jt, :], start=(jt == 0), stop=(jt == 1))
            for m in range(2):
                for jt in range(2):
                    last = pe.matmul(ps[:, 7, HID + m:HID + m + 1], post_h[:, jt, m * P:(m + 1) * P],
                                     b2[:, jt:jt + 1], start=(jt == 0), stop=(jt == 1))
            last.then_inc(fused_done, 1)
            pe.wait_ge(hT_ready, 1)
            pe.wait_ge(bounds_ready, 1)
            for v in range(4):
                for g in range(4):
                    last = pe.matmul(ps[:, v, g * P:(g + 1) * P], bounds_wide[:, g, v, :], ident[:, :],
                                     start=True, stop=True)
            last.then_inc(bounds_spread, 1)
            pe.wait_ge(bounds_taken, 1)
            pe.wait_ge(fused_ready, 4)

            def hidden(g, s, done):
                for k in range(2):
                    for b in range(4):
                        last = pe.matmul(ps[:, 2 * s + k, b * P:(b + 1) * P], w1_pad[:, 4 * s + b, k * P:(k + 1) * P],
                                         hT[:, ds(g, 1), :].rearrange("p a n -> p (a n)"), start=True, stop=True)
                last.then_inc(done, 1)

            def z(g, s, first=False):
                if not first:
                    pe.wait_ge(zT_ready, 2 * g + s - 1)
                hidden(g, s, z_done)

            def messages(g, s, first=False, blocks=4):
                u = 2 * g + s
                pe.wait_ge(zT_ready, u + 1)
                if not first:
                    pe.wait_ge(m_copied, u - 1)
                for b in range(blocks):
                    for k in range(2):
                        last = pe.matmul(ps[:, 4 + 2 * s + b // 2, (b % 2) * HID:(b % 2 + 1) * HID],
                                         zT[:, s, k, b * P:(b + 1) * P], w_msg[:, k, :], start=(k == 0), stop=(k == 1))
                last.then_inc(m_done, 1)

            z(0, 0, True)
            z(0, 1, True)
            messages(0, 0, True)
            z(1, 0)
            messages(0, 1, True)
            with pe.Fori(1, GROUPS - 1) as g:
                z(g, 1)
                messages(g, 0)
                z(g + 1, 0)
                messages(g, 1)
            messages(GROUPS - 1, 0, blocks=2)
            pe.wait_ge(m_copied, UNITS)

            def add_up(i, s, first=False):
                t = 2 * i + s
                pe.wait_ge(onehots_built, t + 1)
                if not first:
                    pe.wait_ge(agg_added, t - 1)
                    pe.wait_ge(counts_copied, t - 1)
                for k in range(TILES):
                    pe.wait_ge(gathered[s * TILES + k], 16 * (i + 1))
                    for half in range(2):
                        pe.matmul(ps[:, 2 * s + half, 0:WINDOW], gat[:, s * TILES + k, half * P:(half + 1) * P],
                                  oh_dst[:, s, k, :], start=(k == 0), stop=(k == TILES - 1))
                    pe.matmul(ps[:, 4 + s, 0:CNT], oh_lo[:, s, k, :], oh_key[:, s, k, :],
                              start=(k == 0), stop=(k == TILES - 1)).then_inc(tiles_used, 1)

            add_up(0, 0, True)
            add_up(0, 1, True)
            with pe.Fori(1, SUPERS // 2) as i:
                add_up(i, 0)
                add_up(i, 1)
            add_up(SUPERS // 2, 0)
            pe.wait_ge(bad_ready, 1)
            pe.matmul(ps[:, 6, 0:1], ones[:, :], bad[:, 3:4], start=True, stop=True).then_inc(bad_summed, 1)
            with pe.If(general_flag(pe)):
                general_pe(pe, 0)

                def turn(b, first=False):
                    pe.wait_ge(b_loaded, 16 * (b + 1))
                    if not first:
                        pe.wait_ge(b_copied, b)
                    for k in range(2):
                        last = pe.transpose(ps[:, 5, k * P:(k + 1) * P], e_back[:, k * P:(k + 1) * P], ident[:, :])
                    last.then_inc(b_turned, 1)

                turn(0, True)
                with pe.Fori(1, BLOCKS) as b:
                    turn(b)
                pe.wait_ge(b_copied, BLOCKS)
            pe.wait_ge(agg_added, SUPERS)
            pe.wait_ge(counts_copied, SUPERS)

            def u_hidden(g, s, first=False):
                if not first:
                    pe.wait_ge(uT_ready, 2 * g + s - 1)
                hidden(g, s, u_done)

            def up(g, s, first=False, n=CHUNK):
                u = 2 * g + s
                pe.wait_ge(uT_ready, u + 1)
                if not first:
                    pe.wait_ge(qT_ready, u)
                for m in range(2):
                    for k in range(2):
                        pe.matmul(ps[:, 4 + m, 0:n], w_up[:, k, m * P:(m + 1) * P], zT[:, s, k, 0:n],
                                  start=(k == 0), stop=False)
                    for k in range(2):
                        last = pe.matmul(ps[:, 4 + m, 0:n], post_agg[:, k, m * P:(m + 1) * P],
                                         agg[:, k, ds(u * CHUNK, n)], start=False, stop=(k == 1))
                last.then_inc(q_done, 1)

            def down(g, s, first=False, blocks=4):
                u = 2 * g + s
                pe.wait_ge(qT_ready, u + 1)
                if not first:
                    pe.wait_ge(o_added, u - 1)
                for b in range(blocks):
                    for k in range(2):
                        last = pe.matmul(ps[:, 6 + s, b * F:(b + 1) * F], qT[:, k, b * P:(b + 1) * P], post2[:, k, :],
                                         start=(k == 0), stop=(k == 1))
                last.then_inc(o_done, 1)

            u_hidden(0, 0, True)
            up(0, 0, True)
            u_hidden(0, 1, True)
            down(0, 0, True)
            up(0, 1)
            u_hidden(1, 0)
            down(0, 1, True)
            with pe.Fori(1, GROUPS - 1) as g:
                up(g, 0)
                u_hidden(g, 1)
                down(g, 0)
                up(g, 1)
                u_hidden(g + 1, 0)
                down(g, 1)
            up(GROUPS - 1, 0, n=2 * P)
            down(GROUPS - 1, 0, blocks=2)
            pe.wait_ge(o_added, UNITS)

            pe.wait_ge(g_split, 1)
            for c in range(CHUNKS):
                n = min(CHUNK, NODES_PAD - c * CHUNK)
                pe.wait_ge(c_loaded[c % NB4], 16 * (c // NB4 + 1))
                if c >= 4:
                    pe.wait_ge(chunk_copied, c - 3)
                for q in range(QTILES):
                    last = pe.matmul(ps[0:3 * F, c % 4, 0:n], g_parts[:, q, :], ctiles[:, c % NB4, q, 0:n],
                                     start=(q == 0), stop=(q == QTILES - 1))
                last.then_inc(chunk_done, 1)
            pe.wait_ge(chunk_copied, CHUNKS)
            by_block = partsT.rearrange("r (l h) -> r l h", h=BLOCKS)
            for b in range(BLOCKS):
                last = pe.matmul(ps[:, 4 + b // 32, (b % 32) * F:(b % 32 + 1) * F], by_block[:, :, b], part_sel[:, :],
                                 start=True, stop=True)
            last.then_inc(sum_done, 1)
            with pe.If(general_flag(pe)):
                general_pe(pe, 1)


def kernel(**inputs):
    import numpy as np
    import concourse.bacc as bacc
    from concourse.bass_utils import run_bass_kernel_spmd

    a = {k: np.ascontiguousarray(v) for k, v in inputs.items()}
    x_pad = np.zeros((GROUPS * 8 * P, F), a["x"].dtype)
    x_pad[:N_NODES] = a["x"]
    src_pad = np.zeros(EDGES_PAD, a["src"].dtype)
    src_pad[:N_EDGES] = a["src"]
    dst_pad = np.full(EDGES_PAD, NOWHERE, a["dst"].dtype)
    dst_pad[:N_EDGES] = a["dst"]

    def by_partition(e):
        return np.ascontiguousarray(e.reshape(SUPERS, P, TILES).transpose(1, 0, 2).reshape(P, SUPERS * TILES))

    arrays = {
        "x": np.ascontiguousarray(x_pad.reshape(GROUPS * 8, P, F).transpose(1, 0, 2).reshape(P, GROUPS * 8 * F)),
        "src": by_partition(src_pad), "dst": by_partition(dst_pad), "dst_flat": dst_pad,
    }
    for name in ("pre_w1", "pre_b1", "pre_w2", "pre_b2", "conv_w", "conv_b", "post_w1", "post_b1", "post_w2", "post_b2"):
        arrays[name] = a["L0_gnn_" + name]
    nc = bacc.Bacc("TRN2", target_bir_lowering=False, num_devices=1)
    maps, args = {}, []
    for name, v in arrays.items():
        maps[f"in_{name}"] = v
        args.append(nc.dram_tensor(f"in_{name}", v.shape, mybir.dt.from_np(v.dtype), kind="ExternalInput").ap())
    args.append(nc.dram_tensor("result", (P, BLOCKS * F), mybir.dt.float32, kind="ExternalOutput").ap())
    gnn_kernel(nc, *args)
    r = run_bass_kernel_spmd(nc, [maps], core_ids=[0])
    y = r.results[0]["result"].reshape(P, BLOCKS, F).transpose(1, 0, 2).reshape(NODES_PAD, F)
    return np.ascontiguousarray(y[:N_NODES])
```

```python
import concourse.bass as bass
from concourse import mybir
from contextlib import ExitStack

P = 128
N_NODES = 12500
F = 16
HID = 256
N_EDGES = 412500
BLOCKS = -(-N_NODES // P)
GROUPS = -(-BLOCKS // 8)
UNITS = -(-BLOCKS // 4)
NODES_PAD = BLOCKS * P
TILES = 8
SUPER = TILES * P
SUPERS = -(-N_EDGES // SUPER)
EDGES_PAD = SUPERS * SUPER
WINDOW = 64
REPEATS = 3
NOWHERE = 16383
CNT = REPEATS * BLOCKS
QROWS = -(-SUPERS * REPEATS // P) * P
QTILES = QROWS // P
SORT_COLS = 100
CHUNK = 512
CHUNKS = -(-NODES_PAD // CHUNK)
PAIRS = SUPERS // 2
UNIT_PAIRS = PAIRS // UNITS
SLACK = 2
COUNT_MAX = 256.0
EPS = 1e-5
WEIGHT_LOADS = 14


def gnn_kernel(nc, x, src, dst, dst_flat, pre_w1, pre_b1, pre_w2, pre_b2, conv_w, conv_b,
               post_w1, post_b1, post_w2, post_b2, out):
    f32, bf16, i32 = mybir.dt.float32, mybir.dt.bfloat16, mybir.dt.int32
    ALU = mybir.AluOpType
    ACT = mybir.ActivationFunctionType
    AX = mybir.AxisListType
    ds = bass.ds

    ctx = ExitStack()
    with ctx:
        ctx.enter_context(nc.allow_non_contiguous_dma(reason="a few hundred strided words"))

        def sb(name, shape, dt=f32):
            return ctx.enter_context(nc.sbuf_tensor(name, shape, dt))

        def sem(name):
            return ctx.enter_context(nc.semaphore(name))

        msg_table = nc.dram_tensor("msg_table", [NODES_PAD, HID], f32).ap()
        count_table = nc.dram_tensor("count_table", [QROWS, NODES_PAD], bf16).ap()
        row_list = nc.dram_tensor("row_list", [4 * P * REPEATS, 1], i32).ap()
        general_agg = nc.dram_tensor("general_agg", [NODES_PAD + P, HID], f32).ap()
        general_out = nc.dram_tensor("general_out", [NODES_PAD + P, F], f32).ap()
        h_table = nc.dram_tensor("h_table", [NODES_PAD, F], f32).ap()

        x_sb = sb("x_sb", [P, GROUPS * 8, F])
        hT = sb("hT", [4 * F, UNITS, P])
        w1_unit = sb("w1_unit", [4 * F, 4, HID])
        post_agg = sb("post_agg", [P, 2, HID])
        post2 = sb("post2", [P, 2, F])
        w_msg = sb("w_msg", [P, 2, HID])
        w_up = sb("w_up", [P, 2, HID])
        b1 = sb("b1", [P, 2])
        b2 = sb("b2", [P, 2])
        msg_bias = sb("msg_bias", [P, HID])
        pb1 = sb("pb1", [P, 2])
        up_bias = sb("up_bias", [P, 2])
        pb2 = sb("pb2", [P, F])
        ident = sb("ident", [P, P])
        ones = sb("ones", [P, P])
        part_sel = sb("part_sel", [3 * F, F])
        eps_col = sb("eps_col", [P, 1])
        unit_zq = sb("unit_zq", [P, 2, CHUNK])
        unit_o = sb("unit_o", [P, 4, F])
        unit_t = sb("unit_t", [P, 4, F])
        unit_x = sb("unit_x", [P, 4, F])
        unit_h = sb("unit_h", [P, 4, F])
        unit_stat = sb("unit_stat", [P, 4])
        unit_dev = sb("unit_dev", [P, 4])
        stat_a = sb("stat_a", [P, GROUPS * 8])
        stat_b = sb("stat_b", [P, GROUPS * 8])

        agg = sb("agg", [P, 2, NODES_PAD + WINDOW])
        gat = sb("gat", [P, 2 * TILES, HID])
        adj = sb("adj", [P, SUPERS * TILES], bf16)
        slo = sb("slo", [P, SUPERS * TILES], bf16)
        key = sb("key", [P, SUPERS * TILES], mybir.dt.int16)
        w2, conv, post_h, w2T = (gat[:, 2 * i:2 * i + 2, :] for i in range(4))
        b2_wide = gat[:, 8, :].rearrange("p (k n) -> p k n", k=2)
        conv_b_wide = gat[:, 9, :]
        src_i = sb("src_i", [P, SUPERS * TILES], i32)
        onehots = sb("onehots", [P, 2 * TILES * WINDOW + TILES * P + TILES * CNT])
        cnt = sb("cnt", [P, 2, CNT], bf16)
        cnt_max = sb("cnt_max", [P, CNT], bf16)
        idx = sb("idx", [P, 2, TILES], i32)
        iota1 = sb("iota1", [P, CNT])
        iota0 = sb("iota0", [P, P])
        base_row = sb("base_row", [1, SUPERS], i32)
        base_i = sb("base_i", [P, 4], i32)
        six_i = sb("six_i", [P, 2, 4], i32)
        rho_i = sb("rho_i", [P, 4], i32)
        rho = sb("rho", [P, 4])
        rows_f = sb("rows_f", [P, 4, REPEATS])
        rows_i = sb("rows_i", [P, 4, REPEATS], i32)
        six_f = sb("six_f", [P, 4])
        bounds = sb("bounds", [P, 4, 4])
        row_idx = sb("row_idx", [P, QTILES], i32)
        bad = sb("bad", [P, 6])
        flag = sb("flag", [1, 2], i32)

        W = SUPERS * TILES
        over = agg[:, :, :].rearrange("p a n -> p (a n)")
        dst_i = over[:, 0:W].bitcast(i32)
        t_i = over[:, W:2 * W].bitcast(i32)
        dstf = over[:, 2 * W:3 * W]
        ta = over[:, 3 * W:4 * W]
        tb = over[:, 4 * W:5 * W]
        tc = over[:, 5 * W:6 * W]
        h0 = over[:, 6 * W:6 * W + GROUPS * 8 * F].rearrange("p (b f) -> p b f", f=F)
        bounds_wide = tb[:, 0:16 * P].rearrange("p (g v n) -> p g v n", g=4, v=4)
        n0 = 6 * W + GROUPS * 8 * F
        bound_all = over[:, n0:n0 + 2048].rearrange("p (v n) -> p v n", v=4)
        n0 += 2048
        near_i = over[:, n0:n0 + 512].bitcast(i32).rearrange("p (g s n) -> p g s n", g=4, s=2)
        near_f = over[:, n0 + 512:n0 + 1024].rearrange("p (g n) -> p g n", g=4)
        near_c = over[:, n0 + 1024:n0 + 1536].rearrange("p (g n) -> p g n", g=4)
        n0 += 1536
        iota_i = over[:, n0:n0 + CNT].bitcast(i32)
        ord_i = over[:, n0 + CNT:n0 + CNT + 2 * SORT_COLS].bitcast(i32).rearrange("p (s n) -> p s n", s=2)
        ord_f = over[:, n0 + CNT + 2 * SORT_COLS:n0 + CNT + 3 * SORT_COLS]
        base_f = over[0:1, W:W + SUPERS]
        zT = gat[:, 0:8, :].rearrange("p a b -> p (a b)").rearrange("p (u k n) -> p u k n", u=2, k=2)
        m_raw = gat[:, 8:16, :].rearrange("p a b -> p (a b)").rearrange("p (u n) -> p u n", u=2)
        n0, n1 = 2 * TILES * WINDOW, 2 * TILES * WINDOW + TILES * P
        oh_dst = onehots[:, 0:n0].rearrange("p (s k n) -> p s k n", s=2, k=TILES)
        oh_lo = onehots[:, n0:n1].bitcast(bf16).rearrange("p (s k n) -> p s k n", s=2, k=TILES)
        oh_key = onehots[:, n1:n1 + TILES * CNT].bitcast(bf16).rearrange("p (s k n) -> p s k n", s=2, k=TILES)
        m_sum = onehots[:, 0:2048].rearrange("p (s n) -> p s n", s=2)
        m_out = onehots[:, 2048:4096].rearrange("p (s n) -> p s n", s=2)
        o_sb = m_sum[:, :, :].rearrange("p a b -> p (a b)")[:, 0:BLOCKS * F].rearrange("p (b f) -> p b f", f=F)
        hb = m_out[:, :, :].rearrange("p a b -> p (a b)")[:, 0:BLOCKS * F].rearrange("p (b f) -> p b f", f=F)
        NB4 = 4
        ctiles = over[:, 0:NB4 * QTILES * CHUNK // 2].bitcast(bf16).rearrange("p (u c n) -> p u c n", u=NB4, c=QTILES)
        o0 = NB4 * QTILES * CHUNK // 2
        partsT = over[0:3 * F, o0:o0 + NODES_PAD]

        g0, gw = o0 + NODES_PAD, QTILES * F
        g_rows = over[:, g0:g0 + gw].rearrange("p (q f) -> p q f", f=F)
        g_rest = over[:, g0 + gw:g0 + 3 * gw].rearrange("p (s q f) -> p s q f", s=2, f=F)
        g_parts = over[:, g0 + 3 * gw:g0 + 3 * gw + 3 * gw // 2].bitcast(bf16).rearrange("p (q f) -> p q f", f=3 * F)

        dst_again = dst_i
        zeros = over[:, W:W + (BLOCKS + 1) * HID // 4]
        e_rows, e_summed, e_back = gat[:, 0, :], gat[:, 1, :], gat[:, 4, :]
        e_wide, e_same = gat[:, 2, 0:P], gat[:, 2, P:2 * P]
        e_lower, e_tmp = gat[:, 3, 0:P], gat[:, 3, P:2 * P]
        e_key, e_pad, e_dup, e_spare, e_count, e_gap, e_to = (gat[:, 5, i:i + 1] for i in range(7))
        e_from_i, e_to_i, e_spare_i, e_look_i = (gat[:, 6, i:i + 1].bitcast(i32) for i in range(4))

        ps = ctx.enter_context(nc.psum_tensor("ps", [P, 8, 512], f32))

        x_loaded = sem("x_loaded")
        edges_loaded = sem("edges_loaded")
        base_loaded = sem("base_loaded")
        weights_loaded = sem("weights_loaded")
        consts = sem("consts")
        w1_zero = sem("w1_zero")
        dve_step = sem("dve_step")
        pool_step = sem("pool_step")
        act_step = sem("act_step")
        var_ready = sem("var_ready")
        std_ready = sem("std_ready")
        h_ready = sem("h_ready")
        hT_done = sem("hT_done")
        hT_ready = sem("hT_ready")
        w2T_done = sem("w2T_done")
        w2T_ready = sem("w2T_ready")
        fused_done = sem("fused_done")
        fused_ready = sem("fused_ready")
        b2_ready = sem("b2_ready")
        near_asked = sem("near_asked")
        near_loaded = sem("near_loaded")
        bounds_ready = sem("bounds_ready")
        bounds_spread = sem("bounds_spread")
        rows_ready = sem("rows_ready")
        rows_stored = sem("rows_stored")
        rows_loaded = sem("rows_loaded")
        z_done = sem("z_done")
        zT_ready = sem("zT_ready")
        m_done = sem("m_done")
        m_copied = sem("m_copied")
        m_ready = sem("m_ready")
        m_added = sem("m_added")
        m_stored = [sem(f"m_stored{i}") for i in range(2)]
        agg_clear = sem("agg_clear")
        pad_rows_stored = sem("pad_rows_stored")
        idx_staged = sem("idx_staged")
        gathered = [sem(f"gathered{i}") for i in range(2 * TILES)]
        onehots_built = sem("onehots_built")
        tiles_used = sem("tiles_used")
        agg_added = sem("agg_added")
        counts_copied = sem("counts_copied")
        counts_maxed = sem("counts_maxed")
        counts_stored = [sem(f"counts_stored{i}") for i in range(2)]
        bad_ready = sem("bad_ready")
        bad_summed = sem("bad_summed")
        flag_ready = sem("flag_ready")
        unit_step = sem("unit_step")
        u_done = sem("u_done")
        uT_ready = sem("uT_ready")
        q_done = sem("q_done")
        qT_ready = sem("qT_ready")
        o_done = sem("o_done")
        o_added = sem("o_added")
        o_tanh = sem("o_tanh")
        var2_ready = sem("var2_ready")
        std2_ready = sem("std2_ready")
        h2_ready = sem("h2_ready")
        h2_stored = sem("h2_stored")
        g_gathered = sem("g_gathered")
        g_split = sem("g_split")
        c_loaded = [sem(f"c_loaded{i}") for i in range(4)]
        chunk_done = sem("chunk_done")
        chunk_copied = sem("chunk_copied")
        sum_done = sem("sum_done")
        out_ready = sem("out_ready")
        out_stored = sem("out_stored")
        base_clear = sem("base_clear")
        bounds_taken = sem("bounds_taken")

        e_ready = [sem(f"e_ready{i}") for i in range(2)]
        e_zeroed = [sem(f"e_zeroed{i}") for i in range(2)]
        e_dst_loaded = [sem(f"e_dst_loaded{i}") for i in range(2)]
        e_consts = [sem(f"e_consts{i}") for i in range(2)]
        e_step = [sem(f"e_step{i}") for i in range(2)]
        e_asked = [sem(f"e_asked{i}") for i in range(2)]
        e_looked = sem("e_looked")
        e_gathered = [sem(f"e_gathered{i}") for i in range(2)]
        e_widened = [sem(f"e_widened{i}") for i in range(2)]
        e_turned = [sem(f"e_turned{i}") for i in range(2)]
        e_compared = [sem(f"e_compared{i}") for i in range(2)]
        e_placed = [sem(f"e_placed{i}") for i in range(2)]
        e_multiplied = [sem(f"e_multiplied{i}") for i in range(2)]
        e_copied = [sem(f"e_copied{i}") for i in range(2)]
        e_scattered = [sem(f"e_scattered{i}") for i in range(2)]
        b_loaded = sem("b_loaded")
        b_turned = sem("b_turned")
        b_copied = sem("b_copied")
        out_summed = sem("out_summed")
        general_summed = sem("general_summed")
        late_step = sem("late_step")
        general_loaded = sem("general_loaded")

        block = ctx.enter_context(nc.Block())

        EDGE_TILES = SUPERS * TILES
        width = (HID, F)

        def flag_of(eng, which):
            eng.wait_ge(flag_ready, which + 1)
            return eng.value_load(flag[0:1, which:which + 1], min_val=0, max_val=1)

        def general_sp(sp, part):
            sp.wait_ge(e_ready[part], 1)
            sp.dma_start(dst_again, dst).then_inc(e_dst_loaded[part], 16)
            target = (general_agg, general_out)[part].rearrange("(p b) n -> p (b n)", p=P)
            step = min(target.shape[1], zeros.shape[1])
            for c in range(0, target.shape[1], step):
                sp.dma_start(target[:, c:c + step], zeros[:, 0:step]).then_inc(e_zeroed[part], 16)

        def general_pool(pool, part):
            pool.wait_ge(e_ready[part], 1)
            pool.iota(e_spare_i, [[0, 1]], base=NODES_PAD, channel_multiplier=1).then_inc(e_consts[part], 1)
            pool.affine_select(out=e_lower, in_=ones[:, :], compare_op=ALU.is_gt, fill=0.0, base=0,
                               pattern=[[-1, P]], channel_multiplier=1).then_inc(e_consts[part], 1)
            pool.wait_ge(e_zeroed[part], 16 * (4, 1)[part])
            asked = pool.alloc_register(f"asked{part}")
            looked = pool.alloc_register(f"looked{part}")
            placed = pool.alloc_register(f"placed{part}")
            pool.reg_mov(asked, 1)
            pool.reg_mov(looked, 16)
            pool.reg_mov(placed, 1)
            with pool.Fori(0, EDGE_TILES):
                pool.wait_ge(e_asked[part], asked)
                pool.reg_add(asked, asked, 1)
                if part == 1:
                    pool.indirect_dma_start(e_look_i, None, dst_flat[:].rearrange("(r n) -> r n", n=1),
                                            bass.IndirectOffsetOnAxis(ap=e_from_i, axis=0)).then_inc(e_looked, 16)
                    pool.wait_ge(e_looked, looked)
                    pool.reg_add(looked, looked, 16)
                pool.indirect_dma_start(e_rows[:, 0:width[part]], None, (msg_table, h_table)[part],
                                        bass.IndirectOffsetOnAxis(ap=(e_from_i, e_look_i)[part], axis=0))\
                    .then_inc(e_gathered[part], 16)
                pool.wait_ge(e_copied[part], placed)
                pool.wait_ge(e_placed[part], placed)
                pool.reg_add(placed, placed, 1)
                pool.indirect_dma_start((general_agg, general_out)[part], bass.IndirectOffsetOnAxis(ap=e_to_i, axis=0),
                                        e_summed[:, 0:width[part]], None, compute_op=ALU.add)\
                    .then_inc(e_scattered[part], 16)

        def general_act(act, part):
            with act.Fori(0, EDGE_TILES) as t:
                act.wait_ge(e_multiplied[part], t + 1)
                act.activation(e_summed[:, 0:width[part]], ps[:, 6, 0:width[part]], ACT.Copy).then_inc(e_copied[part], 1)

        def general_pe(pe, part):
            with pe.Fori(0, EDGE_TILES) as t:
                pe.wait_ge(e_widened[part], t + 1)
                pe.matmul(ps[:, 5, 0:P], e_wide, ident[:, :], start=True, stop=True).then_inc(e_turned[part], 1)
                pe.wait_ge(e_compared[part], t + 1)
                pe.wait_ge(e_gathered[part], 16 * (t + 1))
                pe.matmul(ps[:, 6, 0:width[part]], e_same, e_rows[:, 0:width[part]], start=True, stop=True)\
                    .then_inc(e_multiplied[part], 1)

        def general_dve(dve, part):
            dve.memset(zeros, 0.0).then_inc(e_ready[part], 1)
            dve.wait_ge(e_consts[part], 2)
            dve.tensor_copy(e_spare, e_spare_i)
            dve.wait_ge(e_dst_loaded[part], 16)
            steps = 9 if part else 7

            def tile(t, first=False):
                done = [0]

                def link(ins):
                    done[0] += 1
                    ins.then_inc(e_step[part], 1)
                    dve.wait_ge(e_step[part], steps * t + done[0])

                if not first:
                    dve.wait_ge(e_scattered[part], 16 * t)
                dve.tensor_scalar(e_from_i, (src_i[:, :], dst_again)[part][:, ds(t, 1)], 0.0, None, ALU.add).then_inc(e_asked[part], 1)
                link(dve.tensor_scalar(e_pad, dst_again[:, ds(t, 1)], float(NOWHERE), None, ALU.is_ge))
                if part == 0:
                    link(dve.tensor_scalar(e_key, dst_again[:, ds(t, 1)], 0.0, None, ALU.add))
                else:
                    link(dve.tensor_scalar(e_gap, e_pad, float(NOWHERE), None, ALU.mult))
                    link(dve.tensor_scalar(e_key, src_i[:, ds(t, 1)], 0.0, None, ALU.add))
                    link(dve.tensor_tensor(e_key, e_key, e_gap, ALU.add))
                dve.tensor_copy(e_wide, e_key.to_broadcast([P, P])).then_inc(e_widened[part], 1)
                dve.wait_ge(e_turned[part], t + 1)
                dve.tensor_scalar(e_same, ps[:, 5, 0:P], e_key, None, ALU.is_equal).then_inc(e_compared[part], 1)
                dve.wait_ge(e_compared[part], t + 1)
                link(dve.tensor_tensor(e_tmp, e_same, e_lower, ALU.mult))
                link(dve.tensor_reduce(e_count, e_tmp, AX.X, ALU.add))
                link(dve.scalar_tensor_tensor(out=e_dup, in0=e_count, scalar=0.0, in1=e_pad, op0=ALU.is_gt, op1=ALU.max))
                link(dve.tensor_tensor(e_gap, e_spare, e_key, ALU.subtract))
                link(dve.scalar_tensor_tensor(out=e_to, in0=e_gap, scalar=e_dup, in1=e_key, op0=ALU.mult, op1=ALU.add))
                assert done[0] == steps
                dve.tensor_copy(e_to_i, e_to).then_inc(e_placed[part], 1)

            tile(0, True)
            with dve.Fori(1, EDGE_TILES) as t:
                tile(t)
            dve.wait_ge(e_scattered[part], 16 * EDGE_TILES)

        @block.sync
        def _(sp):
            sp.dma_start(x_sb[:, :, :].rearrange("p b f -> p (b f)"), x).then_inc(x_loaded, 16)
            sp.dma_start(dst_i, dst).then_inc(edges_loaded, 16)
            sp.dma_start(src_i[:, :], src).then_inc(edges_loaded, 16)
            for s in range(2):
                sp.dma_start(ord_i[:, s, :], dst_flat[s:s + P * SORT_COLS].rearrange("(p n) -> p n", n=SORT_COLS))\
                  .then_inc(edges_loaded, 16)
            sp.wait_ge(rows_ready, 1)
            sp.dma_start(row_list.rearrange("(g p r) one -> p g (r one)", p=P, r=REPEATS), rows_i[:, :, :])\
              .then_inc(rows_stored, 16)
            sp.wait_ge(rows_stored, 16)
            sp.dma_start(row_idx[:, :], row_list[0:QROWS, :].rearrange("(c p) one -> p (c one)", p=P))\
              .then_inc(rows_loaded, 16)

            def store_messages(g, s, blocks=4):
                sp.wait_ge(m_ready, 2 * g + s + 1)
                rows = msg_table[ds((8 * g + 4 * s) * P, blocks * P), :].rearrange("(b p) n -> p b n", p=P)
                sp.dma_start(rows, m_out[:, s, 0:blocks * HID].rearrange("p (b n) -> p b n", n=HID))\
                  .then_inc(m_stored[s], 16)

            with sp.Fori(0, GROUPS - 1) as g:
                store_messages(g, 0)
                store_messages(g, 1)
            store_messages(GROUPS - 1, 0, 2)

            def store_counts(i, s):
                t = 2 * i + s
                sp.wait_ge(counts_copied, t + 1)
                rows = count_table[ds(t * REPEATS, REPEATS), :].rearrange("r (l h) -> l r h", h=BLOCKS)
                sp.dma_start(rows, cnt[:, s, :].rearrange("p (r h) -> p r h", r=REPEATS)).then_inc(counts_stored[s], 16)

            with sp.If(flag_of(sp, 0) < 1):
                with sp.Fori(0, PAIRS) as i:
                    store_counts(i, 0)
                    store_counts(i, 1)
                store_counts(PAIRS, 0)

                sp.wait_ge(counts_stored[0], 16 * (PAIRS + 1))
                sp.wait_ge(counts_stored[1], 16 * PAIRS)
                sp.wait_ge(pad_rows_stored, 16)
                sp.wait_ge(q_done, UNITS)
                for c in range(CHUNKS):
                    n = min(CHUNK, NODES_PAD - c * CHUNK)
                    if c >= NB4:
                        sp.wait_ge(chunk_done, c - NB4 + 1)
                    cols = count_table[:, c * CHUNK:c * CHUNK + n].rearrange("(q p) n -> p q n", p=P)
                    sp.dma_start(ctiles[:, c % NB4, :, 0:n], cols).then_inc(c_loaded[c % NB4], 16)

            with sp.If(flag_of(sp, 0) > 0):
                general_sp(sp, 0)
                sp.wait_ge(e_scattered[0], 16 * EDGE_TILES)

                def load_block(b, first=False):
                    if not first:
                        sp.wait_ge(b_turned, b)
                    sp.dma_start(e_back, general_agg[ds(b * P, P), :]).then_inc(b_loaded, 16)

                load_block(0, True)
                with sp.Fori(1, BLOCKS) as b:
                    load_block(b)

            with sp.If(flag_of(sp, 1) > 0):
                general_sp(sp, 1)
                sp.wait_ge(e_scattered[1], 16 * EDGE_TILES)
                sp.dma_start(o_sb, general_out[0:NODES_PAD, :].rearrange("(b p) f -> p b f", p=P))\
                  .then_inc(general_loaded, 16)
            sp.wait_ge(out_ready, 1)
            sp.dma_start(out, hb.rearrange("p b f -> p (b f)")).then_inc(out_stored, 16)
            sp.wait_ge(out_stored, 16)

        @block.gpsimd
        def _(pool):
            pool.memset(w1_unit[:, :, :], 0.0).then_inc(w1_zero, 1)
            pool.memset(ones[:, :], 1.0).then_inc(pool_step, 1)
            pool.wait_ge(pool_step, 1)
            pool.affine_select(out=ident[:, :], in_=ones[:, :], compare_op=ALU.is_equal, fill=0.0, base=0,
                               pattern=[[-1, P]], channel_multiplier=1).then_inc(consts, 1)
            for part in range(3):
                if part == 0:
                    pool.memset(part_sel[:, :], 0.0).then_inc(pool_step, 1)
                pool.wait_ge(pool_step, 2 + part)
                pool.affine_select(out=part_sel[:, :], in_=part_sel[:, :], compare_op=ALU.not_equal, fill=1.0,
                                   base=-F * part, pattern=[[-1, F]], channel_multiplier=1).then_inc(pool_step, 1)
            pool.wait_ge(pool_step, 5)
            pool.iota(iota_i[:, :], [[1, CNT]], base=1, channel_multiplier=0).then_inc(consts, 1)
            pool.wait_ge(near_asked, 1)
            for g in range(4):
                for s in range(2):
                    pool.indirect_dma_start(near_i[:, g, s, :], None, dst_flat[:].rearrange("(r n) -> r n", n=64),
                                            bass.IndirectOffsetOnAxis(ap=six_i[:, s, g:g + 1], axis=0))\
                        .then_inc(near_loaded, 16)
                pool.indirect_dma_start(rho_i[:, g:g + 1], None, dst_flat[:].rearrange("(r n) -> r n", n=1),
                                        bass.IndirectOffsetOnAxis(ap=base_i[:, g:g + 1], axis=0))\
                    .then_inc(near_loaded, 16)

            added_wanted = pool.alloc_register("added_wanted")
            used_wanted = pool.alloc_register("used_wanted")
            pool.reg_mov(added_wanted, 1)
            pool.reg_mov(used_wanted, 1)

            def message_bias(g, s, first=False, cols=1024):
                u = 2 * g + s
                pool.wait_ge(m_copied, u + 1)
                pool.tensor_tensor(m_sum[:, s, 0:cols].rearrange("p (b n) -> p b n", n=HID),
                                   m_raw[:, s, 0:cols].rearrange("p (b n) -> p b n", n=HID),
                                   msg_bias[:, :].unsqueeze(1).to_broadcast([P, cols // HID, HID]),
                                   ALU.add).then_inc(m_added, 1)
                if not first:
                    pool.wait_ge(m_stored[s], 16 * g)
                pool.wait_ge(m_added, added_wanted)
                pool.reg_add(added_wanted, added_wanted, 1)
                pool.tensor_scalar(m_out[:, s, 0:cols], m_sum[:, s, 0:cols], 0.0, None, ALU.max).then_inc(m_ready, 1)

            message_bias(0, 0, True)
            message_bias(0, 1, True)
            with pool.Fori(1, GROUPS - 1) as g:
                message_bias(g, 0)
                message_bias(g, 1)
            message_bias(GROUPS - 1, 0, cols=2 * HID)
            pool.wait_ge(m_stored[0], 16 * GROUPS)
            pool.wait_ge(m_stored[1], 16 * (GROUPS - 1))

            def gather(i, s, first=False):
                t = 2 * i + s
                pool.wait_ge(idx_staged, t + 1)
                for k in range(TILES):
                    if isinstance(t, int) and t >= 2:
                        pool.wait_ge(tiles_used, TILES * (t - 2) + k + 1)
                    elif not first:
                        pool.wait_ge(tiles_used, used_wanted)
                        pool.reg_add(used_wanted, used_wanted, 1)
                    pool.indirect_dma_start(gat[:, s * TILES + k, :], None, msg_table,
                                            bass.IndirectOffsetOnAxis(ap=idx[:, s, k:k + 1], axis=0))\
                        .then_inc(gathered[s * TILES + k], 16)

            with pool.If(flag_of(pool, 0) < 1):
                gather(0, 0, True)
                gather(0, 1, True)
                with pool.Fori(1, PAIRS) as i:
                    gather(i, 0)
                    gather(i, 1)
                gather(PAIRS, 0)

                pool.wait_ge(rows_loaded, 16)
                pool.wait_ge(h2_stored, 16 * UNITS)
                for c in range(QTILES):
                    pool.indirect_dma_start(g_rows[:, c, :], None, h_table,
                                            bass.IndirectOffsetOnAxis(ap=row_idx[:, c:c + 1], axis=0))\
                        .then_inc(g_gathered, 16)
                pool.wait_ge(g_gathered, 16 * QTILES)
            with pool.If(flag_of(pool, 0) > 0):
                general_pool(pool, 0)
            with pool.If(flag_of(pool, 1) > 0):
                general_pool(pool, 1)

        @block.scalar
        def _(act):
            act.dma_start(base_row[:, :], dst_flat[:].rearrange("(t e) -> e t", e=SUPER)[0:1, :]).then_inc(base_loaded, 16)
            act.wait_ge(base_clear, 1)
            for g in range(4):
                n = min(P, SUPERS - g * P)
                act.dma_start(base_i[0:n, g:g + 1], dst_flat[:].rearrange("(t e) -> t e", e=SUPER)[g * P:g * P + n, 0:1])\
                   .then_inc(base_loaded, 16)
            for tile, dram in ((w2, pre_w2), (conv, conv_w), (post_h, post_w1[0:HID, :]),
                               (post_agg, post_w1[HID:2 * HID, :]), (post2, post_w2)):
                act.dma_start(tile[:, :, :], dram.rearrange("(k p) n -> p k n", p=P)).then_inc(weights_loaded, 16)
            for tile, dram in ((b1, pre_b1), (b2, pre_b2), (pb1, post_b1)):
                act.dma_start(tile[:, :], dram.rearrange("(k p) -> p k", p=P)).then_inc(weights_loaded, 16)
            act.dma_start(conv_b_wide[:, :], conv_b.partition_broadcast(P)).then_inc(weights_loaded, 16)
            act.dma_start(pb2[:, :], post_b2.partition_broadcast(P)).then_inc(weights_loaded, 16)
            act.wait_ge(w1_zero, 1)
            for b in range(4):
                act.dma_start(w1_unit[F * b:F * b + F, b, :], pre_w1).then_inc(weights_loaded, 16)
            act.wait_ge(var_ready, 1)
            act.activation(stat_b[:, :], stat_a[:, :], ACT.Sqrt, bias=eps_col[:, 0:1], scale=1.0 / F).then_inc(std_ready, 1)
            act.wait_ge(w2T_done, 1)
            act.activation(w2T[:, :, :].rearrange("p k n -> p (k n)"), ps[:, 4, :], ACT.Copy).then_inc(w2T_ready, 1)
            for first, last in ((0, 16), (16, UNITS)):
                act.wait_ge(hT_done, 1 + first // 16)
                act.activation(hT[:, first:last, :].rearrange("p g n -> p (g n)"),
                               ps[0:4 * F, 0:4, :].rearrange("p a b -> p (a b)")[:, 0:(last - first) * P],
                               ACT.Copy).then_inc(hT_ready, 1)
            act.wait_ge(fused_done, 1)
            act.activation(w_msg[:, :, :].rearrange("p k n -> p (k n)"), ps[:, 5, :], ACT.Copy).then_inc(fused_ready, 1)
            act.activation(w_up[:, :, :].rearrange("p k n -> p (k n)"), ps[:, 6, :], ACT.Copy).then_inc(fused_ready, 1)
            act.wait_ge(weights_loaded, 16 * WEIGHT_LOADS)

            def relu_z(g, s, first=False):
                u = 2 * g + s
                act.wait_ge(z_done, u + 1)
                if not first:
                    act.wait_ge(m_done, u - 1)
                for k in range(2):
                    last = act.activation(zT[:, s, k, :], ps[:, 2 * s + k, :], ACT.Relu, bias=b1[:, k:k + 1])
                last.then_inc(zT_ready, 1)

            def copy_m(g, s, first=False, cols=1024):
                u = 2 * g + s
                act.wait_ge(m_done, u + 1)
                if not first:
                    act.wait_ge(m_added, u - 1)
                act.activation(m_raw[:, s, 0:cols],
                               ps[:, 4 + 2 * s:6 + 2 * s, :].rearrange("p a b -> p (a b)")[:, 0:cols],
                               ACT.Copy).then_inc(m_copied, 1)

            relu_z(0, 0, True)
            relu_z(0, 1, True)
            copy_m(0, 0, True)
            relu_z(1, 0)
            copy_m(0, 1, True)
            with act.Fori(1, GROUPS - 1) as g:
                relu_z(g, 1)
                copy_m(g, 0)
                relu_z(g + 1, 0)
                copy_m(g, 1)
            copy_m(GROUPS - 1, 0, cols=2 * HID)

            def copy_counts(i, s, first=False):
                t = 2 * i + s
                act.wait_ge(tiles_used, TILES * (t + 1))
                if not first:
                    act.wait_ge(counts_stored[s], 16 * i)
                    act.wait_ge(counts_maxed, t - 1)
                act.activation(cnt[:, s, :], ps[:, 4 + s, 0:CNT], ACT.Copy).then_inc(counts_copied, 1)

            def copy_pairs(a, b):
                with act.Fori(a, b) as i:
                    copy_counts(i, 0)
                    copy_counts(i, 1)

            def relu_z_of(u):
                act.wait_ge(u_done, u + 1)
                for k in range(2):
                    last = act.activation(unit_zq[:, k, :], ps[:, 6 + k, :], ACT.Relu, bias=b1[:, k:k + 1])
                last.then_inc(uT_ready, 1)

            def relu_q_of(u, n=CHUNK):
                act.wait_ge(q_done, u + 1)
                for k in range(2):
                    last = act.activation(unit_zq[:, k, 0:n], ps[:, 6 + k, 0:n], ACT.Relu, bias=up_bias[:, k:k + 1])
                last.then_inc(qT_ready, 1)

            def tanh_of(u):
                act.wait_ge(o_added, u + 1)
                act.activation(unit_t[:, :, :], unit_o[:, :, :], ACT.Tanh).then_inc(o_tanh, 1)

            def deviation_of(u):
                act.wait_ge(var2_ready, u + 1)
                act.activation(unit_dev[:, :], unit_stat[:, :], ACT.Sqrt, bias=eps_col[:, 0:1], scale=1.0 / F)\
                   .then_inc(std2_ready, 1)

            def store_h(u, blocks=4):
                act.wait_ge(h2_ready, u + 1)
                act.dma_start(h_table[ds(u * CHUNK, blocks * P), :].rearrange("(b p) f -> p b f", p=P),
                              unit_h[:, 0:blocks, :]).then_inc(h2_stored, 16)

            with act.If(flag_of(act, 0) < 1):
                act.wait_ge(agg_clear, 1)
                n = QROWS - SUPERS * REPEATS
                act.dma_start(count_table[SUPERS * REPEATS:QROWS, :], agg[0:n, 0, 0:NODES_PAD // 2].bitcast(bf16))\
                   .then_inc(pad_rows_stored, 16)
                copy_counts(0, 0, True)
                copy_counts(0, 1, True)
                copy_pairs(1, UNIT_PAIRS + 6)
                relu_z_of(0)
                copy_pairs(UNIT_PAIRS + 6, 2 * UNIT_PAIRS)
                relu_q_of(0)
                with act.Fori(2, UNITS) as w:
                    copy_pairs(w * UNIT_PAIRS, w * UNIT_PAIRS + 3)
                    tanh_of(w - 2)
                    copy_pairs(w * UNIT_PAIRS + 3, w * UNIT_PAIRS + 4)
                    deviation_of(w - 2)
                    copy_pairs(w * UNIT_PAIRS + 4, w * UNIT_PAIRS + 6)
                    store_h(w - 2)
                    relu_z_of(w - 1)
                    copy_pairs(w * UNIT_PAIRS + 6, w * UNIT_PAIRS + 8)
                    relu_q_of(w - 1)
                copy_counts(PAIRS - 1, 0)
                copy_counts(PAIRS - 1, 1)
                copy_counts(PAIRS, 0)
                tanh_of(UNITS - 2)
                deviation_of(UNITS - 2)
                relu_z_of(UNITS - 1)
                store_h(UNITS - 2)
                relu_q_of(UNITS - 1, 2 * P)
                tanh_of(UNITS - 1)
                deviation_of(UNITS - 1)
                store_h(UNITS - 1, 2)
                for c in range(CHUNKS):
                    n = min(CHUNK, NODES_PAD - c * CHUNK)
                    act.wait_ge(chunk_done, c + 1)
                    act.activation(partsT[:, c * CHUNK:c * CHUNK + n], ps[0:3 * F, c % 4, 0:n], ACT.Copy)\
                       .then_inc(chunk_copied, 1)
            with act.If(flag_of(act, 0) > 0):
                general_act(act, 0)
                with act.Fori(0, BLOCKS) as b:
                    act.wait_ge(b_turned, b + 1)
                    act.activation(agg[:, :, ds(b * P, P)], ps[:, 5, 0:2 * P].rearrange("p (k n) -> p k n", k=2),
                                   ACT.Copy).then_inc(b_copied, 1)

                def network_of(u, blocks=4):
                    relu_z_of(u)
                    relu_q_of(u, blocks * P)
                    tanh_of(u)
                    deviation_of(u)
                    store_h(u, blocks)

                with act.Fori(0, UNITS - 1) as u:
                    network_of(u)
                network_of(UNITS - 1, 2)
            act.wait_ge(h2_stored, 16 * UNITS)
            with act.If(flag_of(act, 1) > 0):
                general_act(act, 1)

        @block.vector
        def _(dve):
            chain = [0]

            def link(ins):
                chain[0] += 1
                ins.then_inc(dve_step, 1)
                dve.wait_ge(dve_step, chain[0])

            dve.memset(base_i[:, :], 0).then_inc(base_clear, 1)
            link(dve.memset(eps_col[:, :], EPS))
            link(dve.memset(bad[:, :], 0.0))
            dve.memset(cnt_max[:, :], 0.0)
            dve.wait_ge(x_loaded, 16)
            NB_PAD = GROUPS * 8

            def layernorm(values, centred, squares, total, deviation, n, ready, answer):
                link(dve.tensor_reduce(total[:, 0:n], values, AX.X, ALU.add))
                link(dve.tensor_scalar(total[:, 0:n], total[:, 0:n], 1.0 / F, None, ALU.mult))
                link(dve.tensor_tensor(centred, values, total[:, 0:n].unsqueeze(2).to_broadcast([P, n, F]), ALU.subtract))
                link(dve.tensor_tensor(squares, centred, centred, ALU.mult))
                dve.tensor_reduce(total[:, 0:n], squares, AX.X, ALU.add).then_inc(ready, 1)
                dve.wait_ge(answer, 1)
                link(dve.reciprocal(deviation[:, 0:n], deviation[:, 0:n]))
                link(dve.tensor_tensor(centred, centred, deviation[:, 0:n].unsqueeze(2).to_broadcast([P, n, F]), ALU.mult))

            layernorm(x_sb[:, :, :], h0, ta[:, 0:NB_PAD * F].rearrange("p (b f) -> p b f", f=F), stat_a, stat_b,
                      NB_PAD, var_ready, std_ready)
            dve.tensor_scalar(h0, h0, 0.0, None, ALU.max).then_inc(h_ready, 1)
            dve.wait_ge(weights_loaded, 16 * WEIGHT_LOADS)
            dve.tensor_copy(b2_wide[:, :, :], b2[:, :].unsqueeze(2).to_broadcast([P, 2, P])).then_inc(b2_ready, 1)
            dve.wait_ge(base_loaded, 16 * 5)
            link(dve.tensor_scalar(six_i[:, 0, :], base_i[:, :], 6, None, ALU.logical_shift_right))
            link(dve.tensor_copy(six_f[:, :], six_i[:, 0, :]))
            dve.tensor_scalar(six_i[:, 1, :], six_f[:, :], 1.0, None, ALU.add).then_inc(near_asked, 1)
            dve.tensor_copy(bounds[:, :, 0], base_i[:, :])
            dve.wait_ge(consts, 2)
            link(dve.tensor_copy(iota1[:, :], iota_i[:, :]))
            link(dve.tensor_scalar(iota0[:, :], iota1[:, 0:P], -1.0, None, ALU.add))
            dve.wait_ge(fused_done, 1)
            dve.tensor_tensor(msg_bias[:, :], ps[:, 7, 0:HID], conv_b_wide[:, :], ALU.add).then_inc(fused_ready, 1)
            dve.tensor_tensor(up_bias[:, :], ps[:, 7, HID:HID + 2], pb1[:, :], ALU.add).then_inc(fused_ready, 1)
            dve.wait_ge(near_loaded, 16 * 12)
            link(dve.tensor_copy(rho[:, :], rho_i[:, :]))
            link(dve.tensor_copy(near_f, near_i[:, :, :, :].rearrange("p g s n -> p g (s n)")))
            link(dve.tensor_scalar(six_f[:, :], six_f[:, :], 64.0, None, ALU.mult))
            for k in range(REPEATS):
                link(dve.tensor_scalar(rows_f[:, :, k], rho[:, :], float(k), None, ALU.add))
                link(dve.tensor_tensor(near_c, near_f, rows_f[:, :, k:k + 1].to_broadcast([P, 4, P]), ALU.is_le))
                link(dve.tensor_reduce(bounds[:, :, k + 1], near_c, AX.X, ALU.add))
                link(dve.tensor_tensor(bounds[:, :, k + 1], bounds[:, :, k + 1], six_f[:, :], ALU.add))
            dve.tensor_copy(rows_i[:, :, :], rows_f[:, :, :]).then_inc(rows_ready, 1)
            dve.tensor_copy(bounds_wide[:, :, :, :], bounds[:, :, :].unsqueeze(3).to_broadcast([P, 4, 4, P]))\
               .then_inc(bounds_ready, 1)
            dve.wait_ge(bounds_spread, 1)
            link(dve.tensor_copy(bound_all[:, :, :], ps[:, 0:4, :]))
            dve.nop().then_inc(bounds_taken, 1)

            def of_super(v):
                return bound_all[:, v, 0:SUPERS].unsqueeze(2).to_broadcast([P, SUPERS, TILES])

            def edges(a):
                return a.rearrange("p (t k) -> p t k", k=TILES)

            dve.wait_ge(edges_loaded, 16 * 4)
            link(dve.tensor_copy(dstf, dst_i))
            link(dve.tensor_tensor(edges(ta), edges(dstf), of_super(0), ALU.subtract))
            link(dve.tensor_scalar(tb, ta, 0.0, None, ALU.is_ge))
            link(dve.scalar_tensor_tensor(out=tb, in0=ta, scalar=float(WINDOW), in1=tb, op0=ALU.is_lt, op1=ALU.mult))
            link(dve.scalar_tensor_tensor(out=adj[:, :], in0=ta, scalar=1.0, in1=tb, op0=ALU.add, op1=ALU.mult))
            link(dve.tensor_tensor(edges(ta), edges(dstf), of_super(1), ALU.is_ge))
            link(dve.tensor_tensor(edges(tc), edges(dstf), of_super(2), ALU.is_ge))
            link(dve.tensor_tensor(ta, ta, tc, ALU.add))
            link(dve.tensor_tensor(edges(tc), edges(dstf), of_super(3), ALU.is_lt))
            link(dve.tensor_tensor(tb, tb, tc, ALU.mult))
            link(dve.tensor_scalar(t_i, src_i[:, :], 7, None, ALU.logical_shift_right))
            link(dve.tensor_copy(tc, t_i))
            link(dve.scalar_tensor_tensor(out=tc, in0=ta, scalar=float(BLOCKS), in1=tc, op0=ALU.mult, op1=ALU.add))
            link(dve.scalar_tensor_tensor(out=key[:, :], in0=tc, scalar=1.0, in1=tb, op0=ALU.add, op1=ALU.mult))
            link(dve.tensor_scalar(t_i, src_i[:, :], 127, None, ALU.bitwise_and))
            link(dve.tensor_copy(slo[:, :], t_i))
            link(dve.scalar_tensor_tensor(out=tc, in0=dstf, scalar=float(NOWHERE), in1=tb, op0=ALU.is_lt, op1=ALU.is_gt))
            link(dve.tensor_reduce(bad[:, 0:1], tc, AX.X, ALU.add))
            link(dve.tensor_copy(ord_f[:, :], ord_i[:, 0, :]))
            link(dve.tensor_copy(ta[:, 0:SORT_COLS], ord_i[:, 1, :]))
            link(dve.tensor_tensor(tc[:, 0:SORT_COLS], ord_f[:, :], ta[:, 0:SORT_COLS], ALU.is_gt))
            link(dve.tensor_reduce(bad[:, 1:2], tc[:, 0:SORT_COLS], AX.X, ALU.add))
            link(dve.tensor_copy(base_f[:, :], base_row[:, :]))
            link(dve.tensor_tensor(tc[0:1, 0:SUPERS - 1], base_f[:, 0:SUPERS - 1], base_f[:, 1:SUPERS], ALU.is_gt))
            link(dve.tensor_reduce(bad[0:1, 2:3], tc[0:1, 0:SUPERS - 1], AX.X, ALU.add))
            first = 4 * UNIT_PAIRS - SLACK
            late = base_f[:, first:first + 2 * UNIT_PAIRS * (UNITS - 2) + 1:2 * UNIT_PAIRS]
            link(dve.scalar_tensor_tensor(out=tc[0:1, 0:UNITS - 1], in0=iota1[0:1, 0:UNITS - 1], scalar=float(CHUNK),
                                          in1=late, op0=ALU.mult, op1=ALU.is_gt))
            link(dve.tensor_reduce(bad[0:1, 3:4], tc[0:1, 0:UNITS - 1], AX.X, ALU.add))
            link(dve.tensor_reduce(bad[:, 5:6], bad[:, 0:5], AX.X, ALU.add))
            dve.nop().then_inc(bad_ready, 1)
            dve.wait_ge(hT_done, 2)
            link(dve.memset(agg[:, 0, :], 0.0))
            link(dve.memset(agg[:, 1, :], 0.0))
            dve.nop().then_inc(agg_clear, 1)
            dve.wait_ge(bad_summed, 1)
            dve.tensor_scalar(flag[:, 0:1], ps[0:1, 6, 0:1], 0.0, None, ALU.is_gt).then_inc(flag_ready, 1)

            def stage(t, s):
                dve.tensor_copy(idx[:, s, :], src_i[:, ds(t * TILES, TILES)]).then_inc(idx_staged, 1)

            def build(t, s):
                at = ds(t * TILES, TILES)
                dve.tensor_tensor(oh_dst[:, s, :, :], iota1[:, 0:WINDOW].unsqueeze(1).to_broadcast([P, TILES, WINDOW]),
                                  adj[:, at].unsqueeze(2).to_broadcast([P, TILES, WINDOW]), ALU.is_equal)
                dve.tensor_tensor(oh_lo[:, s, :, :], iota0[:, :].unsqueeze(1).to_broadcast([P, TILES, P]),
                                  slo[:, at].unsqueeze(2).to_broadcast([P, TILES, P]), ALU.is_equal)
                dve.tensor_tensor(oh_key[:, s, :, :], iota1[:, :].unsqueeze(1).to_broadcast([P, TILES, CNT]),
                                  key[:, at].unsqueeze(2).to_broadcast([P, TILES, CNT]), ALU.is_equal)\
                   .then_inc(onehots_built, 1)

            def add(t, s):
                dve.wait_ge(tiles_used, TILES * (t + 1))
                if not isinstance(t, int) or t > 0:
                    dve.wait_ge(agg_added, t)
                base = dve.value_load(base_row[0:1, ds(t, 1)], min_val=0, max_val=NODES_PAD)
                dve.tensor_tensor(agg[:, :, ds(base, WINDOW)], ps[:, 2 * s:2 * s + 2, 0:WINDOW],
                                  agg[:, :, ds(base, WINDOW)], ALU.add).then_inc(agg_added, 1)

            def largest(t, s):
                dve.wait_ge(counts_copied, t + 1)
                if not isinstance(t, int) or t > 0:
                    dve.wait_ge(counts_maxed, t)
                dve.tensor_tensor(cnt_max[:, :], cnt_max[:, :], cnt[:, s, :], ALU.max).then_inc(counts_maxed, 1)

            def step(t, s):
                build(t + 1, 1 - s)
                add(t, s)
                stage(t + 2, s)
                largest(t - 1, 1 - s)

            def pairs(a, b):
                with dve.Fori(a, b) as i:
                    step(2 * i, 0)
                    step(2 * i + 1, 1)

            UNIT_STEPS = 7

            def unit_link(ins, u, n):
                ins.then_inc(unit_step, 1)
                dve.wait_ge(unit_step, UNIT_STEPS * u + n)

            def out_of(u, blocks=4):
                dve.wait_ge(o_done, u + 1)
                dve.tensor_tensor(unit_o[:, 0:blocks, :], ps[:, 6, 0:blocks * F].rearrange("p (b f) -> p b f", f=F),
                                  pb2[:, :].unsqueeze(1).to_broadcast([P, blocks, F]), ALU.add).then_inc(o_added, 1)

            def variance_of(u, blocks=4):
                dve.wait_ge(o_tanh, u + 1)
                here = x_sb[:, ds(u * 4, 4), :]
                unit_link(dve.tensor_tensor(unit_x[:, :, :], here, unit_t[:, :, :], ALU.add), u, 1)
                dve.tensor_scalar(here, unit_x[:, :, :], 0.0, None, ALU.add)
                unit_link(dve.tensor_reduce(unit_stat[:, :], unit_x[:, :, :], AX.X, ALU.add), u, 2)
                unit_link(dve.tensor_scalar(unit_stat[:, :], unit_stat[:, :], 1.0 / F, None, ALU.mult), u, 3)
                unit_link(dve.tensor_tensor(unit_x[:, :, :], unit_x[:, :, :],
                                            unit_stat[:, :].unsqueeze(2).to_broadcast([P, 4, F]), ALU.subtract), u, 4)
                unit_link(dve.tensor_tensor(unit_t[:, :, :], unit_x[:, :, :], unit_x[:, :, :], ALU.mult), u, 5)
                dve.tensor_reduce(unit_stat[:, :], unit_t[:, :, :], AX.X, ALU.add).then_inc(var2_ready, 1)

            def norm_of(u, first=False):
                dve.wait_ge(std2_ready, u + 1)
                unit_link(dve.reciprocal(unit_dev[:, :], unit_dev[:, :]), u, 6)
                unit_link(dve.tensor_tensor(unit_x[:, :, :], unit_x[:, :, :],
                                            unit_dev[:, :].unsqueeze(2).to_broadcast([P, 4, F]), ALU.mult), u, 7)
                if not first:
                    dve.wait_ge(h2_stored, 16 * u)
                dve.tensor_scalar(unit_h[:, :, :], unit_x[:, :, :], 0.0, None, ALU.max).then_inc(h2_ready, 1)

            x1 = x_sb[:, 0:BLOCKS, :]
            dve.memset(unit_o[:, :, :], 0.0)
            dve.wait_ge(m_stored[0], 16 * GROUPS)
            dve.wait_ge(m_stored[1], 16 * (GROUPS - 1))
            with dve.If(flag_of(dve, 0) < 1):
                stage(0, 0)
                stage(1, 1)
                build(0, 0)
                build(1, 1)
                dve.wait_ge(pad_rows_stored, 16)
                add(0, 0)
                stage(2, 0)
                build(2, 0)
                add(1, 1)
                stage(3, 1)
                largest(0, 0)
                pairs(1, 2 * UNIT_PAIRS)

                def unit_between(w, first=False):
                    pairs(w * UNIT_PAIRS, w * UNIT_PAIRS + 3)
                    out_of(w - 2)
                    pairs(w * UNIT_PAIRS + 3, w * UNIT_PAIRS + 4)
                    variance_of(w - 2)
                    pairs(w * UNIT_PAIRS + 4, w * UNIT_PAIRS + 5)
                    norm_of(w - 2, first)
                    pairs(w * UNIT_PAIRS + 5, w * UNIT_PAIRS + 8)

                unit_between(2, True)
                with dve.Fori(3, UNITS) as w:
                    unit_between(w)
                LAST = SUPERS - 1
                build(LAST - 1, 1)
                add(LAST - 2, 0)
                stage(LAST, 0)
                largest(LAST - 3, 1)
                build(LAST, 0)
                add(LAST - 1, 1)
                largest(LAST - 2, 0)
                add(LAST, 0)
                largest(LAST - 1, 1)
                largest(LAST, 0)
                for u in (UNITS - 2, UNITS - 1):
                    out_of(u, 4 if u < UNITS - 1 else 2)
                    variance_of(u)
                    norm_of(u)
                dve.wait_ge(g_gathered, 16 * QTILES)
                link(dve.tensor_copy(g_parts[:, :, 0:F], g_rows[:, :, :]))
                link(dve.tensor_tensor(g_rest[:, 0], g_rows[:, :, :], g_parts[:, :, 0:F], ALU.subtract))
                link(dve.tensor_copy(g_parts[:, :, F:2 * F], g_rest[:, 0]))
                link(dve.tensor_tensor(g_rest[:, 1], g_rest[:, 0], g_parts[:, :, F:2 * F], ALU.subtract))
                dve.tensor_copy(g_parts[:, :, 2 * F:3 * F], g_rest[:, 1]).then_inc(g_split, 1)
                dve.wait_ge(sum_done, 1)
                dve.tensor_tensor(hb, x1,
                                  ps[:, 4:8, :].rearrange("p a b -> p (a b)")[:, 0:BLOCKS * F]
                                  .rearrange("p (b f) -> p b f", f=F), ALU.add).then_inc(out_summed, 1)
                dve.wait_ge(out_summed, 1)
                dve.wait_ge(counts_maxed, SUPERS)
            with dve.If(flag_of(dve, 0) > 0):
                general_dve(dve, 0)

                def network_of(u, blocks=4, first=False):
                    out_of(u, blocks)
                    variance_of(u)
                    norm_of(u, first)

                network_of(0, first=True)
                with dve.Fori(1, UNITS - 1) as u:
                    network_of(u)
                network_of(UNITS - 1, 2)
            dve.tensor_reduce(bad[:, 4:5], cnt_max[:, :], AX.X, ALU.max).then_inc(late_step, 1)
            dve.wait_ge(late_step, 1)
            dve.tensor_scalar(bad[:, 4:5], bad[:, 4:5], COUNT_MAX, None, ALU.is_ge).then_inc(late_step, 1)
            dve.wait_ge(late_step, 2)
            dve.tensor_reduce(bad[:, 5:6], bad[:, 0:5], AX.X, ALU.add).then_inc(bad_ready, 1)
            dve.wait_ge(bad_summed, 2)
            dve.tensor_scalar(flag[:, 1:2], ps[0:1, 0, 0:1], 0.0, None, ALU.is_gt).then_inc(flag_ready, 1)
            with dve.If(flag_of(dve, 1) > 0):
                general_dve(dve, 1)
                dve.wait_ge(general_loaded, 16)
                dve.tensor_tensor(hb, x1, o_sb, ALU.add).then_inc(general_summed, 1)
                dve.wait_ge(general_summed, 1)
            dve.nop().then_inc(out_ready, 1)

        @block.tensor
        def _(pe):
            pe.wait_ge(consts, 1)
            pe.wait_ge(weights_loaded, 16 * WEIGHT_LOADS)
            for jt in range(2):
                for it in range(2):
                    last = pe.transpose(ps[:, 4, jt * HID + it * P:jt * HID + it * P + P],
                                        w2[:, it, jt * P:jt * P + P], ident[:, :])
            last.then_inc(w2T_done, 1)
            pe.wait_ge(h_ready, 1)
            for u in range(UNITS):
                if u == 16:
                    pe.wait_ge(hT_ready, 1)
                last = pe.transpose(ps[0:4 * F, u % 16 // 4, (u % 4) * P:(u % 4 + 1) * P],
                                    h0[:, 4 * u:4 * u + 4, :].rearrange("p b f -> p (b f)"), ident[:, :])
                if u in (15, UNITS - 1):
                    last.then_inc(hT_done, 1)
            pe.wait_ge(w2T_ready, 1)
            pe.wait_ge(b2_ready, 1)
            for bank, right in ((5, conv), (6, post_h)):
                for it in range(2):
                    for jt in range(2):
                        pe.matmul(ps[:, bank, it * HID:(it + 1) * HID], w2T[:, jt, it * P:(it + 1) * P],
                                  right[:, jt, :], start=(jt == 0), stop=(jt == 1))
            for jt in range(2):
                pe.matmul(ps[:, 7, 0:HID], b2_wide[:, jt, :], conv[:, jt, :], start=(jt == 0), stop=(jt == 1))
            for m in range(2):
                for jt in range(2):
                    last = pe.matmul(ps[:, 7, HID + m:HID + m + 1], post_h[:, jt, m * P:(m + 1) * P],
                                     b2[:, jt:jt + 1], start=(jt == 0), stop=(jt == 1))
            last.then_inc(fused_done, 1)
            pe.wait_ge(hT_ready, 2)
            pe.wait_ge(bounds_ready, 1)
            for v in range(4):
                for g in range(4):
                    last = pe.matmul(ps[:, v, g * P:(g + 1) * P], bounds_wide[:, g, v, :], ident[:, :],
                                     start=True, stop=True)
            last.then_inc(bounds_spread, 1)
            pe.wait_ge(bounds_taken, 1)
            pe.wait_ge(fused_ready, 4)

            def hidden(g, s, done):
                for k in range(2):
                    for b in range(4):
                        last = pe.matmul(ps[:, 2 * s + k, b * P:(b + 1) * P], w1_unit[:, b, k * P:(k + 1) * P],
                                         hT[:, ds(2 * g + s, 1), :].rearrange("p a n -> p (a n)"), start=True, stop=True)
                last.then_inc(done, 1)

            def z(g, s, first=False):
                if not first:
                    pe.wait_ge(zT_ready, 2 * g + s - 1)
                hidden(g, s, z_done)

            def messages(g, s, first=False, blocks=4):
                u = 2 * g + s
                pe.wait_ge(zT_ready, u + 1)
                if not first:
                    pe.wait_ge(m_copied, u - 1)
                for b in range(blocks):
                    for k in range(2):
                        last = pe.matmul(ps[:, 4 + 2 * s + b // 2, (b % 2) * HID:(b % 2 + 1) * HID],
                                         zT[:, s, k, b * P:(b + 1) * P], w_msg[:, k, :], start=(k == 0), stop=(k == 1))
                last.then_inc(m_done, 1)

            z(0, 0, True)
            z(0, 1, True)
            messages(0, 0, True)
            z(1, 0)
            messages(0, 1, True)
            with pe.Fori(1, GROUPS - 1) as g:
                z(g, 1)
                messages(g, 0)
                z(g + 1, 0)
                messages(g, 1)
            messages(GROUPS - 1, 0, blocks=2)
            pe.wait_ge(m_copied, UNITS)

            def add_up(i, s, first=False):
                t = 2 * i + s
                pe.wait_ge(onehots_built, t + 1)
                if not first:
                    pe.wait_ge(agg_added, t - 1)
                    pe.wait_ge(counts_copied, t - 1)
                for k in range(TILES):
                    pe.wait_ge(gathered[s * TILES + k], 16 * (i + 1))
                    for half in range(2):
                        pe.matmul(ps[:, 2 * s + half, 0:WINDOW], gat[:, s * TILES + k, half * P:(half + 1) * P],
                                  oh_dst[:, s, k, :], start=(k == 0), stop=(k == TILES - 1))
                    pe.matmul(ps[:, 4 + s, 0:CNT], oh_lo[:, s, k, :], oh_key[:, s, k, :],
                              start=(k == 0), stop=(k == TILES - 1)).then_inc(tiles_used, 1)

            def add_pairs(a, b):
                with pe.Fori(a, b) as i:
                    add_up(i, 0)
                    add_up(i, 1)

            def z_of(u, first=False):
                if not first:
                    pe.wait_ge(o_added, u)
                for k in range(2):
                    for b in range(4):
                        last = pe.matmul(ps[:, 6 + k, b * P:(b + 1) * P], w1_unit[:, b, k * P:(k + 1) * P],
                                         hT[:, ds(u, 1), :].rearrange("p a n -> p (a n)"), start=True, stop=True)
                last.then_inc(u_done, 1)

            def up_of(u, n=CHUNK, added=None):
                pe.wait_ge(uT_ready, u + 1)
                if added is not None:
                    pe.wait_ge(agg_added, added)
                for m in range(2):
                    for k in range(2):
                        pe.matmul(ps[:, 6 + m, 0:n], w_up[:, k, m * P:(m + 1) * P], unit_zq[:, k, 0:n],
                                  start=(k == 0), stop=False)
                    for k in range(2):
                        last = pe.matmul(ps[:, 6 + m, 0:n], post_agg[:, k, m * P:(m + 1) * P],
                                         agg[:, k, ds(u * CHUNK, n)], start=False, stop=(k == 1))
                last.then_inc(q_done, 1)

            def down_of(u, blocks=4):
                pe.wait_ge(qT_ready, u + 1)
                for b in range(blocks):
                    for k in range(2):
                        last = pe.matmul(ps[:, 6, b * F:(b + 1) * F], unit_zq[:, k, b * P:(b + 1) * P], post2[:, k, :],
                                         start=(k == 0), stop=(k == 1))
                last.then_inc(o_done, 1)

            pe.wait_ge(bad_ready, 1)
            pe.matmul(ps[:, 6, 0:1], ones[:, :], bad[:, 5:6], start=True, stop=True).then_inc(bad_summed, 1)
            with pe.If(flag_of(pe, 0) < 1):
                add_up(0, 0, True)
                add_up(0, 1, True)
                add_pairs(1, UNIT_PAIRS + 6)
                z_of(0, True)
                add_pairs(UNIT_PAIRS + 6, 2 * UNIT_PAIRS)
                up_of(0, added=4 * UNIT_PAIRS - SLACK)
                with pe.Fori(2, UNITS) as w:
                    add_pairs(w * UNIT_PAIRS, w * UNIT_PAIRS + 2)
                    down_of(w - 2)
                    add_pairs(w * UNIT_PAIRS + 2, w * UNIT_PAIRS + 6)
                    z_of(w - 1)
                    add_pairs(w * UNIT_PAIRS + 6, w * UNIT_PAIRS + 8)
                    up_of(w - 1, added=2 * UNIT_PAIRS * (w + 1) - SLACK)
                add_up(PAIRS - 1, 0)
                down_of(UNITS - 2)
                add_up(PAIRS - 1, 1)
                add_up(PAIRS, 0)
                z_of(UNITS - 1)
                up_of(UNITS - 1, 2 * P, added=SUPERS)
                down_of(UNITS - 1, 2)
                pe.wait_ge(o_added, UNITS)
                pe.wait_ge(counts_copied, SUPERS)

                pe.wait_ge(g_split, 1)
                for c in range(CHUNKS):
                    n = min(CHUNK, NODES_PAD - c * CHUNK)
                    pe.wait_ge(c_loaded[c % NB4], 16 * (c // NB4 + 1))
                    if c >= 4:
                        pe.wait_ge(chunk_copied, c - 3)
                    for q in range(QTILES):
                        last = pe.matmul(ps[0:3 * F, c % 4, 0:n], g_parts[:, q, :], ctiles[:, c % NB4, q, 0:n],
                                         start=(q == 0), stop=(q == QTILES - 1))
                    last.then_inc(chunk_done, 1)
                pe.wait_ge(chunk_copied, CHUNKS)
                by_block = partsT.rearrange("r (l h) -> r l h", h=BLOCKS)
                for b in range(BLOCKS):
                    last = pe.matmul(ps[:, 4 + b // 32, (b % 32) * F:(b % 32 + 1) * F], by_block[:, :, b], part_sel[:, :],
                                     start=True, stop=True)
                last.then_inc(sum_done, 1)
            with pe.If(flag_of(pe, 0) > 0):
                general_pe(pe, 0)

                def turn(b, first=False):
                    pe.wait_ge(b_loaded, 16 * (b + 1))
                    if not first:
                        pe.wait_ge(b_copied, b)
                    for k in range(2):
                        last = pe.transpose(ps[:, 5, k * P:(k + 1) * P], e_back[:, k * P:(k + 1) * P], ident[:, :])
                    last.then_inc(b_turned, 1)

                turn(0, True)
                with pe.Fori(1, BLOCKS) as b:
                    turn(b)
                pe.wait_ge(b_copied, BLOCKS)

                def network_of(u, blocks=4, first=False):
                    z_of(u, first)
                    up_of(u, blocks * P)
                    down_of(u, blocks)

                network_of(0, first=True)
                with pe.Fori(1, UNITS - 1) as u:
                    network_of(u)
                network_of(UNITS - 1, 2)
            pe.wait_ge(bad_ready, 2)
            pe.matmul(ps[:, 0, 0:1], ones[:, :], bad[:, 5:6], start=True, stop=True).then_inc(bad_summed, 1)
            with pe.If(flag_of(pe, 1) > 0):
                general_pe(pe, 1)


def kernel(**inputs):
    import numpy as np
    import concourse.bacc as bacc
    from concourse.bass_utils import run_bass_kernel_spmd

    a = {k: np.ascontiguousarray(v) for k, v in inputs.items()}
    x_pad = np.zeros((GROUPS * 8 * P, F), a["x"].dtype)
    x_pad[:N_NODES] = a["x"]
    src_pad = np.zeros(EDGES_PAD, a["src"].dtype)
    src_pad[:N_EDGES] = a["src"]
    dst_pad = np.full(EDGES_PAD, NOWHERE, a["dst"].dtype)
    dst_pad[:N_EDGES] = a["dst"]

    def by_partition(e):
        return np.ascontiguousarray(e.reshape(SUPERS, P, TILES).transpose(1, 0, 2).reshape(P, SUPERS * TILES))

    arrays = {
        "x": np.ascontiguousarray(x_pad.reshape(GROUPS * 8, P, F).transpose(1, 0, 2).reshape(P, GROUPS * 8 * F)),
        "src": by_partition(src_pad), "dst": by_partition(dst_pad), "dst_flat": dst_pad,
    }
    for name in ("pre_w1", "pre_b1", "pre_w2", "pre_b2", "conv_w", "conv_b", "post_w1", "post_b1", "post_w2", "post_b2"):
        arrays[name] = a["L0_gnn_" + name]
    nc = bacc.Bacc("TRN2", target_bir_lowering=False, num_devices=1)
    maps, args = {}, []
    for name, v in arrays.items():
        maps[f"in_{name}"] = v
        args.append(nc.dram_tensor(f"in_{name}", v.shape, mybir.dt.from_np(v.dtype), kind="ExternalInput").ap())
    args.append(nc.dram_tensor("result", (P, BLOCKS * F), mybir.dt.float32, kind="ExternalOutput").ap())
    gnn_kernel(nc, *args)
    r = run_bass_kernel_spmd(nc, [maps], core_ids=[0])
    y = r.results[0]["result"].reshape(P, BLOCKS, F).transpose(1, 0, 2).reshape(NODES_PAD, F)
    return np.ascontiguousarray(y[:N_NODES])
```

```python
import concourse.bass as bass
from concourse import mybir
from contextlib import ExitStack

P = 128
N_NODES = 12500
F = 16
HID = 256
N_EDGES = 412500
BLOCKS = -(-N_NODES // P)
GROUPS = -(-BLOCKS // 8)
UNITS = -(-BLOCKS // 4)
NODES_PAD = BLOCKS * P
TILES = 8
SUPER = TILES * P
SUPERS = -(-N_EDGES // SUPER)
EDGES_PAD = SUPERS * SUPER
WINDOW = 64
REPEATS = 3
NOWHERE = 16383
CNT = REPEATS * BLOCKS
BATCHES = 7
BATCH = BLOCKS // BATCHES
SORT_COLS = 100
CHUNK = 512
PAIRS = SUPERS // 2
UNIT_PAIRS = PAIRS // UNITS
LAG = 3
ROUNDS = UNITS - LAG
ROUND = 17 * REPEATS
TAIL = SUPERS * REPEATS - ROUNDS * ROUND
assert all(ROUND * (q + 1) <= 2 * UNIT_PAIRS * REPEATS * (q + LAG) for q in range(ROUNDS)) and TAIL <= P
EARLY_TAIL = 2 * UNIT_PAIRS * UNITS * REPEATS - ROUNDS * ROUND
EARLY_UNITS = UNITS - 3
EARLY_TILES = TILES // 2
EARLY_SUPER = 11
EARLY = EARLY_UNITS * EARLY_TILES
COPIED = 14
SLACK = 2
COUNT_MAX = 256.0
EPS = 1e-5
FUSE_LOADS = 5
WEIGHT_LOADS = 9
HALVES = ((0, 16), (16, UNITS))


def gnn_kernel(nc, x, src, dst, dst_flat, pre_w1, pre_b1, pre_w2, pre_b2, conv_w, conv_b,
               post_w1, post_b1, post_w2, post_b2, out):
    f32, bf16, i32 = mybir.dt.float32, mybir.dt.bfloat16, mybir.dt.int32
    ALU = mybir.AluOpType
    ACT = mybir.ActivationFunctionType
    AX = mybir.AxisListType
    ds = bass.ds

    ctx = ExitStack()
    with ctx:
        ctx.enter_context(nc.allow_non_contiguous_dma(reason="a few hundred strided words"))

        def sb(name, shape, dt=f32):
            return ctx.enter_context(nc.sbuf_tensor(name, shape, dt))

        def sem(name):
            return ctx.enter_context(nc.semaphore(name))

        h0_table = nc.dram_tensor("h0_table", [GROUPS * 8 * P, F], f32).ap()
        early_table = nc.dram_tensor("early_table", [P, EARLY * F], f32).ap()
        msg_table = nc.dram_tensor("msg_table", [NODES_PAD, HID], f32).ap()
        count_table = nc.dram_tensor("count_table", [SUPERS * REPEATS, NODES_PAD], bf16).ap()
        sum_table = nc.dram_tensor("sum_table", [NODES_PAD, F], f32).ap()
        bound_list = nc.dram_tensor("bound_list", [P * 16], f32).ap()
        row_list = nc.dram_tensor("row_list", [4 * P * REPEATS, 1], i32).ap()
        general_agg = nc.dram_tensor("general_agg", [NODES_PAD + P, HID], f32).ap()
        general_out = nc.dram_tensor("general_out", [NODES_PAD + P, F], f32).ap()
        h_table = nc.dram_tensor("h_table", [NODES_PAD, F], f32).ap()

        x_sb = sb("x_sb", [P, GROUPS * 8, F])
        hT = sb("hT", [4 * F, UNITS, P])
        w1_unit = sb("w1_unit", [4 * F, 4, HID])
        post_agg = sb("post_agg", [P, 2, HID])
        post2 = sb("post2", [P, 2, F])
        w_msg = sb("w_msg", [P, 2, HID])
        w_up = sb("w_up", [P, 2, HID])
        b1 = sb("b1", [P, 2])
        b2 = sb("b2", [P, 2])
        msg_bias = sb("msg_bias", [P, HID])
        pb1 = sb("pb1", [P, 2])
        up_bias = sb("up_bias", [P, 2])
        pb2 = sb("pb2", [P, F])
        ident = sb("ident", [P, P])
        ones = sb("ones", [P, P])
        eps_col = sb("eps_col", [P, 1])
        unit_zq = sb("unit_zq", [P, 2, CHUNK])
        unit_o = sb("unit_o", [P, 4, F])
        unit_t = sb("unit_t", [P, 4, F])
        unit_x = sb("unit_x", [P, 4, F])
        unit_h = sb("unit_h", [P, 4, F])
        unit_stat = sb("unit_stat", [P, 4])
        unit_dev = sb("unit_dev", [P, 4])
        stat = sb("stat", [P, 2 * GROUPS * 8])
        stat_a, stat_b = stat[:, 0:GROUPS * 8], stat[:, GROUPS * 8:]
        early_rows = stat[:, 0:EARLY_TILES * F]
        early_T = stat[0:EARLY_TILES * F, EARLY_TILES * F:EARLY_TILES * F + P]

        agg = sb("agg", [P, 2, NODES_PAD + WINDOW])
        gat = sb("gat", [P, 2 * TILES, HID])
        adj = sb("adj", [P, SUPERS * TILES], mybir.dt.uint8)
        slo = sb("slo", [P, SUPERS * TILES], mybir.dt.uint8)
        key = sb("key", [P, SUPERS * TILES], mybir.dt.int16)
        w2, conv, post_h, w2T = (gat[:, 2 * i:2 * i + 2, :] for i in range(4))
        b2_wide = gat[:, 8, :].rearrange("p (k n) -> p k n", k=2)
        conv_b_wide = gat[:, 9, :]
        src_s = sb("src_s", [P, SUPERS * TILES], mybir.dt.int16)
        onehots = sb("onehots", [P, 2 * TILES * WINDOW + TILES * P + TILES * CNT])
        cnt = sb("cnt", [P, 2, CNT], bf16)
        cnt_max = sb("cnt_max", [P, CNT], bf16)
        idx = sb("idx", [P, 2, TILES], i32)
        iota1 = sb("iota1", [P, CNT])
        iota0 = sb("iota0", [P, P])
        base_row = sb("base_row", [1, SUPERS], i32)
        base_i = sb("base_i", [P, 4], i32)
        six_i = sb("six_i", [P, 2, 4], i32)
        rho_i = sb("rho_i", [P, 4], i32)
        rho = sb("rho", [P, 4])
        rows_f = sb("rows_f", [P, 4, REPEATS])
        rows_i = sb("rows_i", [P, 4, REPEATS], i32)
        six_f = sb("six_f", [P, 4])
        bounds = sb("bounds", [P, 4, 4])
        row_s = sb("row_s", [P, SUPERS * REPEATS], mybir.dt.int16)
        row_of_i = sb("row_of_i", [P, 4], i32)
        row_of = sb("row_of", [P, 4])
        h_first = sb("h_first", [P, 4, 3 * F], bf16)
        sums = sb("sums", [WINDOW, HID])
        oh_row = sb("oh_row", [P, 4, max(ROUND, TAIL)], bf16)
        g_round = sb("g_round", [max(ROUND, TAIL), 3 * F], bf16)
        c_batch = sb("c_batch", [ROUND, BATCH, P], bf16)
        acc = sb("acc", [P, BLOCKS, F])
        bad = sb("bad", [P, 7])
        flag = sb("flag", [1, 2], i32)

        W = SUPERS * TILES
        over = agg[:, :, :].rearrange("p a n -> p (a n)")
        dst_i = over[:, 0:W].bitcast(i32)
        t_i = over[:, W:2 * W].bitcast(i32)
        src_i = over[:, 2 * W:3 * W].bitcast(i32)
        dstf = over[:, 3 * W:4 * W]
        ta = over[:, 4 * W:5 * W]
        tb = over[:, 5 * W:6 * W]
        tc = t_i.bitcast(f32)
        row_i = over[:, 6 * W:6 * W + SUPERS * REPEATS].bitcast(i32)
        h0 = over[:, 6 * W:6 * W + GROUPS * 8 * F].rearrange("p (b f) -> p b f", f=F)
        n0 = 6 * W + GROUPS * 8 * F
        bound_all = over[:, n0:n0 + 2048]
        n0 += 2048
        near_i = over[:, n0:n0 + 512].bitcast(i32).rearrange("p (g s n) -> p g s n", g=4, s=2)
        near_f = over[:, n0 + 512:n0 + 1024].rearrange("p (g n) -> p g n", g=4)
        near_c = over[:, n0 + 1024:n0 + 1536].rearrange("p (g n) -> p g n", g=4)
        n0 += 1536
        iota_i = over[:, n0:n0 + CNT].bitcast(i32)
        ord_i = over[:, n0 + CNT:n0 + CNT + 2 * SORT_COLS].bitcast(i32).rearrange("p (s n) -> p s n", s=2)
        ord_f = over[:, n0 + CNT + 2 * SORT_COLS:n0 + CNT + 3 * SORT_COLS]
        c_tail = agg[0:TAIL, 0, 0:NODES_PAD // 2].bitcast(bf16).rearrange("r (j n) -> r j n", n=P)
        base_f = over[0:1, 5 * W:5 * W + SUPERS]
        zT = gat[:, 0:8, :].rearrange("p a b -> p (a b)").rearrange("p (u k n) -> p u k n", u=2, k=2)
        m_raw = gat[:, 8:16, :].rearrange("p a b -> p (a b)").rearrange("p (u n) -> p u n", u=2)
        n0, n1 = 2 * TILES * WINDOW, 2 * TILES * WINDOW + TILES * P
        oh_dst = onehots[:, 0:n0].rearrange("p (s k n) -> p s k n", s=2, k=TILES)
        oh_lo = onehots[:, n0:n1].bitcast(bf16).rearrange("p (s k n) -> p s k n", s=2, k=TILES)
        oh_key = onehots[:, n1:n1 + TILES * CNT].bitcast(bf16).rearrange("p (s k n) -> p s k n", s=2, k=TILES)
        m_sum = onehots[:, 0:2048].rearrange("p (s n) -> p s n", s=2)
        m_out = onehots[:, 2048:4096].rearrange("p (s n) -> p s n", s=2)
        o_sb = m_sum[:, :, :].rearrange("p a b -> p (a b)")[:, 0:BLOCKS * F].rearrange("p (b f) -> p b f", f=F)
        hb = m_out[:, :, :].rearrange("p a b -> p (a b)")[:, 0:BLOCKS * F].rearrange("p (b f) -> p b f", f=F)
        dst_again = dst_i
        zeros = over[:, W:W + (BLOCKS + 1) * HID // 4]
        e_rows, e_summed, e_back = gat[:, 0, :], gat[:, 1, :], gat[:, 4, :]
        e_wide, e_same = gat[:, 2, 0:P], gat[:, 2, P:2 * P]
        e_lower, e_tmp = gat[:, 3, 0:P], gat[:, 3, P:2 * P]
        e_key, e_pad, e_dup, e_spare, e_count, e_gap, e_to = (gat[:, 5, i:i + 1] for i in range(7))
        e_from_i, e_to_i, e_spare_i, e_look_i = (gat[:, 6, i:i + 1].bitcast(i32) for i in range(4))

        ps = ctx.enter_context(nc.psum_tensor("ps", [P, 8, 512], f32))

        def product(b):
            return ps[:, 2 + b % 2, 0:BATCH * F]

        x_loaded = [sem(f"x_loaded{i}") for i in range(2)]
        edges_loaded = sem("edges_loaded")
        base_loaded = sem("base_loaded")
        fuse_loaded = sem("fuse_loaded")
        weights_loaded = sem("weights_loaded")
        consts = sem("consts")
        w1_zero = sem("w1_zero")
        dve_step = sem("dve_step")
        pool_step = sem("pool_step")
        var_ready = sem("var_ready")
        std_ready = sem("std_ready")
        h_ready = sem("h_ready")
        hT_done = sem("hT_done")
        hT_ready = sem("hT_ready")
        w2T_done = sem("w2T_done")
        w2T_ready = sem("w2T_ready")
        fused_done = sem("fused_done")
        fused_ready = sem("fused_ready")
        bias_ready = sem("bias_ready")
        b2_ready = sem("b2_ready")
        near_asked = sem("near_asked")
        near_loaded = sem("near_loaded")
        bounds_ready = sem("bounds_ready")
        bounds_stored = sem("bounds_stored")
        bounds_loaded = sem("bounds_loaded")
        rows_ready = sem("rows_ready")
        rows_stored = sem("rows_stored")
        rows_loaded = sem("rows_loaded")
        z_done = sem("z_done")
        zT_ready = sem("zT_ready")
        m_done = sem("m_done")
        h0_stored = sem("h0_stored")
        early_gathered = sem("early_gathered")
        early_stored = sem("early_stored")
        early_loaded = sem("early_loaded")
        early_turned = sem("early_turned")
        early_copied = sem("early_copied")
        early_z_done = sem("early_z_done")
        early_z_ready = sem("early_z_ready")
        early_m_done = sem("early_m_done")
        early_summed = sem("early_summed")
        early_ready = sem("early_ready")
        m_copied = sem("m_copied")
        m_ready = sem("m_ready")
        m_added = sem("m_added")
        m_stored = [sem(f"m_stored{i}") for i in range(2)]
        idx_staged = sem("idx_staged")
        gathered = [sem(f"gathered{i}") for i in range(2 * TILES)]
        onehots_built = sem("onehots_built")
        tiles_used = sem("tiles_used")
        sums_copied = sem("sums_copied")
        sums_turned = sem("sums_turned")
        agg_added = sem("agg_added")
        counts_copied = sem("counts_copied")
        counts_maxed = sem("counts_maxed")
        counts_stored = [sem(f"counts_stored{i}") for i in range(2)]
        cleared = sem("cleared")
        bad_ready = sem("bad_ready")
        bad_summed = sem("bad_summed")
        flag_ready = sem("flag_ready")
        unit_step = sem("unit_step")
        u_done = sem("u_done")
        uT_ready = sem("uT_ready")
        q_done = sem("q_done")
        qT_ready = sem("qT_ready")
        o_done = sem("o_done")
        o_added = sem("o_added")
        o_tanh = sem("o_tanh")
        var2_ready = sem("var2_ready")
        std2_ready = sem("std2_ready")
        h2_ready = sem("h2_ready")
        h2_stored = sem("h2_stored")
        rows_built = sem("rows_built")
        g_done = sem("g_done")
        g_taken = sem("g_taken")
        c_loaded = sem("c_loaded")
        batch_done = sem("batch_done")
        acc_added = sem("acc_added")
        tail_loaded = sem("tail_loaded")
        sums_stored = sem("sums_stored")
        sums_loaded = sem("sums_loaded")
        out_ready = sem("out_ready")
        out_stored = sem("out_stored")
        base_clear = sem("base_clear")

        e_ready = [sem(f"e_ready{i}") for i in range(2)]
        e_zeroed = [sem(f"e_zeroed{i}") for i in range(2)]
        e_dst_loaded = [sem(f"e_dst_loaded{i}") for i in range(2)]
        e_consts = [sem(f"e_consts{i}") for i in range(2)]
        e_step = [sem(f"e_step{i}") for i in range(2)]
        e_asked = [sem(f"e_asked{i}") for i in range(2)]
        e_looked = sem("e_looked")
        e_gathered = [sem(f"e_gathered{i}") for i in range(2)]
        e_widened = [sem(f"e_widened{i}") for i in range(2)]
        e_turned = [sem(f"e_turned{i}") for i in range(2)]
        e_compared = [sem(f"e_compared{i}") for i in range(2)]
        e_placed = [sem(f"e_placed{i}") for i in range(2)]
        e_multiplied = [sem(f"e_multiplied{i}") for i in range(2)]
        e_copied = [sem(f"e_copied{i}") for i in range(2)]
        e_scattered = [sem(f"e_scattered{i}") for i in range(2)]
        b_loaded = sem("b_loaded")
        b_turned = sem("b_turned")
        b_copied = sem("b_copied")
        out_summed = sem("out_summed")
        general_summed = sem("general_summed")
        late_step = sem("late_step")
        general_loaded = sem("general_loaded")

        def half_blocks(half):
            first, last = HALVES[half]
            return 4 * first, 4 * last if last < UNITS else GROUPS * 8

        block = ctx.enter_context(nc.Block())

        EDGE_TILES = SUPERS * TILES
        width = (HID, F)

        def flag_of(eng, which):
            eng.wait_ge(flag_ready, which + 1)
            return eng.value_load(flag[0:1, which:which + 1], min_val=0, max_val=1)

        def general_sp(sp, part):
            sp.wait_ge(e_ready[part], 1)
            sp.dma_start(dst_again, dst).then_inc(e_dst_loaded[part], 16)
            target = (general_agg, general_out)[part].rearrange("(p b) n -> p (b n)", p=P)
            step = min(target.shape[1], zeros.shape[1])
            for c in range(0, target.shape[1], step):
                sp.dma_start(target[:, c:c + step], zeros[:, 0:step]).then_inc(e_zeroed[part], 16)

        def general_pool(pool, part):
            pool.wait_ge(e_ready[part], 1)
            pool.iota(e_spare_i, [[0, 1]], base=NODES_PAD, channel_multiplier=1).then_inc(e_consts[part], 1)
            pool.affine_select(out=e_lower, in_=ones[:, :], compare_op=ALU.is_gt, fill=0.0, base=0,
                               pattern=[[-1, P]], channel_multiplier=1).then_inc(e_consts[part], 1)
            pool.wait_ge(e_zeroed[part], 16 * (4, 1)[part])
            asked = pool.alloc_register(f"asked{part}")
            looked = pool.alloc_register(f"looked{part}")
            placed = pool.alloc_register(f"placed{part}")
            pool.reg_mov(asked, 1)
            pool.reg_mov(looked, 16)
            pool.reg_mov(placed, 1)
            with pool.Fori(0, EDGE_TILES):
                pool.wait_ge(e_asked[part], asked)
                pool.reg_add(asked, asked, 1)
                if part == 1:
                    pool.indirect_dma_start(e_look_i, None, dst_flat[:].rearrange("(r n) -> r n", n=1),
                                            bass.IndirectOffsetOnAxis(ap=e_from_i, axis=0)).then_inc(e_looked, 16)
                    pool.wait_ge(e_looked, looked)
                    pool.reg_add(looked, looked, 16)
                pool.indirect_dma_start(e_rows[:, 0:width[part]], None, (msg_table, h_table)[part],
                                        bass.IndirectOffsetOnAxis(ap=(e_from_i, e_look_i)[part], axis=0))\
                    .then_inc(e_gathered[part], 16)
                pool.wait_ge(e_copied[part], placed)
                pool.wait_ge(e_placed[part], placed)
                pool.reg_add(placed, placed, 1)
                pool.indirect_dma_start((general_agg, general_out)[part], bass.IndirectOffsetOnAxis(ap=e_to_i, axis=0),
                                        e_summed[:, 0:width[part]], None, compute_op=ALU.add)\
                    .then_inc(e_scattered[part], 16)

        def general_act(act, part):
            with act.Fori(0, EDGE_TILES) as t:
                act.wait_ge(e_multiplied[part], t + 1)
                act.activation(e_summed[:, 0:width[part]], ps[:, 6, 0:width[part]], ACT.Copy).then_inc(e_copied[part], 1)

        def general_pe(pe, part):
            with pe.Fori(0, EDGE_TILES) as t:
                pe.wait_ge(e_widened[part], t + 1)
                pe.matmul(ps[:, 5, 0:P], e_wide, ident[:, :], start=True, stop=True).then_inc(e_turned[part], 1)
                pe.wait_ge(e_compared[part], t + 1)
                pe.wait_ge(e_gathered[part], 16 * (t + 1))
                pe.matmul(ps[:, 6, 0:width[part]], e_same, e_rows[:, 0:width[part]], start=True, stop=True)\
                    .then_inc(e_multiplied[part], 1)

        def general_dve(dve, part):
            dve.memset(zeros, 0.0).then_inc(e_ready[part], 1)
            dve.wait_ge(e_consts[part], 2)
            dve.tensor_copy(e_spare, e_spare_i)
            dve.wait_ge(e_dst_loaded[part], 16)
            steps = 9 if part else 7

            def tile(t, first=False):
                done = [0]

                def link(ins):
                    done[0] += 1
                    ins.then_inc(e_step[part], 1)
                    dve.wait_ge(e_step[part], steps * t + done[0])

                if not first:
                    dve.wait_ge(e_scattered[part], 16 * t)
                dve.tensor_scalar(e_from_i, (src_s[:, :], dst_again)[part][:, ds(t, 1)], 0.0, None, ALU.add).then_inc(e_asked[part], 1)
                link(dve.tensor_scalar(e_pad, dst_again[:, ds(t, 1)], float(NOWHERE), None, ALU.is_ge))
                if part == 0:
                    link(dve.tensor_scalar(e_key, dst_again[:, ds(t, 1)], 0.0, None, ALU.add))
                else:
                    link(dve.tensor_scalar(e_gap, e_pad, float(NOWHERE), None, ALU.mult))
                    link(dve.tensor_scalar(e_key, src_s[:, ds(t, 1)], 0.0, None, ALU.add))
                    link(dve.tensor_tensor(e_key, e_key, e_gap, ALU.add))
                dve.tensor_copy(e_wide, e_key.to_broadcast([P, P])).then_inc(e_widened[part], 1)
                dve.wait_ge(e_turned[part], t + 1)
                dve.tensor_scalar(e_same, ps[:, 5, 0:P], e_key, None, ALU.is_equal).then_inc(e_compared[part], 1)
                dve.wait_ge(e_compared[part], t + 1)
                link(dve.tensor_tensor(e_tmp, e_same, e_lower, ALU.mult))
                link(dve.tensor_reduce(e_count, e_tmp, AX.X, ALU.add))
                link(dve.scalar_tensor_tensor(out=e_dup, in0=e_count, scalar=0.0, in1=e_pad, op0=ALU.is_gt, op1=ALU.max))
                link(dve.tensor_tensor(e_gap, e_spare, e_key, ALU.subtract))
                link(dve.scalar_tensor_tensor(out=e_to, in0=e_gap, scalar=e_dup, in1=e_key, op0=ALU.mult, op1=ALU.add))
                assert done[0] == steps
                dve.tensor_copy(e_to_i, e_to).then_inc(e_placed[part], 1)

            tile(0, True)
            with dve.Fori(1, EDGE_TILES) as t:
                tile(t)
            dve.wait_ge(e_scattered[part], 16 * EDGE_TILES)

        @block.sync
        def _(sp):
            def load_x(half):
                first, last = half_blocks(half)
                sp.dma_start(x_sb[:, first:last, :].rearrange("p b f -> p (b f)"), x[:, first * F:last * F])\
                  .then_inc(x_loaded[half], 16)

            def load_square(tile, dram, loaded):
                sp.dma_start(tile[:, :, :], dram.rearrange("(k p) n -> p k n", p=P)).then_inc(loaded, 16)

            load_x(0)
            load_square(w2, pre_w2, fuse_loaded)
            load_x(1)
            load_square(conv, conv_w, fuse_loaded)
            load_square(post_h, post_w1[0:HID, :], fuse_loaded)
            sp.dma_start(b2[:, :], pre_b2.rearrange("(k p) -> p k", p=P)).then_inc(fuse_loaded, 16)
            sp.dma_start(conv_b_wide[:, :], conv_b.partition_broadcast(P)).then_inc(fuse_loaded, 16)
            sp.wait_ge(w1_zero, 1)
            for b in range(4):
                sp.dma_start(w1_unit[F * b:F * b + F, b, :], pre_w1).then_inc(weights_loaded, 16)
            for tile, dram in ((b1, pre_b1), (pb1, post_b1)):
                sp.dma_start(tile[:, :], dram.rearrange("(k p) -> p k", p=P)).then_inc(weights_loaded, 16)
            sp.dma_start(pb2[:, :], post_b2.partition_broadcast(P)).then_inc(weights_loaded, 16)
            load_square(post_agg, post_w1[HID:2 * HID, :], weights_loaded)
            load_square(post2, post_w2, weights_loaded)
            sp.dma_start(dst_i, dst).then_inc(edges_loaded, 16)
            sp.dma_start(src_i, src).then_inc(edges_loaded, 16)
            for s in range(2):
                sp.dma_start(ord_i[:, s, :], dst_flat[s:s + P * SORT_COLS].rearrange("(p n) -> p n", n=SORT_COLS))\
                  .then_inc(edges_loaded, 16)
            for half in range(2):
                first, last = half_blocks(half)
                sp.wait_ge(h_ready, half + 1)
                sp.dma_start(h0_table[first * P:last * P, :].rearrange("(b p) f -> p b f", p=P), h0[:, first:last, :])\
                  .then_inc(h0_stored, 16)
            sp.wait_ge(rows_ready, 1)
            sp.wait_ge(bounds_ready, 1)
            sp.dma_start(bound_list.rearrange("(p n) -> p n", p=P), bounds[:, :, :].rearrange("p g v -> p (g v)"))\
              .then_inc(bounds_stored, 16)
            sp.dma_start(row_list.rearrange("(p n) one -> p (n one)", p=P), rows_i[:, :, :].rearrange("p g r -> p (g r)"))\
              .then_inc(rows_stored, 16)
            sp.wait_ge(bounds_stored, 16)
            sp.dma_start(bound_all, bound_list.partition_broadcast(P)).then_inc(bounds_loaded, 16)
            sp.wait_ge(rows_stored, 16)
            sp.wait_ge(hT_done, 2)
            sp.wait_ge(h0_stored, 32)
            sp.dma_start(row_i, row_list[0:SUPERS * REPEATS, :].rearrange("n one -> (n one)").partition_broadcast(P))\
              .then_inc(rows_loaded, 16)

            def store_messages(g, s, blocks=4):
                sp.wait_ge(m_ready, 2 * g + s + 1)
                rows = msg_table[ds((8 * g + 4 * s) * P, blocks * P), :].rearrange("(b p) n -> p b n", p=P)
                sp.dma_start(rows, m_out[:, s, 0:blocks * HID].rearrange("p (b n) -> p b n", n=HID))\
                  .then_inc(m_stored[s], 16)

            with sp.Fori(0, GROUPS - 1) as g:
                store_messages(g, 0)
                store_messages(g, 1)
            store_messages(GROUPS - 1, 0, 2)
            sp.wait_ge(early_gathered, 16 * EARLY)
            sp.dma_start(early_table, acc[:, 0:EARLY, :].rearrange("p t f -> p (t f)")).then_inc(early_stored, 16)

            def store_counts(i, s):
                t = 2 * i + s
                sp.wait_ge(counts_copied, t + 1)
                rows = count_table[ds(t * REPEATS, REPEATS), :].rearrange("r (l h) -> l r h", h=BLOCKS)
                sp.dma_start(rows, cnt[:, s, :].rearrange("p (r h) -> p r h", r=REPEATS)).then_inc(counts_stored[s], 16)

            def store_pairs(a, b):
                with sp.Fori(a, b) as i:
                    store_counts(i, 0)
                    store_counts(i, 1)

            def load_batch(q, b):
                if b or not isinstance(q, int):
                    sp.wait_ge(batch_done, BATCHES * q + b)
                sp.dma_start(c_batch[:, :, :].rearrange("r j n -> r (j n)"),
                             count_table[ds(q * ROUND, ROUND), b * BATCH * P:(b + 1) * BATCH * P]).then_inc(c_loaded, 16)

            def load_round(w):
                at = w * UNIT_PAIRS
                for b in range(BATCHES):
                    if b == 0:
                        sp.wait_ge(counts_stored[0], 16 * at)
                        sp.wait_ge(counts_stored[1], 16 * at)
                    load_batch(w - LAG, b)
                    store_pairs(at + b, at + b + 1)
                store_pairs(at + 7, at + 8)

            with sp.If(flag_of(sp, 0) < 1):
                store_pairs(0, LAG * UNIT_PAIRS)
                load_round(LAG)
                with sp.Fori(LAG + 1, UNITS) as w:
                    load_round(w)
                for s in range(2):
                    sp.wait_ge(counts_stored[s], 16 * (PAIRS - 1))
                tail = c_tail.rearrange("r j n -> r (j n)")

                def load_tail(rows, cols):
                    sp.dma_start(tail[rows, cols], count_table[ROUNDS * ROUND:SUPERS * REPEATS, :][rows, cols])\
                      .then_inc(tail_loaded, 16)

                load_tail(slice(0, EARLY_TAIL), slice(0, NODES_PAD // 2))
                store_counts(PAIRS - 1, 0)
                load_tail(slice(0, EARLY_TAIL), slice(NODES_PAD // 2, NODES_PAD))
                store_counts(PAIRS - 1, 1)
                store_counts(PAIRS, 0)
                sp.wait_ge(counts_stored[0], 16 * (PAIRS + 1))
                sp.wait_ge(counts_stored[1], 16 * PAIRS)
                load_tail(slice(EARLY_TAIL, TAIL), slice(0, NODES_PAD))
                for b in range(BATCHES):
                    sp.wait_ge(acc_added, BATCHES * ROUNDS + b + 1)
                    sp.dma_start(sum_table[b * BATCH * P:(b + 1) * BATCH * P, :].rearrange("(j p) f -> p j f", p=P),
                                 acc[:, b * BATCH:(b + 1) * BATCH, :]).then_inc(sums_stored, 16)
                sp.wait_ge(sums_stored, 16 * BATCHES)
                sp.dma_start(hb, sum_table.rearrange("(l h) f -> l h f", h=BLOCKS)).then_inc(sums_loaded, 16)

            with sp.If(flag_of(sp, 0) > 0):
                general_sp(sp, 0)
                sp.wait_ge(e_scattered[0], 16 * EDGE_TILES)

                def load_block(b, first=False):
                    if not first:
                        sp.wait_ge(b_turned, b)
                    sp.dma_start(e_back, general_agg[ds(b * P, P), :]).then_inc(b_loaded, 16)

                load_block(0, True)
                with sp.Fori(1, BLOCKS) as b:
                    load_block(b)

            with sp.If(flag_of(sp, 1) > 0):
                general_sp(sp, 1)
                sp.wait_ge(e_scattered[1], 16 * EDGE_TILES)
                sp.dma_start(o_sb, general_out[0:NODES_PAD, :].rearrange("(b p) f -> p b f", p=P))\
                  .then_inc(general_loaded, 16)
            sp.wait_ge(out_ready, 1)
            sp.dma_start(out, hb.rearrange("p b f -> p (b f)")).then_inc(out_stored, 16)
            sp.wait_ge(out_stored, 16)

        @block.gpsimd
        def _(pool):
            pool.memset(w1_unit[:, :, :], 0.0).then_inc(w1_zero, 1)
            pool.memset(ones[:, :], 1.0).then_inc(pool_step, 1)
            pool.wait_ge(pool_step, 1)
            pool.affine_select(out=ident[:, :], in_=ones[:, :], compare_op=ALU.is_equal, fill=0.0, base=0,
                               pattern=[[-1, P]], channel_multiplier=1).then_inc(consts, 1)
            pool.iota(iota_i, [[1, CNT]], base=1, channel_multiplier=0).then_inc(consts, 1)
            pool.iota(row_of_i[:, :], [[P, 4]], base=0, channel_multiplier=1).then_inc(consts, 1)
            pool.wait_ge(fuse_loaded, 16 * FUSE_LOADS)
            pool.tensor_tensor(b2_wide, ones[:, :].unsqueeze(1).to_broadcast([P, 2, P]),
                               b2[:, :].unsqueeze(2).to_broadcast([P, 2, P]), ALU.mult).then_inc(b2_ready, 1)
            pool.wait_ge(near_asked, 1)
            for g in range(4):
                for s in range(2):
                    pool.indirect_dma_start(near_i[:, g, s, :], None, dst_flat[:].rearrange("(r n) -> r n", n=64),
                                            bass.IndirectOffsetOnAxis(ap=six_i[:, s, g:g + 1], axis=0))\
                        .then_inc(near_loaded, 16)
                pool.indirect_dma_start(rho_i[:, g:g + 1], None, dst_flat[:].rearrange("(r n) -> r n", n=1),
                                        bass.IndirectOffsetOnAxis(ap=base_i[:, g:g + 1], axis=0))\
                    .then_inc(near_loaded, 16)

            def message_bias(u):
                s = u % 2
                pool.wait_ge(m_copied, u + 1)
                if u > 1:
                    pool.wait_ge(m_ready, u - 1)
                pool.tensor_tensor(m_sum[:, s, :].rearrange("p (b n) -> p b n", n=HID),
                                   m_raw[:, s, :].rearrange("p (b n) -> p b n", n=HID),
                                   msg_bias[:, :].unsqueeze(1).to_broadcast([P, 4, HID]),
                                   ALU.add).then_inc(m_added, 1)

            pool.wait_ge(bias_ready, 1)
            pool.wait_ge(edges_loaded, 16 * 4)
            pool.wait_ge(h0_stored, 32)

            def gather_early(first, last):
                for e in range(first, last):
                    t = (2 + e // EARLY_TILES) * 2 * UNIT_PAIRS + EARLY_SUPER
                    column = t * TILES + TILES - EARLY_TILES + e % EARLY_TILES
                    pool.indirect_dma_start(acc[:, e, :], None, h0_table,
                                            bass.IndirectOffsetOnAxis(ap=src_i[:, column:column + 1], axis=0))\
                        .then_inc(early_gathered, 16)

            for u in range(COPIED):
                message_bias(u)
                gather_early(11 * u // 4, 11 * (u + 1) // 4)
            gather_early(11 * COPIED // 4, EARLY)
            staged_wanted = pool.alloc_register("staged_wanted")
            pool.reg_mov(staged_wanted, 4 * UNIT_PAIRS + 1)
            pool.wait_ge(m_stored[0], 16 * GROUPS)
            pool.wait_ge(m_stored[1], 16 * (GROUPS - 1))

            def gather(i, s, tiles=TILES):
                t = 2 * i + s
                if isinstance(t, int):
                    pool.wait_ge(idx_staged, t + 1)
                else:
                    pool.wait_ge(idx_staged, staged_wanted)
                    pool.reg_add(staged_wanted, staged_wanted, 1)
                for k in range(tiles):
                    pool.indirect_dma_start(gat[:, s * TILES + k, :], None, msg_table,
                                            bass.IndirectOffsetOnAxis(ap=idx[:, s, k:k + 1], axis=0))\
                        .then_inc(gathered[s * TILES + k], 16)

            with pool.If(flag_of(pool, 0) < 1):
                gather(0, 0)
                gather(0, 1)
                for i in range(1, UNIT_PAIRS):
                    gather(i, 0)
                    gather(i, 1)

                def gather_unit(w, early):
                    for n in range(2 * UNIT_PAIRS):
                        gather(w * UNIT_PAIRS + n // 2, n % 2, TILES - EARLY_TILES * (early and n == EARLY_SUPER))

                gather_unit(1, False)
                with pool.Fori(2, UNITS - 1) as w:
                    gather_unit(w, True)
                gather_unit(UNITS - 1, False)
                gather(PAIRS - 1, 0)
                gather(PAIRS - 1, 1)
                gather(PAIRS, 0)
            with pool.If(flag_of(pool, 0) > 0):
                general_pool(pool, 0)
            with pool.If(flag_of(pool, 1) > 0):
                pool.wait_ge(h2_stored, 16 * UNITS)
                general_pool(pool, 1)

        @block.scalar
        def _(act):
            act.dma_start(base_row[:, :], dst_flat[:].rearrange("(t e) -> e t", e=SUPER)[0:1, :]).then_inc(base_loaded, 16)
            act.wait_ge(base_clear, 1)
            whole = SUPERS // 4
            by_super = dst_flat[:].rearrange("(t e) -> t e", e=SUPER)
            act.dma_start(base_i[0:whole, :], by_super[0:4 * whole, 0].rearrange("(p g) -> p g", g=4))\
               .then_inc(base_loaded, 16)
            act.dma_start(base_i[whole:whole + 1, 0:SUPERS - 4 * whole],
                          by_super[4 * whole:SUPERS, 0].rearrange("(p g) -> p g", p=1)).then_inc(base_loaded, 16)
            act.wait_ge(w2T_done, 1)
            act.activation(w2T[:, :, :].rearrange("p k n -> p (k n)"), ps[:, 4, :], ACT.Copy).then_inc(w2T_ready, 1)
            for half in range(2):
                first, last = half_blocks(half)
                act.wait_ge(var_ready, half + 1)
                act.activation(stat_b[:, first:last], stat_a[:, first:last], ACT.Sqrt, bias=eps_col[:, 0:1],
                               scale=1.0 / F).then_inc(std_ready, 1)
            act.wait_ge(fused_done, 1)
            act.activation(w_msg[:, :, :].rearrange("p k n -> p (k n)"), ps[:, 5, :], ACT.Copy).then_inc(fused_ready, 1)
            act.activation(w_up[:, :, :].rearrange("p k n -> p (k n)"), ps[:, 6, :], ACT.Copy).then_inc(fused_ready, 1)
            for half, (first, last) in enumerate(HALVES):
                act.wait_ge(hT_done, half + 1)
                act.activation(hT[:, first:last, :].rearrange("p g n -> p (g n)"),
                               ps[0:4 * F, 4 * half:4 * half + 4, :].rearrange("p a b -> p (a b)")[:, 0:(last - first) * P],
                               ACT.Copy).then_inc(hT_ready, 1)
            act.wait_ge(weights_loaded, 16 * WEIGHT_LOADS)

            def relu_z(g, s, first=False):
                u = 2 * g + s
                act.wait_ge(z_done, u + 1)
                if not first:
                    act.wait_ge(m_done, u - 1)
                for k in range(2):
                    last = act.activation(zT[:, s, k, :], ps[:, 2 * s + k, :], ACT.Relu, bias=b1[:, k:k + 1])
                last.then_inc(zT_ready, 1)

            def copy_m(g, s, first=False):
                u = 2 * g + s
                act.wait_ge(m_done, u + 1)
                if not first:
                    act.wait_ge(m_added, u - 1)
                act.activation(m_raw[:, s, :], ps[:, 4 + 2 * s:6 + 2 * s, :].rearrange("p a b -> p (a b)"),
                               ACT.Copy).then_inc(m_copied, 1)

            def relu_m(g, s, first=False, cols=1024):
                act.wait_ge(m_added, 2 * g + s + 1)
                if not first:
                    act.wait_ge(m_stored[s], 16 * g)
                act.activation(m_out[:, s, 0:cols], m_sum[:, s, 0:cols], ACT.Relu).then_inc(m_ready, 1)

            relu_z(0, 0, True)
            relu_z(0, 1, True)
            act.wait_ge(bias_ready, 2)
            copy_m(0, 0, True)
            relu_z(1, 0)
            copy_m(0, 1, True)
            relu_m(0, 0, True)
            relu_z(1, 1)
            copy_m(1, 0)
            relu_m(0, 1, True)
            relu_z(2, 0)
            copy_m(1, 1)
            relu_m(1, 0)
            with act.Fori(2, COPIED // 2) as g:
                relu_z(g, 1)
                copy_m(g, 0)
                relu_m(g - 1, 1)
                relu_z(g + 1, 0)
                copy_m(g, 1)
                relu_m(g, 0)
            with act.Fori(COPIED // 2, GROUPS - 1) as g:
                relu_z(g, 1)
                relu_m(g - 1, 1)
                relu_z(g + 1, 0)
                relu_m(g, 0)
            relu_m(GROUPS - 2, 1)
            relu_m(GROUPS - 1, 0, cols=2 * HID)

            def copy_counts(i, s, first=False):
                t = 2 * i + s
                act.wait_ge(tiles_used, TILES * (t + 1))
                if not isinstance(t, int) or t > 0:
                    act.wait_ge(sums_turned, t)
                act.activation(sums[:, :], ps[0:WINDOW, s, 0:HID], ACT.Copy).then_inc(sums_copied, 1)
                if not first:
                    act.wait_ge(counts_stored[s], 16 * i)
                    act.wait_ge(counts_maxed, t - 1)
                act.activation(cnt[:, s, :], ps[:, 4 + s, 0:CNT], ACT.Copy).then_inc(counts_copied, 1)

            def copy_pairs(a, b):
                with act.Fori(a, b) as i:
                    copy_counts(i, 0)
                    copy_counts(i, 1)

            def relu_z_of(u):
                act.wait_ge(u_done, u + 1)
                for k in range(2):
                    last = act.activation(unit_zq[:, k, :], ps[:, 6 + k, :], ACT.Relu, bias=b1[:, k:k + 1])
                last.then_inc(uT_ready, 1)

            def relu_q_of(u, n=CHUNK):
                act.wait_ge(q_done, u + 1)
                for k in range(2):
                    last = act.activation(unit_zq[:, k, 0:n], ps[:, 6 + k, 0:n], ACT.Relu, bias=up_bias[:, k:k + 1])
                last.then_inc(qT_ready, 1)

            def tanh_of(u):
                act.wait_ge(o_added, u + 1)
                act.activation(unit_t[:, :, :], unit_o[:, :, :], ACT.Tanh).then_inc(o_tanh, 1)

            def deviation_of(u):
                act.wait_ge(var2_ready, u + 1)
                act.activation(unit_dev[:, :], unit_stat[:, :], ACT.Sqrt, bias=eps_col[:, 0:1], scale=1.0 / F)\
                   .then_inc(std2_ready, 1)

            def store_h(u, blocks=4):
                act.wait_ge(h2_ready, u + 1)
                act.dma_start(h_table[ds(u * CHUNK, blocks * P), :].rearrange("(b p) f -> p b f", p=P),
                              unit_h[:, 0:blocks, :]).then_inc(h2_stored, 16)

            with act.If(flag_of(act, 0) < 1):
                copy_counts(0, 0, True)
                copy_counts(0, 1, True)
                copy_pairs(1, UNIT_PAIRS)

                def unit_between(w, before=True, early=False):
                    v = w - 2
                    for n in range(2 * UNIT_PAIRS):
                        copy_counts(w * UNIT_PAIRS + n // 2, n % 2)
                        if n == 0 and before:
                            relu_q_of(w - 2)
                        elif n == 1 and early:
                            if not isinstance(v, int) or v:
                                act.wait_ge(early_turned, v)
                            act.dma_start(early_rows, early_table[:, ds(v * EARLY_TILES * F, EARLY_TILES * F)])\
                               .then_inc(early_loaded, 16)
                        elif n == 5 and before:
                            if early:
                                act.wait_ge(early_turned, v + 1)
                                act.activation(early_T, ps[0:EARLY_TILES * F, 6, 0:P], ACT.Copy).then_inc(early_copied, 1)
                            tanh_of(w - 2)
                        elif n == 7 and before:
                            if early:
                                act.wait_ge(early_z_done, v + 1)
                                for k in range(2):
                                    last = act.activation(unit_zq[:, k, :], ps[:, 6 + k, :], ACT.Relu, bias=b1[:, k:k + 1])
                                last.then_inc(early_z_ready, 1)
                            deviation_of(w - 2)
                        elif n == 11:
                            relu_z_of(w - 1)
                        elif n == 12 and before:
                            store_h(w - 2)

                unit_between(1, False)
                act.wait_ge(early_stored, 16)
                unit_between(2, early=True)
                with act.Fori(3, UNITS - 1) as w:
                    unit_between(w, early=True)
                unit_between(UNITS - 1)
                copy_counts(PAIRS - 1, 0)
                relu_q_of(UNITS - 2)
                copy_counts(PAIRS - 1, 1)
                tanh_of(UNITS - 2)
                deviation_of(UNITS - 2)
                copy_counts(PAIRS, 0)
                relu_z_of(UNITS - 1)
                relu_q_of(UNITS - 1, 2 * P)
                store_h(UNITS - 2)
                tanh_of(UNITS - 1)
                deviation_of(UNITS - 1)
                store_h(UNITS - 1, 2)
            with act.If(flag_of(act, 0) > 0):
                general_act(act, 0)
                with act.Fori(0, BLOCKS) as b:
                    act.wait_ge(b_turned, b + 1)
                    act.activation(agg[:, :, ds(b * P, P)], ps[:, 5, 0:2 * P].rearrange("p (k n) -> p k n", k=2),
                                   ACT.Copy).then_inc(b_copied, 1)

                def network_of(u, blocks=4):
                    relu_z_of(u)
                    relu_q_of(u, blocks * P)
                    tanh_of(u)
                    deviation_of(u)
                    store_h(u, blocks)

                with act.Fori(0, UNITS - 1) as u:
                    network_of(u)
                network_of(UNITS - 1, 2)
            act.wait_ge(h2_stored, 16 * UNITS)
            with act.If(flag_of(act, 1) > 0):
                general_act(act, 1)

        @block.vector
        def _(dve):
            chain = [0]

            def link(ins):
                chain[0] += 1
                ins.then_inc(dve_step, 1)
                dve.wait_ge(dve_step, chain[0])

            dve.memset(base_i[:, :], 0).then_inc(base_clear, 1)
            link(dve.memset(eps_col[:, :], EPS))
            link(dve.memset(bad[:, :], 0.0))
            dve.memset(cnt_max[:, :], 0.0)
            dve.wait_ge(base_loaded, 16 * 3)
            link(dve.tensor_scalar(six_i[:, 0, :], base_i[:, :], 6, None, ALU.logical_shift_right))
            link(dve.tensor_copy(six_f[:, :], six_i[:, 0, :]))
            dve.tensor_scalar(six_i[:, 1, :], six_f[:, :], 1.0, None, ALU.add).then_inc(near_asked, 1)
            dve.tensor_copy(bounds[:, :, 0], base_i[:, :])
            squares = ta[:, 0:GROUPS * 8 * F].rearrange("p (b f) -> p b f", f=F)
            for half in range(2):
                first, last = half_blocks(half)
                here, total = slice(first, last), stat_a[:, first:last]
                dve.wait_ge(x_loaded[half], 16)
                link(dve.tensor_reduce(total, x_sb[:, here, :], AX.X, ALU.add))
                link(dve.tensor_scalar(total, total, 1.0 / F, None, ALU.mult))
                link(dve.tensor_tensor(h0[:, here, :], x_sb[:, here, :],
                                       total.unsqueeze(2).to_broadcast([P, last - first, F]), ALU.subtract))
                link(dve.tensor_tensor(squares[:, here, :], h0[:, here, :], h0[:, here, :], ALU.mult))
                dve.tensor_reduce(total, squares[:, here, :], AX.X, ALU.add).then_inc(var_ready, 1)
            for half in range(2):
                first, last = half_blocks(half)
                here, deviation = slice(first, last), stat_b[:, first:last]
                dve.wait_ge(std_ready, half + 1)
                link(dve.reciprocal(deviation, deviation))
                dve.scalar_tensor_tensor(out=h0[:, here, :], in0=h0[:, here, :], scalar=0.0,
                                         in1=deviation.unsqueeze(2).to_broadcast([P, last - first, F]),
                                         op0=ALU.max, op1=ALU.mult).then_inc(h_ready, 1)
            dve.wait_ge(fused_done, 1)
            dve.tensor_tensor(msg_bias[:, :], ps[:, 7, 0:HID], conv_b_wide[:, :], ALU.add).then_inc(bias_ready, 1)
            dve.wait_ge(weights_loaded, 16 * WEIGHT_LOADS)
            dve.tensor_tensor(up_bias[:, :], ps[:, 7, HID:HID + 2], pb1[:, :], ALU.add).then_inc(bias_ready, 1)
            dve.wait_ge(consts, 3)
            dve.tensor_copy(row_of[:, :], row_of_i[:, :])
            link(dve.tensor_copy(iota1[:, :], iota_i))
            link(dve.tensor_scalar(iota0[:, :], iota1[:, 0:P], -1.0, None, ALU.add))
            dve.wait_ge(near_loaded, 16 * 12)
            link(dve.tensor_copy(rho[:, :], rho_i[:, :]))
            link(dve.tensor_copy(near_f, near_i[:, :, :, :].rearrange("p g s n -> p g (s n)")))
            link(dve.tensor_scalar(six_f[:, :], six_f[:, :], 64.0, None, ALU.mult))
            for k in range(REPEATS):
                link(dve.tensor_scalar(rows_f[:, :, k], rho[:, :], float(k), None, ALU.add))
                link(dve.tensor_tensor(near_c, near_f, rows_f[:, :, k:k + 1].to_broadcast([P, 4, P]), ALU.is_le))
                link(dve.tensor_reduce(bounds[:, :, k + 1], near_c, AX.X, ALU.add))
                link(dve.tensor_tensor(bounds[:, :, k + 1], bounds[:, :, k + 1], six_f[:, :], ALU.add))
            dve.tensor_copy(rows_i[:, :, :], rows_f[:, :, :]).then_inc(rows_ready, 1)
            dve.nop().then_inc(bounds_ready, 1)

            def of_super(v):
                return bound_all.rearrange("p (t v) -> p t v", v=4)[:, 0:SUPERS, v].unsqueeze(2).to_broadcast([P, SUPERS, TILES])

            def edges(a):
                return a.rearrange("p (t k) -> p t k", k=TILES)

            dve.wait_ge(edges_loaded, 16 * 4)
            dve.wait_ge(bounds_loaded, 16)
            dve.tensor_copy(src_s[:, :], src_i)
            link(dve.tensor_copy(dstf, dst_i))
            link(dve.tensor_tensor(edges(ta), edges(dstf), of_super(0), ALU.subtract))
            link(dve.tensor_scalar(tb, ta, 0.0, None, ALU.is_ge))
            link(dve.scalar_tensor_tensor(out=tb, in0=ta, scalar=float(WINDOW), in1=tb, op0=ALU.is_lt, op1=ALU.mult))
            link(dve.scalar_tensor_tensor(out=adj[:, :], in0=ta, scalar=1.0, in1=tb, op0=ALU.add, op1=ALU.mult))
            link(dve.tensor_tensor(edges(ta), edges(dstf), of_super(1), ALU.is_ge))
            link(dve.tensor_tensor(edges(tc), edges(dstf), of_super(2), ALU.is_ge))
            link(dve.tensor_tensor(ta, ta, tc, ALU.add))
            link(dve.tensor_tensor(edges(tc), edges(dstf), of_super(3), ALU.is_lt))
            link(dve.tensor_tensor(tb, tb, tc, ALU.mult))
            link(dve.tensor_scalar(t_i, src_i, 7, None, ALU.logical_shift_right))
            link(dve.scalar_tensor_tensor(out=ta, in0=ta, scalar=float(BLOCKS), in1=t_i, op0=ALU.mult, op1=ALU.add))
            link(dve.scalar_tensor_tensor(out=key[:, :], in0=ta, scalar=1.0, in1=tb, op0=ALU.add, op1=ALU.mult))
            link(dve.tensor_scalar(t_i, src_i, 127, None, ALU.bitwise_and))
            link(dve.tensor_copy(slo[:, :], t_i))
            link(dve.scalar_tensor_tensor(out=tc, in0=dstf, scalar=float(NOWHERE), in1=tb, op0=ALU.is_lt, op1=ALU.is_gt))
            link(dve.tensor_reduce(bad[:, 0:1], tc, AX.X, ALU.add))
            link(dve.tensor_copy(ord_f, ord_i[:, 0, :]))
            link(dve.tensor_copy(ta[:, 0:SORT_COLS], ord_i[:, 1, :]))
            link(dve.tensor_tensor(tc[:, 0:SORT_COLS], ord_f, ta[:, 0:SORT_COLS], ALU.is_gt))
            link(dve.tensor_reduce(bad[:, 1:2], tc[:, 0:SORT_COLS], AX.X, ALU.add))
            link(dve.tensor_copy(base_f, base_row[:, :]))
            link(dve.tensor_tensor(tc[0:1, 0:SUPERS - 1], base_f[:, 0:SUPERS - 1], base_f[:, 1:SUPERS], ALU.is_gt))
            link(dve.tensor_reduce(bad[0:1, 2:3], tc[0:1, 0:SUPERS - 1], AX.X, ALU.add))
            first = 4 * UNIT_PAIRS - SLACK
            late = base_f[:, first:first + 2 * UNIT_PAIRS * (UNITS - 2) + 1:2 * UNIT_PAIRS]
            link(dve.scalar_tensor_tensor(out=tc[0:1, 0:UNITS - 1], in0=iota1[0:1, 0:UNITS - 1], scalar=float(CHUNK),
                                          in1=late, op0=ALU.mult, op1=ALU.is_gt))
            link(dve.tensor_reduce(bad[0:1, 3:4], tc[0:1, 0:UNITS - 1], AX.X, ALU.add))
            link(dve.tensor_scalar(six_f[:, :], rho[:, :], float(CHUNK - REPEATS), None, ALU.is_gt))
            link(dve.tensor_reduce(bad[:, 4:5], six_f[:, :], AX.X, ALU.add))
            link(dve.tensor_reduce(bad[:, 6:7], bad[:, 0:5], AX.X, ALU.add))
            dve.nop().then_inc(bad_ready, 1)
            dve.wait_ge(rows_loaded, 16)
            link(dve.tensor_copy(row_s[:, :], row_i))
            dve.wait_ge(hT_done, 2)
            to_clear = [agg[:, 0, 0:2 * W], agg[:, 0, 3 * W:], agg[:, 1, 0:2 * W], agg[:, 1, 2 * W:]]
            for u in range(COPIED, UNITS):
                s, blocks = u % 2, 4 if u < UNITS - 1 else 2
                dve.wait_ge(m_done, u + 1)
                dve.wait_ge(m_added, u)
                dve.wait_ge(m_ready, u - 1)
                dve.tensor_tensor(m_sum[:, s, 0:blocks * HID].rearrange("p (b n) -> p b n", n=HID),
                                  ps[:, 4 + 2 * s:6 + 2 * s, :].rearrange("p c (b n) -> p (c b) n", n=HID)[:, 0:blocks],
                                  msg_bias[:, :].unsqueeze(1).to_broadcast([P, blocks, HID]), ALU.add)\
                   .then_inc(m_copied, 1)
                dve.wait_ge(m_copied, u + 1)
                dve.nop().then_inc(m_added, 1)
                if to_clear:
                    dve.memset(to_clear.pop(0), 0.0).then_inc(cleared, 1)
            dve.wait_ge(bad_summed, 1)
            dve.tensor_scalar(flag[:, 0:1], ps[0:1, 6, 0:1], 0.0, None, ALU.is_gt).then_inc(flag_ready, 1)

            def stage(t, s):
                if not isinstance(t, int) or t > 1:
                    dve.wait_ge(tiles_used, TILES * (t - 1))
                dve.tensor_copy(idx[:, s, :], src_s[:, ds(t * TILES, TILES)]).then_inc(idx_staged, 1)

            def build(t, s):
                at = ds(t * TILES, TILES)
                dve.tensor_tensor(oh_dst[:, s, :, :], iota1[:, 0:WINDOW].unsqueeze(1).to_broadcast([P, TILES, WINDOW]),
                                  adj[:, at].unsqueeze(2).to_broadcast([P, TILES, WINDOW]), ALU.is_equal)
                dve.tensor_tensor(oh_lo[:, s, :, :], iota0[:, :].unsqueeze(1).to_broadcast([P, TILES, P]),
                                  slo[:, at].unsqueeze(2).to_broadcast([P, TILES, P]), ALU.is_equal)
                dve.tensor_tensor(oh_key[:, s, :, :], iota1[:, :].unsqueeze(1).to_broadcast([P, TILES, CNT]),
                                  key[:, at].unsqueeze(2).to_broadcast([P, TILES, CNT]), ALU.is_equal)\
                   .then_inc(onehots_built, 1)

            def add(t, s):
                dve.wait_ge(sums_turned, t + 1)
                if not isinstance(t, int) or t > 0:
                    dve.wait_ge(agg_added, t)
                base = dve.value_load(base_row[0:1, ds(t, 1)], min_val=0, max_val=NODES_PAD)
                dve.tensor_tensor(agg[:, :, ds(base, WINDOW)], ps[:, s, HID:HID + 2 * WINDOW].rearrange("p (a n) -> p a n", a=2),
                                  agg[:, :, ds(base, WINDOW)], ALU.add).then_inc(agg_added, 1)

            def largest(t, s):
                dve.wait_ge(counts_copied, t + 1)
                if not isinstance(t, int) or t > 0:
                    dve.wait_ge(counts_maxed, t)
                dve.tensor_tensor(cnt_max[:, :], cnt_max[:, :], cnt[:, s, :], ALU.max).then_inc(counts_maxed, 1)

            def step(t, s):
                build(t + 1, 1 - s)
                add(t - 1, 1 - s)
                stage(t + 2, s)
                largest(t - 1, 1 - s)

            def pairs(a, b):
                with dve.Fori(a, b) as i:
                    step(2 * i, 0)
                    step(2 * i + 1, 1)

            UNIT_STEPS = 7

            def unit_link(ins, u, n):
                ins.then_inc(unit_step, 1)
                dve.wait_ge(unit_step, UNIT_STEPS * u + n)

            def out_of(u, blocks=4):
                dve.wait_ge(o_done, u + 1)
                dve.tensor_tensor(unit_o[:, 0:blocks, :], ps[:, 6, 0:blocks * F].rearrange("p (b f) -> p b f", f=F),
                                  pb2[:, :].unsqueeze(1).to_broadcast([P, blocks, F]), ALU.add).then_inc(o_added, 1)

            def variance_of(u, blocks=4):
                dve.wait_ge(o_tanh, u + 1)
                here = x_sb[:, ds(u * 4, 4), :]
                unit_link(dve.tensor_tensor(unit_x[:, :, :], here, unit_t[:, :, :], ALU.add), u, 1)
                dve.tensor_scalar(here, unit_x[:, :, :], 0.0, None, ALU.add)
                unit_link(dve.tensor_reduce(unit_stat[:, :], unit_x[:, :, :], AX.X, ALU.add), u, 2)
                unit_link(dve.tensor_scalar(unit_stat[:, :], unit_stat[:, :], 1.0 / F, None, ALU.mult), u, 3)
                unit_link(dve.tensor_tensor(unit_x[:, :, :], unit_x[:, :, :],
                                            unit_stat[:, :].unsqueeze(2).to_broadcast([P, 4, F]), ALU.subtract), u, 4)
                unit_link(dve.tensor_tensor(unit_t[:, :, :], unit_x[:, :, :], unit_x[:, :, :], ALU.mult), u, 5)
                dve.tensor_reduce(unit_stat[:, :], unit_t[:, :, :], AX.X, ALU.add).then_inc(var2_ready, 1)

            def norm_of(u, first=False):
                dve.wait_ge(std2_ready, u + 1)
                unit_link(dve.reciprocal(unit_dev[:, :], unit_dev[:, :]), u, 6)
                unit_link(dve.tensor_tensor(unit_x[:, :, :], unit_x[:, :, :],
                                            unit_dev[:, :].unsqueeze(2).to_broadcast([P, 4, F]), ALU.mult), u, 7)
                if not first:
                    dve.wait_ge(h2_stored, 16 * u)
                dve.tensor_scalar(unit_h[:, :, :], unit_x[:, :, :], 0.0, None, ALU.max).then_inc(h2_ready, 1)

            x1 = x_sb[:, 0:BLOCKS, :]
            dve.memset(unit_o[:, :, :], 0.0)

            def prelude_over():
                dve.wait_ge(m_stored[0], 16 * GROUPS)
                dve.wait_ge(m_stored[1], 16 * (GROUPS - 1))
                dve.wait_ge(early_stored, 16)

            with dve.If(flag_of(dve, 0) < 1):
                stage(0, 0)
                stage(1, 1)
                prelude_over()
                build(0, 0)
                build(1, 1)
                dve.memset(agg[:, 0, 2 * W:3 * W], 0.0).then_inc(cleared, 1)
                dve.memset(acc[:, :, :], 0.0).then_inc(cleared, 1)
                dve.wait_ge(cleared, 6)
                stage(2, 0)
                build(2, 0)
                add(0, 0)
                stage(3, 1)
                largest(0, 0)
                pairs(1, 2 * UNIT_PAIRS)

                def split_first():
                    h_rest = (unit_t[:, :, :], unit_o[:, :, :])
                    for part in range(3):
                        here = h_first[:, :, part * F:(part + 1) * F]
                        rest = unit_h[:, :, :] if part == 0 else h_rest[part - 1]
                        link(dve.tensor_copy(here, rest))
                        if part < 2:
                            link(dve.tensor_tensor(h_rest[part], rest, here, ALU.subtract))

                def build_rows(q, rows=ROUND):
                    if not isinstance(q, int) or q:
                        dve.wait_ge(g_done, q)
                    for b in range(4):
                        last = dve.tensor_scalar(oh_row[:, b, 0:rows], row_s[:, ds(q * ROUND, rows)], row_of[:, b:b + 1],
                                                 None, ALU.is_equal)
                    last.then_inc(rows_built, 1)

                def take_rows(q, rows=ROUND):
                    dve.wait_ge(g_done, q + 1)
                    if not isinstance(q, int) or q:
                        dve.wait_ge(batch_done, BATCHES * q)
                    dve.tensor_copy(g_round[0:rows, :], ps[0:rows, 3, 0:3 * F]).then_inc(g_taken, 1)

                def add_batch(q, b):
                    dve.wait_ge(batch_done, BATCHES * q + b + 1)
                    if not isinstance(q, int) or q:
                        dve.wait_ge(acc_added, BATCHES * q + b)
                    here = acc[:, b * BATCH:(b + 1) * BATCH, :]
                    dve.tensor_tensor(here, here, product(b).rearrange("p (j f) -> p j f", f=F), ALU.add)\
                       .then_inc(acc_added, 1)

                def early_messages(v):
                    slots = gat[:, 2 * TILES - EARLY_TILES:2 * TILES, :]
                    dve.wait_ge(early_m_done, v + 1)
                    dve.tensor_tensor(slots, ps[:, 6:8, :].rearrange("p c (b n) -> p (c b) n", n=HID),
                                      msg_bias[:, :].unsqueeze(1).to_broadcast([P, EARLY_TILES, HID]), ALU.add)\
                       .then_inc(early_summed, 1)
                    dve.wait_ge(early_summed, v + 1)
                    dve.tensor_scalar(slots, slots, 0.0, None, ALU.max).then_inc(early_ready, 1)

                def unit_between(w, first=False, rounds=True, before=True, after=ROUND, early=False):
                    q = w - LAG
                    at = w * UNIT_PAIRS
                    pairs(at, at + 1)
                    if rounds:
                        if before:
                            add_batch(q - 1, BATCHES - 1)
                        take_rows(q)
                    for b in range(BATCHES):
                        if early and b + 1 == EARLY_SUPER // 2:
                            step(2 * (at + 1 + b), 0)
                            early_messages(w - 2)
                            step(2 * (at + 1 + b) + 1, 1)
                        else:
                            pairs(at + 1 + b, at + 2 + b)
                        if b == 0:
                            out_of(w - 2)
                        elif b == 2:
                            variance_of(w - 2)
                        elif b == 3:
                            norm_of(w - 2, first)
                        if rounds and b:
                            add_batch(q, b - 1)
                    if rounds:
                        build_rows(q + 1, after)

                unit_between(2, True, False, early=True)
                dve.wait_ge(h2_ready, 1)
                split_first()
                build_rows(0)
                unit_between(LAG, before=False, early=True)
                with dve.Fori(LAG + 1, UNITS - 1) as w:
                    unit_between(w, early=True)
                unit_between(UNITS - 1, after=TAIL)
                LAST = SUPERS - 1
                build(LAST - 1, 1)
                add(LAST - 3, 1)
                stage(LAST, 0)
                add_batch(ROUNDS - 1, BATCHES - 1)
                largest(LAST - 3, 1)
                build(LAST, 0)
                add(LAST - 2, 0)
                take_rows(ROUNDS, TAIL)
                largest(LAST - 2, 0)
                out_of(UNITS - 2)
                variance_of(UNITS - 2)
                norm_of(UNITS - 2)
                add(LAST - 1, 1)
                largest(LAST - 1, 1)
                add(LAST, 0)
                largest(LAST, 0)
                for b in range(BATCHES):
                    add_batch(ROUNDS, b)
                    if b == 1:
                        out_of(UNITS - 1, 2)
                    elif b == 4:
                        variance_of(UNITS - 1)
                norm_of(UNITS - 1)
                dve.wait_ge(counts_maxed, SUPERS)
            with dve.If(flag_of(dve, 0) > 0):
                prelude_over()
                general_dve(dve, 0)

                def network_of(u, blocks=4, first=False):
                    out_of(u, blocks)
                    variance_of(u)
                    norm_of(u, first)

                network_of(0, first=True)
                with dve.Fori(1, UNITS - 1) as u:
                    network_of(u)
                network_of(UNITS - 1, 2)
            dve.tensor_reduce(bad[:, 5:6], cnt_max[:, :], AX.X, ALU.max).then_inc(late_step, 1)
            dve.wait_ge(late_step, 1)
            dve.tensor_scalar(bad[:, 5:6], bad[:, 5:6], COUNT_MAX, None, ALU.is_ge).then_inc(late_step, 1)
            dve.wait_ge(late_step, 2)
            dve.tensor_reduce(bad[:, 6:7], bad[:, 0:6], AX.X, ALU.add).then_inc(bad_ready, 1)
            dve.wait_ge(bad_summed, 2)
            dve.tensor_scalar(flag[:, 1:2], ps[0:1, 0, 0:1], 0.0, None, ALU.is_gt).then_inc(flag_ready, 1)
            with dve.If(flag_of(dve, 1) < 1):
                dve.wait_ge(sums_loaded, 16)
                dve.tensor_tensor(hb, x1, hb, ALU.add).then_inc(out_summed, 1)
                dve.wait_ge(out_summed, 1)
            with dve.If(flag_of(dve, 1) > 0):
                general_dve(dve, 1)
                dve.wait_ge(general_loaded, 16)
                dve.tensor_tensor(hb, x1, o_sb, ALU.add).then_inc(general_summed, 1)
                dve.wait_ge(general_summed, 1)
            dve.nop().then_inc(out_ready, 1)

        @block.tensor
        def _(pe):
            pe.wait_ge(consts, 1)
            pe.wait_ge(fuse_loaded, 16 * FUSE_LOADS)
            for jt in range(2):
                for it in range(2):
                    last = pe.transpose(ps[:, 4, jt * HID + it * P:jt * HID + it * P + P],
                                        w2[:, it, jt * P:jt * P + P], ident[:, :])
            last.then_inc(w2T_done, 1)
            pe.wait_ge(w2T_ready, 1)
            pe.wait_ge(b2_ready, 1)
            for bank, right in ((5, conv), (6, post_h)):
                for it in range(2):
                    for jt in range(2):
                        pe.matmul(ps[:, bank, it * HID:(it + 1) * HID], w2T[:, jt, it * P:(it + 1) * P],
                                  right[:, jt, :], start=(jt == 0), stop=(jt == 1))
            for jt in range(2):
                pe.matmul(ps[:, 7, 0:HID], b2_wide[:, jt, :], conv[:, jt, :], start=(jt == 0), stop=(jt == 1))
            for m in range(2):
                for jt in range(2):
                    last = pe.matmul(ps[:, 7, HID + m:HID + m + 1], post_h[:, jt, m * P:(m + 1) * P],
                                     b2[:, jt:jt + 1], start=(jt == 0), stop=(jt == 1))
            last.then_inc(fused_done, 1)
            for half, (first, last_unit) in enumerate(HALVES):
                pe.wait_ge(h_ready, half + 1)
                if half:
                    pe.wait_ge(fused_ready, 2)
                for u in range(first, last_unit):
                    last = pe.transpose(ps[0:4 * F, 4 * half + (u - first) // 4, (u - first) % 4 * P:((u - first) % 4 + 1) * P],
                                        h0[:, 4 * u:4 * u + 4, :].rearrange("p b f -> p (b f)"), ident[:, :])
                last.then_inc(hT_done, 1)
            pe.wait_ge(weights_loaded, 16 * WEIGHT_LOADS)
            pe.wait_ge(hT_ready, 1)

            def hidden(g, s, done):
                for k in range(2):
                    for b in range(4):
                        last = pe.matmul(ps[:, 2 * s + k, b * P:(b + 1) * P], w1_unit[:, b, k * P:(k + 1) * P],
                                         hT[:, ds(2 * g + s, 1), :].rearrange("p a n -> p (a n)"), start=True, stop=True)
                last.then_inc(done, 1)

            def z(g, s, first=False):
                if not first:
                    pe.wait_ge(zT_ready, 2 * g + s - 1)
                hidden(g, s, z_done)

            def messages(g, s, first=False, blocks=4):
                u = 2 * g + s
                pe.wait_ge(zT_ready, u + 1)
                if not first:
                    pe.wait_ge(m_copied, u - 1)
                for b in range(blocks):
                    for k in range(2):
                        last = pe.matmul(ps[:, 4 + 2 * s + b // 2, (b % 2) * HID:(b % 2 + 1) * HID],
                                         zT[:, s, k, b * P:(b + 1) * P], w_msg[:, k, :], start=(k == 0), stop=(k == 1))
                last.then_inc(m_done, 1)

            z(0, 0, True)
            z(0, 1, True)
            pe.wait_ge(hT_ready, 2)
            messages(0, 0, True)
            z(1, 0)
            pe.wait_ge(bias_ready, 2)
            messages(0, 1, True)
            with pe.Fori(1, GROUPS - 1) as g:
                z(g, 1)
                messages(g, 0)
                z(g + 1, 0)
                messages(g, 1)
            messages(GROUPS - 1, 0, blocks=2)
            pe.wait_ge(m_copied, UNITS)

            def add_up(i, s, first=False, late=None, early=None):
                t = 2 * i + s
                late = i + 1 if late is None else late
                pe.wait_ge(onehots_built, t + 1)
                if not isinstance(t, int) or t > 1:
                    pe.wait_ge(agg_added, t - 1)
                    pe.wait_ge(counts_copied, t - 1)
                for k in range(TILES):
                    if k < TILES - EARLY_TILES or s != EARLY_SUPER % 2:
                        pe.wait_ge(gathered[s * TILES + k], 16 * (i + 1))
                    elif early is None:
                        pe.wait_ge(gathered[s * TILES + k], 16 * late)
                    elif k == TILES - EARLY_TILES:
                        pe.wait_ge(early_ready, early)
                    pe.matmul(ps[0:WINDOW, s, 0:HID], oh_dst[:, s, k, :], gat[:, s * TILES + k, :],
                              start=(k == 0), stop=(k == TILES - 1))
                    pe.matmul(ps[:, 4 + s, 0:CNT], oh_lo[:, s, k, :], oh_key[:, s, k, :],
                              start=(k == 0), stop=(k == TILES - 1)).then_inc(tiles_used, 1)
                    if k == 1 and not first:
                        turn_sums(t - 1, 1 - s)

            def turn_sums(t, s):
                pe.wait_ge(sums_copied, t + 1)
                for half in range(2):
                    last = pe.matmul(ps[:, s, HID + half * WINDOW:HID + (half + 1) * WINDOW],
                                     sums[:, half * P:(half + 1) * P], ident[0:WINDOW, 0:WINDOW], start=True, stop=True)
                last.then_inc(sums_turned, 1)

            def z_of(u, first=False):
                if not first:
                    pe.wait_ge(o_added, u)
                for k in range(2):
                    for b in range(4):
                        last = pe.matmul(ps[:, 6 + k, b * P:(b + 1) * P], w1_unit[:, b, k * P:(k + 1) * P],
                                         hT[:, ds(u, 1), :].rearrange("p a n -> p (a n)"), start=True, stop=True)
                last.then_inc(u_done, 1)

            def up_from_z(u, m, n=CHUNK):
                if m == 0:
                    pe.wait_ge(uT_ready, u + 1)
                for k in range(2):
                    pe.matmul(ps[:, 6 + m, 0:n], w_up[:, k, m * P:(m + 1) * P], unit_zq[:, k, 0:n],
                              start=(k == 0), stop=False)

            def up_from_agg(u, m, n=CHUNK, added=None):
                if added is not None:
                    pe.wait_ge(agg_added, added)
                for k in range(2):
                    last = pe.matmul(ps[:, 6 + m, 0:n], post_agg[:, k, m * P:(m + 1) * P],
                                     agg[:, k, ds(u * CHUNK, n)], start=False, stop=(k == 1))
                if m == 1:
                    last.then_inc(q_done, 1)

            def up_of(u, n=CHUNK):
                for m in range(2):
                    up_from_z(u, m, n)
                for m in range(2):
                    up_from_agg(u, m, n)

            def down_of(u, blocks=4):
                pe.wait_ge(qT_ready, u + 1)
                for b in range(blocks):
                    for k in range(2):
                        last = pe.matmul(ps[:, 6, b * F:(b + 1) * F], unit_zq[:, k, b * P:(b + 1) * P], post2[:, k, :],
                                         start=(k == 0), stop=(k == 1))
                last.then_inc(o_done, 1)

            pe.wait_ge(bad_ready, 1)
            pe.matmul(ps[:, 6, 0:1], ones[:, :], bad[:, 6:7], start=True, stop=True).then_inc(bad_summed, 1)
            with pe.If(flag_of(pe, 0) < 1):
                add_up(0, 0, True)
                add_up(0, 1)
                for i in range(1, UNIT_PAIRS):
                    add_up(i, 0)
                    add_up(i, 1)

                def find_rows(q, rows=ROUND):
                    pe.wait_ge(rows_built, q + 1)
                    if not isinstance(q, int) or q:
                        pe.wait_ge(acc_added, BATCHES * q - 1)
                    for b in range(4):
                        last = pe.matmul(ps[0:rows, 3, 0:3 * F], oh_row[:, b, 0:rows], h_first[:, b, :],
                                         start=(b == 0), stop=(b == 3))
                    last.then_inc(g_done, 1)

                def multiply(q, b, tail=False):
                    rows = TAIL if tail else ROUND
                    if b == 0:
                        pe.wait_ge(g_taken, q + 1)
                    if not tail:
                        pe.wait_ge(c_loaded, 16 * (BATCHES * q + b + 1))
                    elif b == 0:
                        pe.wait_ge(tail_loaded, 48)
                    if b > 1 or not isinstance(q, int) or q:
                        pe.wait_ge(acc_added, BATCHES * q + max(b - 1, 0))
                    for j in range(BATCH):
                        here = c_tail[:, b * BATCH + j, :] if tail else c_batch[:, j, :]
                        for part in range(3):
                            last = pe.matmul(product(b)[:, j * F:(j + 1) * F], here,
                                             g_round[0:rows, part * F:(part + 1) * F], start=(part == 0), stop=(part == 2))
                    last.then_inc(batch_done, 1)

                def unit_between(w, rounds=True, before=True, early=False):
                    q, v = w - LAG, w - 2
                    if rounds:
                        find_rows(q)
                    for n in range(2 * UNIT_PAIRS):
                        if not early:
                            add_up(w * UNIT_PAIRS + n // 2, n % 2,
                                   late=w * UNIT_PAIRS + n // 2 + 1 - (EARLY_UNITS if before else 0))
                        elif n == EARLY_SUPER:
                            add_up(w * UNIT_PAIRS + n // 2, n % 2, early=v + 1)
                        else:
                            add_up(w * UNIT_PAIRS + n // 2, n % 2,
                                   late=w * (UNIT_PAIRS - 1) + n // 2 + 3 - (n > EARLY_SUPER))
                        if n % 2 and n > 1 and rounds:
                            multiply(q, n // 2 - 1)
                        if n == 0 and before:
                            up_from_agg(w - 2, 1)
                        elif n == 2 and before:
                            down_of(w - 2)
                        elif n == 4 and early:
                            pe.wait_ge(o_added, v + 1)
                            pe.wait_ge(early_loaded, 16 * (v + 1))
                            pe.matmul(ps[0:EARLY_TILES * F, 6, 0:P], early_rows, ident[:, :], start=True, stop=True)\
                                .then_inc(early_turned, 1)
                        elif n == 6 and early:
                            pe.wait_ge(early_copied, v + 1)
                            for k in range(2):
                                for b in range(EARLY_TILES):
                                    last = pe.matmul(ps[:, 6 + k, b * P:(b + 1) * P], w1_unit[:, b, k * P:(k + 1) * P],
                                                     early_T, start=True, stop=True)
                            last.then_inc(early_z_done, 1)
                        elif n in (8, 9) and early:
                            if n == 8:
                                pe.wait_ge(early_z_ready, v + 1)
                            for b in (0, 1):
                                tile = 2 * (n - 8) + b
                                for k in range(2):
                                    last = pe.matmul(ps[:, n - 2, b * HID:(b + 1) * HID],
                                                     unit_zq[:, k, tile * P:(tile + 1) * P], w_msg[:, k, :],
                                                     start=(k == 0), stop=(k == 1))
                            if n == 9:
                                last.then_inc(early_m_done, 1)
                        elif n == 11:
                            if early:
                                pe.wait_ge(early_summed, v + 1)
                            z_of(w - 1, not before)
                        elif n == 12:
                            up_from_z(w - 1, 0)
                        elif n == 13:
                            up_from_z(w - 1, 1)
                        elif n == 14:
                            up_from_agg(w - 1, 0, added=2 * UNIT_PAIRS * (w + 1) - SLACK)

                unit_between(1, False, False)
                unit_between(2, False, early=True)
                unit_between(LAG, early=True)
                with pe.Fori(LAG + 1, UNITS - 1) as w:
                    unit_between(w, early=True)
                unit_between(UNITS - 1)
                add_up(PAIRS - 1, 0)
                up_from_agg(UNITS - 2, 1)
                find_rows(ROUNDS, TAIL)
                add_up(PAIRS - 1, 1, late=PAIRS - EARLY_UNITS)
                down_of(UNITS - 2)
                add_up(PAIRS, 0)
                z_of(UNITS - 1)
                turn_sums(SUPERS - 1, 0)
                for m in range(2):
                    up_from_z(UNITS - 1, m, 2 * P)
                for m in range(2):
                    up_from_agg(UNITS - 1, m, 2 * P, added=SUPERS)
                for b in range(BATCHES):
                    multiply(ROUNDS, b, True)
                    if b == 1:
                        down_of(UNITS - 1, 2)
                pe.wait_ge(o_added, UNITS)
                pe.wait_ge(counts_copied, SUPERS)
                pe.wait_ge(acc_added, BATCHES * (ROUNDS + 1))
            with pe.If(flag_of(pe, 0) > 0):
                general_pe(pe, 0)

                def turn(b, first=False):
                    pe.wait_ge(b_loaded, 16 * (b + 1))
                    if not first:
                        pe.wait_ge(b_copied, b)
                    for k in range(2):
                        last = pe.transpose(ps[:, 5, k * P:(k + 1) * P], e_back[:, k * P:(k + 1) * P], ident[:, :])
                    last.then_inc(b_turned, 1)

                turn(0, True)
                with pe.Fori(1, BLOCKS) as b:
                    turn(b)
                pe.wait_ge(b_copied, BLOCKS)

                def network_of(u, blocks=4, first=False):
                    z_of(u, first)
                    up_of(u, blocks * P)
                    down_of(u, blocks)

                network_of(0, first=True)
                with pe.Fori(1, UNITS - 1) as u:
                    network_of(u)
                network_of(UNITS - 1, 2)
            pe.wait_ge(bad_ready, 2)
            pe.matmul(ps[:, 0, 0:1], ones[:, :], bad[:, 6:7], start=True, stop=True).then_inc(bad_summed, 1)
            with pe.If(flag_of(pe, 1) > 0):
                general_pe(pe, 1)


def kernel(**inputs):
    import numpy as np
    import concourse.bacc as bacc
    from concourse.bass_utils import run_bass_kernel_spmd

    a = {k: np.ascontiguousarray(v) for k, v in inputs.items()}
    x_pad = np.zeros((GROUPS * 8 * P, F), a["x"].dtype)
    x_pad[:N_NODES] = a["x"]
    src_pad = np.zeros(EDGES_PAD, a["src"].dtype)
    src_pad[:N_EDGES] = a["src"]
    dst_pad = np.full(EDGES_PAD, NOWHERE, a["dst"].dtype)
    dst_pad[:N_EDGES] = a["dst"]

    def by_partition(e):
        return np.ascontiguousarray(e.reshape(SUPERS, P, TILES).transpose(1, 0, 2).reshape(P, SUPERS * TILES))

    arrays = {
        "x": np.ascontiguousarray(x_pad.reshape(GROUPS * 8, P, F).transpose(1, 0, 2).reshape(P, GROUPS * 8 * F)),
        "src": by_partition(src_pad), "dst": by_partition(dst_pad), "dst_flat": dst_pad,
    }
    for name in ("pre_w1", "pre_b1", "pre_w2", "pre_b2", "conv_w", "conv_b", "post_w1", "post_b1", "post_w2", "post_b2"):
        arrays[name] = a["L0_gnn_" + name]
    nc = bacc.Bacc("TRN2", target_bir_lowering=False, num_devices=1)
    maps, args = {}, []
    for name, v in arrays.items():
        maps[f"in_{name}"] = v
        args.append(nc.dram_tensor(f"in_{name}", v.shape, mybir.dt.from_np(v.dtype), kind="ExternalInput").ap())
    args.append(nc.dram_tensor("result", (P, BLOCKS * F), mybir.dt.float32, kind="ExternalOutput").ap())
    gnn_kernel(nc, *args)
    r = run_bass_kernel_spmd(nc, [maps], core_ids=[0])
    y = r.results[0]["result"].reshape(P, BLOCKS, F).transpose(1, 0, 2).reshape(NODES_PAD, F)
    return np.ascontiguousarray(y[:N_NODES])
```
